# Optimizing a Trainium2 kernel written in Bass

```python
import numpy as np
import jax
import jax.numpy as jnp

def _softmax(x, axis=-1):
    return jax.nn.softmax(x, axis=axis)

def _gelu(x):
    return jax.nn.gelu(x, approximate=True)

def _silu(x):
    return jax.nn.silu(x)

def _sigmoid(x):
    return jax.nn.sigmoid(x)

def _layernorm(x, axis=-1, eps=1e-05):
    m = jnp.mean(x, axis=axis, keepdims=True)
    v = jnp.var(x, axis=axis, keepdims=True)
    return (x - m) / jnp.sqrt(v + eps)

def _scatter_add(tgt, idx, src, axis=0):
    return tgt.at[idx].add(src)

def _segment_sum(src, seg, n):
    return jax.ops.segment_sum(src, seg, n)
kernel_name = 'mk_xattn_ffn_d2_seqx_r8_8b9961'

def setup_inputs(seed: int=0):
    np.random.seed(seed)
    _w = jnp.asarray

    def _rec_inputs():
        import jax
        import jax.numpy as jnp
        _rk = jax.random.key(seed)
        x = -0.0003929 + 0.9999 * jax.random.normal(jax.random.fold_in(_rk, 1), (32, 64, 512), jnp.float32)
        _lenS = 64 - jax.random.randint(jax.random.fold_in(_rk, 7), (32,), 0, max(1, 64 // 4) + 1, jnp.int32)
        _lenS2 = 64 - jax.random.randint(jax.random.fold_in(_rk, 8), (32,), 0, max(1, 64 // 4) + 1, jnp.int32)
        _ctx_4096P = jax.random.normal(jax.random.fold_in(_rk, 11), (32, 16, 512), jnp.float32)
        _ctx_4096c = jax.random.dirichlet(jax.random.fold_in(_rk, 511), 0.3 * jnp.ones((16,), jnp.float32), (32, 64))
        _ctx_4096t = jnp.einsum('bsk,bkd->bsd', _ctx_4096c, _ctx_4096P)
        _ctx_4096t = _ctx_4096t * jax.lax.rsqrt(jnp.mean(jnp.square(_ctx_4096t)) + 1e-12) * 0.953939
        ctx_4096 = -5.78663e-05 + 0.999831 * (_ctx_4096t + 0.3 * jax.random.normal(jax.random.fold_in(_rk, 611), (32, 64, 512), jnp.float32))
        _validS = jnp.arange(64)[None, :] < _lenS[:, None]
        _validS2 = jnp.arange(64)[None, :] < _lenS2[:, None]
        _causal = jnp.tril(jnp.ones((64, 64), dtype=bool))
        mask_1x1xSxS2_ff0 = jnp.where(jnp.ones((1, 1, 64, 64), dtype=bool), 0.0, -1000000000.0).astype(jnp.float32)
        return (x, ctx_4096, mask_1x1xSxS2_ff0)
    x, ctx_4096, mask_1x1xSxS2_ff0 = _rec_inputs()

    def _L0_xattn_setup():
        import jax, jax.numpy as jnp
        import numpy as np
        EPS = 1e-06

        def rmsnorm(x, w):
            xf = x.astype(jnp.float32)
            var = jnp.mean(xf * xf, axis=-1, keepdims=True)
            return (xf * jax.lax.rsqrt(var + EPS)).astype(x.dtype) * w
        key = jax.random.key(seed)
        ks = jax.random.split(key, 6)
        B, T, S, Dt, Df = (4, 128, 72, 512, 512)
        text = jax.random.normal(ks[0], (B, T, Dt), dtype=jnp.float32)
        features = jax.random.normal(ks[1], (B, S, Df), dtype=jnp.float32)
        lim_q = float(np.sqrt(6.0 / (Dt + Df)))
        lim_k = float(np.sqrt(6.0 / (Df + Df)))
        Wq_w = jax.random.uniform(ks[2], (Df, Dt), minval=-lim_q, maxval=lim_q, dtype=jnp.float32)
        Wk_w = jax.random.uniform(ks[3], (Df, Df), minval=-lim_k, maxval=lim_k, dtype=jnp.float32)
        bq = 1.0 / np.sqrt(Dt)
        bk = 1.0 / np.sqrt(Df)
        Wq_b = jax.random.uniform(ks[4], (Df,), minval=-bq, maxval=bq, dtype=jnp.float32)
        Wk_b = jax.random.uniform(ks[5], (Df,), minval=-bk, maxval=bk, dtype=jnp.float32)
        fn_w = jnp.ones((Df,), dtype=jnp.float32)
        qn_w = jnp.ones((Df,), dtype=jnp.float32)
        kn_w = jnp.ones((Df,), dtype=jnp.float32)
        return {'text': text, 'features': features, 'Wq_w': Wq_w, 'Wq_b': Wq_b, 'Wk_w': Wk_w, 'Wk_b': Wk_b, 'fn_w': fn_w, 'qn_w': qn_w, 'kn_w': kn_w}
    _L0_xattn_all = _L0_xattn_setup()
    _L0_xattn_in = {k: v for k, v in _L0_xattn_all.items() if k in ('Wq_w', 'Wq_b', 'Wk_w', 'Wk_b', 'fn_w', 'qn_w', 'kn_w')}
    del _L0_xattn_all

    def _L0_ffn_setup():
        import jax, jax.numpy as jnp
        import numpy as np
        DIM = 512
        INTER = 1792
        SPARSITY = 32
        RANK = 16
        key = jax.random.key(seed)
        ks = jax.random.split(key, 5)
        B, T = (32, 1)
        x = jax.random.normal(ks[0], (B, T, DIM), dtype=jnp.float32)
        c1_w = jax.random.normal(ks[1], (RANK, DIM), dtype=jnp.float32) * (1.0 / np.sqrt(DIM))
        c2_w = jax.random.normal(ks[2], (INTER, RANK), dtype=jnp.float32) * (1.0 / np.sqrt(RANK))
        w1 = jax.random.normal(ks[3], (INTER, DIM), dtype=jnp.float32) * (1.0 / np.sqrt(DIM))
        w2t = jax.random.normal(ks[4], (INTER, DIM), dtype=jnp.float32) * (1.0 / np.sqrt(INTER))
        return {'x': x, 'c1_w': c1_w, 'c2_w': c2_w, 'w1': w1, 'w2t': w2t}
    _L0_ffn_all = _L0_ffn_setup()
    _L0_ffn_in = {k: v for k, v in _L0_ffn_all.items() if k in ('c1_w', 'c2_w', 'w1', 'w2t')}
    del _L0_ffn_all

    def _L1_xattn_setup():
        import jax, jax.numpy as jnp
        import numpy as np
        B, Q, K, D = (1, 128, 6404, 512)
        H, KVH, HD = (32, 8, 128)
        GROUPS = H // KVH
        EPS = 1e-05

        def _rmsnorm(x, w):
            xf = x.astype(jnp.float32)
            var = jnp.mean(xf * xf, axis=-1, keepdims=True)
            return (xf * jax.lax.rsqrt(var + EPS)).astype(x.dtype) * w
        key = jax.random.key(seed)
        ks = jax.random.split(key, 8)
        s = 0.02
        return {'hidden_states': jax.random.normal(ks[0], (B, Q, D), jnp.float32), 'cross_attention_states': jax.random.normal(ks[1], (B, K, D), jnp.float32), 'attention_mask': jnp.zeros((B, 1, Q, K), jnp.float32), 'Wq': jax.random.normal(ks[2], (H * HD, D), jnp.float32) * s, 'Wk': jax.random.normal(ks[3], (KVH * HD, D), jnp.float32) * s, 'Wv': jax.random.normal(ks[4], (KVH * HD, D), jnp.float32) * s, 'Wo': jax.random.normal(ks[5], (D, H * HD), jnp.float32) * s, 'q_norm_w': jnp.ones((HD,), jnp.float32), 'k_norm_w': jnp.ones((HD,), jnp.float32)}
    _L1_xattn_all = _L1_xattn_setup()
    _L1_xattn_in = {k: v for k, v in _L1_xattn_all.items() if k in ('Wq', 'Wk', 'Wv', 'Wo', 'q_norm_w', 'k_norm_w')}
    del _L1_xattn_all

    def _L1_ffn_setup():
        import jax, jax.numpy as jnp
        import numpy as np
        IN_F = 512
        OUT_F = 512
        N_CLUSTERS = 64
        THRESHOLD = 0.01
        TEMPERATURE = 0.1
        BATCH, SEQ = (4, 256)
        key = jax.random.key(seed)
        k1, k2, k3, k4, k5 = jax.random.split(key, 5)
        s = 1.0 / np.sqrt(IN_F)
        return {'input': jax.random.normal(k1, (BATCH, SEQ, IN_F), dtype=jnp.float32), 'weight': jax.random.normal(k2, (OUT_F, IN_F), dtype=jnp.float32) * s, 'bias': jax.random.uniform(k3, (OUT_F,), dtype=jnp.float32, minval=-s, maxval=s), 'centroids': jax.random.normal(k4, (N_CLUSTERS, IN_F), dtype=jnp.float32) * s, 'assignments': jax.random.randint(k5, (OUT_F,), 0, N_CLUSTERS, dtype=jnp.int32)}
    _L1_ffn_all = _L1_ffn_setup()
    _L1_ffn_in = {k: v for k, v in _L1_ffn_all.items() if k in ('weight', 'bias', 'centroids', 'assignments')}
    del _L1_ffn_all
    return {'x': x, 'ctx_4096': ctx_4096, 'mask_1x1xSxS2_ff0': mask_1x1xSxS2_ff0, 'L0_xattn_Wq_w': _L0_xattn_in['Wq_w'], 'L0_xattn_Wq_b': _L0_xattn_in['Wq_b'], 'L0_xattn_Wk_w': _L0_xattn_in['Wk_w'], 'L0_xattn_Wk_b': _L0_xattn_in['Wk_b'], 'L0_xattn_fn_w': _L0_xattn_in['fn_w'], 'L0_xattn_qn_w': _L0_xattn_in['qn_w'], 'L0_xattn_kn_w': _L0_xattn_in['kn_w'], 'L0_ffn_c1_w': _L0_ffn_in['c1_w'], 'L0_ffn_c2_w': _L0_ffn_in['c2_w'], 'L0_ffn_w1': _L0_ffn_in['w1'], 'L0_ffn_w2t': _L0_ffn_in['w2t'], 'L1_xattn_Wq': _L1_xattn_in['Wq'], 'L1_xattn_Wk': _L1_xattn_in['Wk'], 'L1_xattn_Wv': _L1_xattn_in['Wv'], 'L1_xattn_Wo': _L1_xattn_in['Wo'], 'L1_xattn_q_norm_w': _L1_xattn_in['q_norm_w'], 'L1_xattn_k_norm_w': _L1_xattn_in['k_norm_w'], 'L1_ffn_weight': _L1_ffn_in['weight'], 'L1_ffn_bias': _L1_ffn_in['bias'], 'L1_ffn_centroids': _L1_ffn_in['centroids'], 'L1_ffn_assignments': _L1_ffn_in['assignments']}

def reference(x, ctx_4096, mask_1x1xSxS2_ff0, L0_xattn_Wq_w, L0_xattn_Wq_b, L0_xattn_Wk_w, L0_xattn_Wk_b, L0_xattn_fn_w, L0_xattn_qn_w, L0_xattn_kn_w, L0_ffn_c1_w, L0_ffn_c2_w, L0_ffn_w1, L0_ffn_w2t, L1_xattn_Wq, L1_xattn_Wk, L1_xattn_Wv, L1_xattn_Wo, L1_xattn_q_norm_w, L1_xattn_k_norm_w, L1_ffn_weight, L1_ffn_bias, L1_ffn_centroids, L1_ffn_assignments):
    import jax
    import jax.numpy as jnp

    def _L0_xattn_ref(text, features, Wq_w, Wq_b, Wk_w, Wk_b, fn_w, qn_w, kn_w):
        import jax, jax.numpy as jnp
        import numpy as np
        EPS = 1e-06

        def rmsnorm(x, w):
            xf = x.astype(jnp.float32)
            var = jnp.mean(xf * xf, axis=-1, keepdims=True)
            return (xf * jax.lax.rsqrt(var + EPS)).astype(x.dtype) * w
        features_n = rmsnorm(features, fn_w)
        Q = jnp.einsum('btd,fd->btf', text, Wq_w) + Wq_b
        K = jnp.einsum('bsd,fd->bsf', features_n, Wk_w) + Wk_b
        Q = rmsnorm(Q, qn_w)
        K = rmsnorm(K, kn_w)
        scale = 1.0 / jnp.sqrt(jnp.asarray(K.shape[-1], dtype=Q.dtype))
        scores = jnp.einsum('btf,bsf->bts', Q, K) * scale
        attn = jax.nn.softmax(scores, axis=-1)
        attended = jnp.einsum('bts,bsf->btf', attn, features_n)
        return attended

    def _L0_ffn_ref(x, c1_w, c2_w, w1, w2t):
        import jax, jax.numpy as jnp
        import numpy as np
        DIM = 512
        INTER = 1792
        SPARSITY = 32
        RANK = 16
        B, T, M = x.shape
        xf = x.reshape(B * T, M)
        inter = xf @ c1_w.T @ c2_w.T
        n_blocks = INTER // SPARSITY
        blk = inter.reshape(B * T, n_blocks, SPARSITY)
        idx = jnp.argmax(blk, axis=-1) + jnp.arange(0, INTER, SPARSITY)
        w1_g = w1[idx]
        w2_g = w2t[idx]
        h = jax.nn.relu(jnp.einsum('bkm,bm->bk', w1_g, xf))
        out = jnp.einsum('bk,bkm->bm', h, w2_g)
        return out.reshape(B, T, M)

    def _L1_xattn_ref(hidden_states, cross_attention_states, attention_mask, Wq, Wk, Wv, Wo, q_norm_w, k_norm_w):
        import jax, jax.numpy as jnp
        import numpy as np
        B, Q, K, D = (1, 128, 6404, 512)
        H, KVH, HD = (32, 8, 128)
        GROUPS = H // KVH
        EPS = 1e-05

        def _rmsnorm(x, w):
            xf = x.astype(jnp.float32)
            var = jnp.mean(xf * xf, axis=-1, keepdims=True)
            return (xf * jax.lax.rsqrt(var + EPS)).astype(x.dtype) * w
        bsz, q_len, _ = hidden_states.shape
        kv_len = cross_attention_states.shape[1]
        q = (hidden_states @ Wq.T).reshape(bsz, q_len, H, HD).transpose(0, 2, 1, 3)
        k = (cross_attention_states @ Wk.T).reshape(bsz, kv_len, KVH, HD).transpose(0, 2, 1, 3)
        v = (cross_attention_states @ Wv.T).reshape(bsz, kv_len, KVH, HD).transpose(0, 2, 1, 3)
        q = _rmsnorm(q, q_norm_w)
        k = jnp.repeat(k, GROUPS, axis=1)
        v = jnp.repeat(v, GROUPS, axis=1)
        k = _rmsnorm(k, k_norm_w)
        scale = 1.0 / np.sqrt(HD)
        scores = jnp.einsum('bhqd,bhkd->bhqk', q, k) * scale
        scores = scores + attention_mask[:, :, :, :kv_len]
        probs = jax.nn.softmax(scores.astype(jnp.float32), axis=-1).astype(q.dtype)
        out = jnp.einsum('bhqk,bhkd->bhqd', probs, v)
        out = out.transpose(0, 2, 1, 3).reshape(bsz, q_len, H * HD)
        return out @ Wo.T

    def _L1_ffn_ref(input, weight, bias, centroids, assignments):
        import jax, jax.numpy as jnp
        import numpy as np
        IN_F = 512
        OUT_F = 512
        N_CLUSTERS = 64
        THRESHOLD = 0.01
        TEMPERATURE = 0.1
        BATCH, SEQ = (4, 256)
        shape = input.shape
        x = input.reshape(-1, shape[-1])
        dots = jax.nn.softmax(x @ centroids.T / TEMPERATURE, axis=-1)
        hits = dots > THRESHOLD
        query_sel = jnp.any(hits, axis=1)
        cluster_sel = jnp.any(hits, axis=0)
        row_sel = cluster_sel[assignments]
        dense = x @ weight.T + bias
        out = jnp.where(query_sel[:, None] & row_sel[None, :], dense, jnp.zeros((), dense.dtype))
        return out.reshape(*shape[:-1], -1)
    x = x + _L0_xattn_ref(_layernorm(x, axis=-1), ctx_4096, L0_xattn_Wq_w, L0_xattn_Wq_b, L0_xattn_Wk_w, L0_xattn_Wk_b, L0_xattn_fn_w, L0_xattn_qn_w, L0_xattn_kn_w)
    x = x + _L0_ffn_ref(_layernorm(x, axis=-1), L0_ffn_c1_w, L0_ffn_c2_w, L0_ffn_w1, L0_ffn_w2t)
    x = x + _L1_xattn_ref(_layernorm(x, axis=-1), ctx_4096, mask_1x1xSxS2_ff0, L1_xattn_Wq, L1_xattn_Wk, L1_xattn_Wv, L1_xattn_Wo, L1_xattn_q_norm_w, L1_xattn_k_norm_w)
    x = x + _L1_ffn_ref(_layernorm(x, axis=-1), L1_ffn_weight, L1_ffn_bias, L1_ffn_centroids, L1_ffn_assignments)
    return x

_drawn_inputs = setup_inputs


def setup_inputs(seed=0):
    import zlib

    import numpy as np

    out = dict(_drawn_inputs(seed))
    spreads = {'L0_xattn_fn_w': (1.0, 0.2),
     'L0_xattn_qn_w': (1.0, 0.2),
     'L0_xattn_kn_w': (1.0, 0.2),
     'L1_xattn_q_norm_w': (1.0, 0.6),
     'L1_xattn_k_norm_w': (1.0, 0.6)}
    factors = {'L0_xattn_Wq_b': 5.482, 'L0_xattn_Wk_b': 8.0, 'L1_ffn_bias': 3.62}
    for name, (base, spread) in spreads.items():
        noise = np.random.default_rng([zlib.crc32(name.encode()), seed]).standard_normal(out[name].shape)
        drawn = base * np.exp(spread * noise) if base else spread * noise
        out[name] = jnp.asarray(drawn.astype(out[name].dtype))
    for name, factor in factors.items():
        out[name] = (out[name] * factor).astype(out[name].dtype)
    return out
```

```python
from contextlib import ExitStack

import numpy as np

import concourse.bass as bass
from concourse import mybir

F32 = mybir.dt.float32
F32R = mybir.dt.float32r
BF16 = mybir.dt.bfloat16
I32 = mybir.dt.int32
ALU = mybir.AluOpType
ACT = mybir.ActivationFunctionType
AX = mybir.AxisListType

P = 128
D = 512
KD = D // P
ROWS = 2048
S = 64
CHUNK = 512
TPC = CHUNK // P
NCH = ROWS // CHUNK
NT = ROWS // P
INTER = 1792
NI = INTER // P
QC = 448
NQ = INTER // QC
SPARSE = 32
BPQ = QC // SPARSE
RANK = 16
RK3 = 3 * 32
H = 32
KVH = 8
HD = 128
G = H // KVH
NCL = 64
LN_EPS = 1e-5
L0_EPS = 1e-6
L1_EPS = 1e-5
OFF = -3e38


def split_mm(pe, out, a_hi, a_lo, b_hi, b_lo, first, last):
    pe.matmul(out, a_hi, b_hi, start=first, stop=False)
    pe.matmul(out, a_lo, b_hi, start=False, stop=False)
    return pe.matmul(out, a_hi, b_lo, start=False, stop=last)


class Prep:

    def __init__(self, nc, ctx, mem):
        self.m = mem
        sem = lambda n: ctx.enter_context(nc.semaphore(n))
        self.stat, self.agg, self.var = sem("ln_stat"), sem("ln_agg"), sem("ln_var")
        self.rstd, self.norm, self.ps = sem("ln_rstd"), sem("ln_norm"), sem("xT_ps")
        self.hi, self.lo = sem("xT_hi_done"), sem("xT_lo_done")

    def dve_stats(self, dve, p, cn):
        m = self.m
        for t in range(TPC):
            ins = dve.bn_stats(m.ln_st[:, t, :], m.x[:, bass.ts(cn * TPC + t, D)])
        ins.then_inc(self.stat, 1)
        dve.wait_ge(self.stat, p + 1)
        dve.memset(m.ln_ve[:, :], LN_EPS)
        for t in range(TPC):
            ins = dve.bn_aggr(m.ln_mv[:, t, :], m.ln_st[:, t, :])
        ins.then_inc(self.agg, 1)
        dve.wait_ge(self.agg, p + 1)
        dve.tensor_scalar(m.ln_ve[:, :], m.ln_mv[:, :, 1], LN_EPS, None, ALU.add).then_inc(self.var, 1)

    def pool_rstd(self, pool, p):
        m = self.m
        pool.wait_ge(self.var, p + 1)
        pool.tensor_tensor(m.ln_rs[:, :], m.ln_ve[:, :], m.neg_half[:, 0:TPC], ALU.pow).then_inc(self.rstd, 1)

    def dve_norm(self, dve, p, cn):
        m = self.m
        dve.wait_ge(self.rstd, p + 1)
        for t in range(TPC):
            ins = dve.tensor_scalar(m.xln[:, t, :], m.x[:, bass.ts(cn * TPC + t, D)], m.ln_mv[:, t, 0:1],
                                    m.ln_rs[:, t:t + 1], ALU.subtract, ALU.mult)
        ins.then_inc(self.norm, 1)

    def pe_transpose(self, pe, p, banks):
        m = self.m
        pe.wait_ge(self.norm, p + 1)
        for k in range(KD):
            for t in range(TPC):
                ins = pe.transpose(banks[k][:, t * P:(t + 1) * P], m.xln[:, t, k * P:(k + 1) * P], m.ident[:, :])
            ins.then_inc(self.ps, 1)

    def act_hi(self, act, p, banks):
        for k in range(KD):
            act.wait_ge(self.ps, p * KD + k + 1)
            act.copy(self.m.xT_hi[:, k, :], banks[k][:, :]).then_inc(self.hi, 1)

    def dve_lo(self, dve, p, banks):
        for k in range(KD):
            dve.wait_ge(self.hi, p * KD + k + 1)
            dve.tensor_tensor(self.m.xT_lo[:, k, :], banks[k][:, :], self.m.xT_hi[:, k, :],
                              ALU.subtract).then_inc(self.lo, 1)

    def wait_ready(self, pe, p):
        pe.wait_ge(self.lo, (p + 1) * KD)


class Mem:
    pass


def persistent(nc, ctx):
    m = Mem()
    sb = lambda n, s, d=F32: ctx.enter_context(nc.sbuf_tensor(n, s, d))
    m.x = sb("x_res", [P, NT * D])
    m.xT_hi, m.xT_lo = sb("xT_hi", [P, KD, CHUNK], F32R), sb("xT_lo", [P, KD, CHUNK], F32R)
    m.xln = sb("xln", [P, TPC, D])
    m.ident = sb("ident", [P, P])
    m.ones = sb("ones", [P, 1])
    m.neg_half = sb("neg_half", [P, TPC * G])
    m.ln_st, m.ln_mv = sb("ln_st", [P, TPC, 6]), sb("ln_mv", [P, TPC, 2])
    m.ln_ve, m.ln_rs = sb("ln_ve", [P, TPC]), sb("ln_rs", [P, TPC])
    m.bank = [ctx.enter_context(nc.psum_tensor(f"bank{i}", [P, 512], F32)) for i in range(8)]
    return m


def stage_l0_attention(nc, m, prep, a):
    with ExitStack() as ctx:
        sb = lambda n, s, d=F32: ctx.enter_context(nc.sbuf_tensor("a0_" + n, s, d))
        sem = lambda n: ctx.enter_context(nc.semaphore("a0_" + n))
        bank = m.bank
        wraw = [sb(f"w{n}_raw", [P, KD, D]) for n in "qk"]
        w_hi = [sb(f"w{n}_hi", [P, KD, D], F32R) for n in "qk"]
        w_lo = [sb(f"w{n}_lo", [P, KD, D], F32R) for n in "qk"]
        bq, bk = sb("bq", [P, KD]), sb("bk", [P, D])
        fnw, qnw, wqk = sb("fnw", [P, D]), sb("qnw", [P, D]), sb("wqk", [P, D])
        off = sb("off", [P, P])
        craw, f = sb("craw", [P, TPC, D]), sb("f", [P, TPC, D])
        f_hi, f_lo = sb("f_hi", [P, TPC, D], F32R), sb("f_lo", [P, TPC, D], F32R)
        cT_hi, cT_lo = sb("cT_hi", [P, KD, CHUNK], F32R), sb("cT_lo", [P, KD, CHUNK], F32R)
        qT_hi, qT_lo = sb("qT_hi", [P, KD, CHUNK], F32R), sb("qT_lo", [P, KD, CHUNK], F32R)
        q2 = sb("q2", [P, KD, CHUNK])
        kb = sb("kb", [P, TPC, D])
        kT_hi, kT_lo = cT_hi, cT_lo
        sS, prob = sb("scores", [P, TPC, P]), sb("prob", [P, TPC, P])
        pT_hi, pT_lo = sb("pT_hi", [P, TPC, P], F32R), sb("pT_lo", [P, TPC, P], F32R)
        css, cve, crs = sb("css", [P, TPC]), sb("cve", [P, TPC]), sb("crs", [P, TPC])
        kss, kve, krs = sb("kss", [P, TPC]), sb("kve", [P, TPC]), sb("krs", [P, TPC])
        qve, qrs = sb("qve", [P, TPC]), sb("qrs", [P, TPC])
        nmx, den, rden = sb("nmx", [P, TPC]), sb("den", [P, TPC]), sb("rden", [P, TPC])

        const_in, x_in, w_in, c_in = sem("const_in"), sem("x_in"), [sem("wq_in"), sem("wk_in")], sem("c_in")
        zero, ident_ok, off_ok, half_ok = sem("zero"), sem("ident_ok"), sem("off_ok"), sem("half_ok")
        wh_ok, wl_ok, wqk_ok = sem("w_hi_ok"), sem("w_lo_ok"), sem("wqk_ok")
        s_css, s_cve, s_crs, s_f = sem("css_ok"), sem("cve_ok"), sem("crs_ok"), sem("f_ok")
        s_fh, s_fl, s_cT, s_cTh, s_cTl = sem("f_hi_ok"), sem("f_lo_ok"), sem("cT_ps"), sem("cT_hi_ok"), sem("cT_lo_ok")
        s_q, s_qact, s_ql, s_qss, s_qve, s_qrs = (sem("q_ps"), sem("q_act"), sem("q_lo_ok"), sem("qss_ps"),
                                                  sem("qve_ok"), sem("qrs_ok"))
        s_k, s_kb, s_kss, s_kve, s_krs, s_kn = (sem("k_ps"), sem("kb_ok"), sem("kss_ok"), sem("kve_ok"),
                                                sem("krs_ok"), sem("kn_ok"))
        s_kT, s_kTh, s_kTl = sem("kT_ps"), sem("kT_hi_ok"), sem("kT_lo_ok")
        s_s, s_sS, s_nmx, s_p, s_rden = sem("s_ps"), sem("scores_ok"), sem("nmx_ok"), sem("prob_ok"), sem("rden_ok")
        s_pT, s_pTh, s_pTl, s_att, s_x = sem("pT_ps"), sem("pT_hi_ok"), sem("pT_lo_ok"), sem("att_ps"), sem("x_ok")
        block = ctx.enter_context(nc.Block())

        x_rows = a.x.rearrange("(c t p) d -> c p t d", c=NCH, p=P)
        c_rows = a.ctx.rearrange("(n p) d -> p n d", p=P)

        @block.sync
        def _(sp):
            sp.dma_start(m.x[:, 0:TPC * D].rearrange("p (t d) -> p t d", t=TPC), x_rows[0]).then_inc(x_in, 16)
            sp.dma_start(craw[:, :, :], c_rows[:, 0:TPC, :]).then_inc(c_in, 16)
            sp.dma_start(wraw[0][:, :, :], a.l0_wq).then_inc(w_in[0], 16)
            sp.dma_start(wraw[1][:, :, :], a.l0_wk).then_inc(w_in[1], 16)
            for n in range(1, NCH):
                sp.dma_start(m.x[:, n * TPC * D:(n + 1) * TPC * D].rearrange("p (t d) -> p t d", t=TPC),
                             x_rows[n]).then_inc(x_in, 16)
            with sp.Fori(1, NCH) as c:
                sp.wait_ge(s_f, c)
                sp.dma_start(craw[:, :, :], c_rows[:, bass.ts(c, TPC), :]).then_inc(c_in, 16)

        @block.gpsimd
        def _(pool):
            pool.memset(m.ident[:, :], 0.0).then_inc(zero, 1)
            pool.memset(m.neg_half[:, :], -0.5).then_inc(half_ok, 1)
            pool.wait_ge(zero, 1)
            pool.affine_select(out=m.ident[:, :], in_=m.ident[:, :], compare_op=ALU.not_equal, fill=1.0, base=0,
                               pattern=[[-1, P]], channel_multiplier=1).then_inc(ident_ok, 1)
            pool.memset(m.ones[:, :], 1.0).then_inc(half_ok, 1)
            pool.wait_ge(half_ok, 2)
            prep.pool_rstd(pool, 0)
            with pool.Fori(0, NCH) as c:
                pool.wait_ge(s_cve, c + 1)
                pool.tensor_tensor(crs[:, :], cve[:, :], m.neg_half[:, 0:TPC], ALU.pow).then_inc(s_crs, 1)
                pool.wait_ge(s_fh, c + 1)
                pool.tensor_tensor(f_lo[:, :, :], f[:, :, :], f_hi[:, :, :], ALU.subtract).then_inc(s_fl, 1)
                pool.wait_ge(s_qve, c + 1)
                pool.tensor_tensor(qrs[:, :], qve[:, :], m.neg_half[:, 0:TPC], ALU.pow).then_inc(s_qrs, 1)
                pool.wait_ge(s_kve, c + 1)
                pool.tensor_tensor(krs[:, :], kve[:, :], m.neg_half[:, 0:TPC], ALU.pow).then_inc(s_krs, 1)
                prep.pool_rstd(pool, c + 1)

        @block.scalar
        def _(act):
            act.dma_start(bq[:, :], a.l0_bq).then_inc(const_in, 16)
            act.dma_start(bk[:, :], a.l0_bk.partition_broadcast(P)).then_inc(const_in, 16)
            act.dma_start(fnw[:, :], a.l0_fnw.partition_broadcast(P)).then_inc(const_in, 16)
            act.dma_start(qnw[:, :], a.l0_qnw.partition_broadcast(P)).then_inc(const_in, 16)
            act.dma_start(wqk[:, :], a.l0_knw.partition_broadcast(P)).then_inc(const_in, 16)
            for n in range(2):
                act.wait_ge(w_in[n], 16)
                act.copy(w_hi[n][:, :, :], wraw[n][:, :, :]).then_inc(wh_ok, 1)
            act.wait_ge(const_in, 80)
            prep.act_hi(act, 0, bank[4:8])
            with act.Fori(0, NCH) as c:
                act.wait_ge(c_in, (c + 1) * 16)
                for t in range(TPC):
                    ins = act.activation(f[:, t, :], craw[:, t, :], ACT.Square, accum_out=css[:, t:t + 1])
                ins.then_inc(s_css, 1)
                act.wait_ge(s_f, c + 1)
                act.copy(f_hi[:, :, :], f[:, :, :]).then_inc(s_fh, 1)
                for k in range(KD):
                    act.wait_ge(s_cT, c * KD + k + 1)
                    act.copy(cT_hi[:, k, :], bank[k][:, :]).then_inc(s_cTh, 1)
                for j in range(KD):
                    act.wait_ge(s_q, c * KD + j + 1)
                    act.activation(qT_hi[:, j, :], bank[4 + j][:, :], ACT.Identity, bias=bq[:, j:j + 1])
                    act.activation(q2[:, j, :], bank[4 + j][:, :], ACT.Square, bias=bq[:, j:j + 1]).then_inc(s_qact, 1)
                act.wait_ge(s_fl, c + 1)
                for t in range(TPC):
                    act.wait_ge(s_kb, c * TPC + t + 1)
                    ins = act.activation(f[:, t, :], kb[:, t, :], ACT.Square, accum_out=kss[:, t:t + 1])
                ins.then_inc(s_kss, 1)
                for k in range(KD):
                    act.wait_ge(s_kT, c * KD + k + 1)
                    act.copy(kT_hi[:, k, :], bank[k][:, :]).then_inc(s_kTh, 1)
                act.wait_ge(s_nmx, c + 1)
                for t in range(TPC):
                    ins = act.activation(prob[:, t, :], sS[:, t, :], ACT.Exp, bias=nmx[:, t:t + 1],
                                         accum_out=den[:, t:t + 1])
                ins.then_inc(s_p, 1)
                act.wait_ge(s_pT, c + 1)
                act.copy(pT_hi[:, :, :], bank[6][:, :].rearrange("p (t s) -> p t s", t=TPC)).then_inc(s_pTh, 1)
                prep.act_hi(act, c + 1, bank[0:4])

        @block.vector
        def _(dve):
            dve.memset(off[:, :], OFF).then_inc(off_ok, 1)
            dve.wait_ge(off_ok, 1)
            dve.memset(off[0:S, 0:S], 0.0)
            dve.memset(off[S:P, S:P], 0.0).then_inc(off_ok, 1)
            dve.wait_ge(x_in, 16 * NCH)
            prep.dve_stats(dve, 0, 0)
            prep.dve_norm(dve, 0, 0)
            for n in range(2):
                dve.wait_ge(wh_ok, n + 1)
                dve.tensor_tensor(w_lo[n][:, :, :], wraw[n][:, :, :], w_hi[n][:, :, :], ALU.subtract).then_inc(wl_ok, 1)
            dve.wait_ge(const_in, 80)
            dve.tensor_tensor(wqk[:, :], wqk[:, :], qnw[:, :], ALU.mult).then_inc(wqk_ok, 1)
            dve.wait_ge(off_ok, 2)
            dve.wait_ge(wqk_ok, 1)
            prep.dve_lo(dve, 0, bank[4:8])
            with dve.Fori(0, NCH) as c:
                dve.wait_ge(s_css, c + 1)
                dve.tensor_scalar(cve[:, :], css[:, :], 1.0 / D, L0_EPS, ALU.mult, ALU.add).then_inc(s_cve, 1)
                dve.wait_ge(s_crs, c + 1)
                for t in range(TPC):
                    ins = dve.scalar_tensor_tensor(f[:, t, :], craw[:, t, :], crs[:, t:t + 1], fnw[:, :],
                                                   ALU.mult, ALU.mult)
                ins.then_inc(s_f, 1)
                for k in range(KD):
                    dve.wait_ge(s_cTh, c * KD + k + 1)
                    dve.tensor_tensor(cT_lo[:, k, :], bank[k][:, :], cT_hi[:, k, :], ALU.subtract).then_inc(s_cTl, 1)
                for j in range(KD):
                    dve.wait_ge(s_qact, c * KD + j + 1)
                    dve.scalar_tensor_tensor(qT_lo[:, j, :], bank[4 + j][:, :], bq[:, j:j + 1], qT_hi[:, j, :],
                                             ALU.add, ALU.subtract).then_inc(s_ql, 1)
                for t in range(TPC):
                    dve.wait_ge(s_k, c * TPC + t + 1)
                    dve.tensor_tensor(kb[:, t, :], bank[t][:, :], bk[:, :], ALU.add).then_inc(s_kb, 1)
                dve.wait_ge(s_qss, c + 1)
                dve.tensor_scalar(qve[:, :], bank[4][:, 0:TPC], D * L0_EPS, None, ALU.add).then_inc(s_qve, 1)
                dve.wait_ge(s_kss, c + 1)
                dve.tensor_scalar(kve[:, :], kss[:, :], 1.0 / D, L0_EPS, ALU.mult, ALU.add).then_inc(s_kve, 1)
                dve.wait_ge(s_krs, c + 1)
                for t in range(TPC):
                    ins = dve.scalar_tensor_tensor(kb[:, t, :], kb[:, t, :], krs[:, t:t + 1], wqk[:, :],
                                                   ALU.mult, ALU.mult)
                ins.then_inc(s_kn, 1)
                for k in range(KD):
                    dve.wait_ge(s_kTh, c * KD + k + 1)
                    dve.tensor_tensor(kT_lo[:, k, :], bank[k][:, :], kT_hi[:, k, :], ALU.subtract).then_inc(s_kTl, 1)
                dve.wait_ge(s_qrs, c + 1)
                dve.wait_ge(s_s, c + 1)
                for t in range(TPC):
                    ins = dve.scalar_tensor_tensor(sS[:, t, :], bank[5][:, t * P:(t + 1) * P], qrs[:, t:t + 1],
                                                   off[:, :], ALU.mult, ALU.add)
                ins.then_inc(s_sS, 1)
                dve.wait_ge(s_sS, c + 1)
                dve.tensor_reduce(nmx[:, :], sS[:, :, :], AX.X, ALU.max, negate=True).then_inc(s_nmx, 1)
                prep.dve_stats(dve, c + 1, (c + 1) % NCH)
                dve.wait_ge(s_p, c + 1)
                dve.reciprocal(rden[:, :], den[:, :]).then_inc(s_rden, 1)
                prep.dve_norm(dve, c + 1, (c + 1) % NCH)
                dve.wait_ge(s_pTh, c + 1)
                dve.tensor_tensor(pT_lo[:, :, :], bank[6][:, :].rearrange("p (t s) -> p t s", t=TPC), pT_hi[:, :, :],
                                  ALU.subtract).then_inc(s_pTl, 1)
                prep.dve_lo(dve, c + 1, bank[0:4])
                dve.wait_ge(s_rden, c + 1)
                for t in range(TPC):
                    dve.wait_ge(s_att, c * TPC + t + 1)
                    xt = m.x[:, bass.ts(c * TPC + t, D)]
                    dve.scalar_tensor_tensor(xt, bank[[4, 5, 7, 6][t]][:, :], rden[:, t:t + 1], xt,
                                             ALU.mult, ALU.add).then_inc(s_x, 1)

        @block.tensor
        def _(pe):
            pe.wait_ge(ident_ok, 1)
            pe.wait_ge(half_ok, 2)
            prep.pe_transpose(pe, 0, bank[4:8])
            prep.wait_ready(pe, 0)
            pe.wait_ge(wl_ok, 2)
            with pe.Fori(0, NCH) as c:
                pe.wait_ge(s_f, c + 1)
                for k in range(KD):
                    for t in range(TPC):
                        ins = pe.transpose(bank[k][:, t * P:(t + 1) * P], f[:, t, k * P:(k + 1) * P], m.ident[:, :])
                    ins.then_inc(s_cT, 1)
                for j in range(KD):
                    for k in range(KD):
                        cols = slice(j * P, (j + 1) * P)
                        ins = split_mm(pe, bank[4 + j][:, :], w_hi[0][:, k, cols], w_lo[0][:, k, cols],
                                       m.xT_hi[:, k, :], m.xT_lo[:, k, :], k == 0, k == KD - 1)
                    ins.then_inc(s_q, 1)
                pe.wait_ge(s_cTl, (c + 1) * KD)
                for t in range(TPC):
                    for k in range(KD):
                        rows = slice(t * P, (t + 1) * P)
                        ins = split_mm(pe, bank[t][:, :], cT_hi[:, k, rows], cT_lo[:, k, rows],
                                       w_hi[1][:, k, :], w_lo[1][:, k, :], k == 0, k == KD - 1)
                    ins.then_inc(s_k, 1)
                pe.wait_ge(s_ql, (c + 1) * KD)
                for t in range(TPC):
                    for j in range(KD):
                        ins = pe.matmul(bank[4][:, t:t + 1], q2[:, j, t * P:(t + 1) * P], m.ones[:, :],
                                        start=(j == 0), stop=(j == KD - 1))
                ins.then_inc(s_qss, 1)
                pe.wait_ge(s_kn, c + 1)
                for k in range(KD):
                    for t in range(TPC):
                        ins = pe.transpose(bank[k][:, t * P:(t + 1) * P], kb[:, t, k * P:(k + 1) * P], m.ident[:, :])
                    ins.then_inc(s_kT, 1)
                pe.wait_ge(s_kTl, (c + 1) * KD)
                for t in range(TPC):
                    rows = slice(t * P, (t + 1) * P)
                    for k in range(KD):
                        ins = split_mm(pe, bank[5][:, rows], qT_hi[:, k, rows], qT_lo[:, k, rows],
                                       kT_hi[:, k, rows], kT_lo[:, k, rows], k == 0, k == KD - 1)
                ins.then_inc(s_s, 1)
                pe.wait_ge(s_p, c + 1)
                for t in range(TPC):
                    ins = pe.transpose(bank[6][:, t * P:(t + 1) * P], prob[:, t, :], m.ident[:, :])
                ins.then_inc(s_pT, 1)
                pe.wait_ge(s_fl, c + 1)
                prep.pe_transpose(pe, c + 1, bank[0:4])
                pe.wait_ge(s_pTl, c + 1)
                for t in range(TPC):
                    b = bank[[4, 5, 7, 6][t]]
                    ins = split_mm(pe, b[:, :], pT_hi[:, t, :], pT_lo[:, t, :], f_hi[:, t, :], f_lo[:, t, :], True, True)
                    ins.then_inc(s_att, 1)
                prep.wait_ready(pe, c + 1)
                pe.wait_ge(s_x, (c + 1) * TPC)


def stage_sparse_ffn(nc, m, prep, a):
    p0 = NCH
    with ExitStack() as ctx:
        sb = lambda n, s, d=F32: ctx.enter_context(nc.sbuf_tensor("f0_" + n, s, d))
        sem = lambda n: ctx.enter_context(nc.semaphore("f0_" + n))
        bank = m.bank
        w1_hi, w1_lo = sb("w1_hi", [P, KD, INTER], F32R), sb("w1_lo", [P, KD, INTER], F32R)
        w2_hi, w2_lo = sb("w2_hi", [P, NI, D], F32R), sb("w2_lo", [P, NI, D], F32R)
        h = sb("h", [P, INTER])
        raw = [h[:, :], m.xln[:, :, :].rearrange("p t d -> p (t d)")[:, 0:INTER]]
        c1raw = sb("c1raw", [P, KD, RK3])
        c1_hi, c1_lo = sb("c1_hi", [P, KD, RK3], F32R), sb("c1_lo", [P, KD, RK3], F32R)
        c2st = sb("c2st", [RK3, INTER], F32R)
        low = sb("low", [RK3, CHUNK], F32R)
        desc = sb("desc", [P, SPARSE], BF16)
        desc_i = sb("desc_i", [P, SPARSE], I32)
        bmax = [sb(f"bmax{n}", [P, BPQ]) for n in range(2)]
        eq = [sb(f"eq{n}", [P, QC], BF16) for n in range(2)]
        rank = [sb(f"rank{n}", [P, QC], BF16) for n in range(2)]
        rmax = [sb(f"rmax{n}", [P, BPQ], BF16) for n in range(2)]
        hT_hi, hT_lo = sb("hT_hi", [P, NI, P], F32R), sb("hT_lo", [P, NI, P], F32R)

        raw_in, wh_ok, wl_ok = [sem("raw0_in"), sem("raw1_in")], sem("w_hi_ok"), sem("w_lo_ok")
        c1_zero, c1_in, c1h_ok, c1l_ok, c2_ok = sem("c1_zero"), sem("c1_in"), sem("c1_hi_ok"), sem("c1_lo_ok"), sem("c2_ok")
        iota_ok, desc_ok = sem("iota_ok"), sem("desc_ok")
        s_low, s_lowh, s_lowl = sem("low_ps"), sem("low_hi_ok"), sem("low_ok")
        s_i, s_h, s_max, s_eq, s_rank = sem("inter_ps"), sem("h_ps"), sem("bmax_ok"), sem("eq_ok"), sem("rank_ok")
        s_rmax, s_hot, s_hm = sem("rmax_ok"), sem("one_hot_ok"), sem("h_ok")
        s_hT, s_hTh, s_hTl, s_o, s_x = sem("hT_ps"), sem("hT_hi_ok"), sem("hT_lo_ok"), sem("out_ps"), sem("x_ok")
        block = ctx.enter_context(nc.Block())

        def piece(n):
            if n == 0:
                return c2st[:, :], None
            if n <= KD:
                return w1_hi[:, n - 1, :], w1_lo[:, n - 1, :]
            w = slice((n - 1 - KD) * INTER, (n - KD) * INTER)
            return (w2_hi[:, :, :].rearrange("p j d -> p (j d)")[:, w], w2_lo[:, :, :].rearrange("p j d -> p (j d)")[:, w])

        NP = 1 + 2 * KD
        TG = [slice(4 * g, min(4 * g + 4, NI)) for g in range(NQ)]

        @block.sync
        def _(sp):
            for n in range(3):
                if n == 0:
                    sp.wait_ge(c1_zero, 2)
                sp.dma_start(c1raw[:, :, 32 * n:32 * n + RANK], a.c1).then_inc(c1_in, 16)
                sp.dma_start(raw[0][32 * n:32 * n + RANK, :], a.c2).then_inc(raw_in[0], 16)
            for n in range(1, NP):
                if n >= 2:
                    sp.wait_ge(wl_ok, n - 1)
                src = a.w1[:, n - 1, :] if n <= KD else a.w2[:, (n - 1 - KD) * INTER:(n - KD) * INTER]
                sp.dma_start(raw[n % 2], src).then_inc(raw_in[n % 2], 16)

        @block.gpsimd
        def _(pool):
            pool.memset(c1raw[:, :, :], 0.0).then_inc(c1_zero, 1)
            pool.memset(raw[0][0:RK3, :], 0.0).then_inc(c1_zero, 1)
            pool.wait_ge(c1_zero, 2)
            pool.iota(desc_i[:, :], pattern=[[-1, SPARSE]], base=SPARSE, channel_multiplier=0).then_inc(iota_ok, 1)
            pool.wait_ge(iota_ok, 1)
            pool.tensor_copy(desc[:, :], desc_i[:, :]).then_inc(desc_ok, 1)
            pool.wait_ge(desc_ok, 1)
            with pool.Fori(0, NCH) as c:
                for t in range(TPC):
                    for q in range(NQ):
                        n = c * TPC * NQ + t * NQ + q
                        pool.wait_ge(s_eq, n + 1)
                        pool.tensor_tensor(rank[q % 2][:, :].rearrange("p (b s) -> p b s", s=SPARSE),
                                           eq[q % 2][:, :].rearrange("p (b s) -> p b s", s=SPARSE),
                                           desc[:, :].unsqueeze(1).broadcast_to([P, BPQ, SPARSE]),
                                           ALU.mult).then_inc(s_rank, 1)
                prep.pool_rstd(pool, p0 + c + 1)

        @block.scalar
        def _(act):
            act.wait_ge(c1_in, 48)
            act.copy(c1_hi[:, :, :], c1raw[:, :, :]).then_inc(c1h_ok, 1)
            for n in range(NP):
                act.wait_ge(raw_in[n % 2], 16 * (n // 2 + (3 if n % 2 == 0 else 1)))
                src = raw[0][0:RK3, :] if n == 0 else raw[n % 2]
                act.copy(piece(n)[0], src).then_inc(wh_ok, 1)
            with act.Fori(0, NCH) as c:
                act.wait_ge(s_low, c + 1)
                act.copy(low[:, :], bank[6][0:RK3, :]).then_inc(s_lowh, 1)
                for t in range(1, TPC + 1):
                    for g in range(NQ):
                        w = TG[g].stop - TG[g].start
                        act.wait_ge(s_hT, (c * TPC + t - 1) * NQ + g + 1)
                        act.copy(hT_hi[:, TG[g], :], bank[4 + g % 2][:, 0:w * P].rearrange("p (j s) -> p j s", s=P))\
                           .then_inc(s_hTh, 1)
                prep.act_hi(act, p0 + c + 1, bank[0:4])

        @block.vector
        def _(dve):
            dve.wait_ge(c1h_ok, 1)
            dve.tensor_tensor(c1_lo[:, :, :], c1raw[:, :, :], c1_hi[:, :, :], ALU.subtract).then_inc(c1l_ok, 1)
            for n in range(NP):
                dve.wait_ge(wh_ok, n + 1)
                hi, lo = piece(n)
                if n == 0:
                    dve.tensor_tensor(c2st[64:96, :], raw[0][64:96, :], c2st[64:96, :], ALU.subtract).then_inc(wl_ok, 1)
                else:
                    dve.tensor_tensor(lo, raw[n % 2], hi, ALU.subtract).then_inc(wl_ok, 1)

            def find_max(c, t, q):
                n = c * TPC * NQ + t * NQ + q
                inter = bank[q % 2][:, 0:QC].rearrange("p (b s) -> p b s", s=SPARSE)
                dve.wait_ge(s_i, n + 1)
                dve.tensor_reduce(bmax[q % 2][:, :], inter, AX.X, ALU.max).then_inc(s_max, 1)
                dve.wait_ge(s_max, n + 1)
                dve.tensor_tensor(eq[q % 2][:, :].rearrange("p (b s) -> p b s", s=SPARSE), inter,
                                  bmax[q % 2][:, :].unsqueeze(2).broadcast_to([P, BPQ, SPARSE]),
                                  ALU.is_equal).then_inc(s_eq, 1)

            def select(c, t, q):
                n = c * TPC * NQ + t * NQ + q
                rk = rank[q % 2][:, :].rearrange("p (b s) -> p b s", s=SPARSE)
                dve.wait_ge(s_rank, n + 1)
                dve.tensor_reduce(rmax[q % 2][:, :], rk, AX.X, ALU.max).then_inc(s_rmax, 1)
                dve.wait_ge(s_rmax, n + 1)
                dve.tensor_tensor(rank[q % 2][:, :].rearrange("p (b s) -> p b s", s=SPARSE), rk,
                                  rmax[q % 2][:, :].unsqueeze(2).broadcast_to([P, BPQ, SPARSE]),
                                  ALU.is_equal).then_inc(s_hot, 1)
                dve.wait_ge(s_hot, n + 1)
                dve.wait_ge(s_h, n + 1)
                dve.scalar_tensor_tensor(h[:, q * QC:(q + 1) * QC], bank[2 + q % 2][:, 0:QC], 0.0, rank[q % 2][:, :],
                                         ALU.max, ALU.mult).then_inc(s_hm, 1)

            def hidden_lo(c, t, g):
                w = TG[g].stop - TG[g].start
                dve.wait_ge(s_hTh, (c * TPC + t) * NQ + g + 1)
                dve.tensor_tensor(hT_lo[:, TG[g], :], bank[4 + g % 2][:, 0:w * P].rearrange("p (j s) -> p j s", s=P),
                                  hT_hi[:, TG[g], :], ALU.subtract).then_inc(s_hTl, 1)

            def add_out(c, t):
                dve.wait_ge(s_o, c * TPC + t + 1)
                xt = m.x[:, bass.ts(c * TPC + t, D)]
                dve.tensor_tensor(xt, bank[6 + t % 2][:, :], xt, ALU.add).then_inc(s_x, 1)

            with dve.Fori(0, NCH) as c:
                dve.wait_ge(s_lowh, c + 1)
                dve.tensor_tensor(low[32:64, :], bank[6][32:64, :], low[32:64, :], ALU.subtract).then_inc(s_lowl, 1)
                for t in range(TPC):
                    for q in range(NQ):
                        find_max(c, t, q)
                        if t >= 1:
                            hidden_lo(c, t - 1, q)
                        if q >= 1:
                            select(c, t, q - 1)
                    select(c, t, NQ - 1)
                    if t >= 1:
                        add_out(c, t - 1)
                for g in range(NQ):
                    hidden_lo(c, TPC - 1, g)
                prep.dve_stats(dve, p0 + c + 1, (c + 1) % NCH)
                prep.dve_norm(dve, p0 + c + 1, (c + 1) % NCH)
                add_out(c, TPC - 1)
                prep.dve_lo(dve, p0 + c + 1, bank[0:4])

        @block.tensor
        def _(pe):
            def hidden_T(c, t, g):
                pe.wait_ge(s_hm, (c * TPC + t + 1) * NQ)
                if g >= 2:
                    pe.wait_ge(s_hTl, (c * TPC + t) * NQ + g - 1)
                for n, j in enumerate(range(TG[g].start, TG[g].stop)):
                    ins = pe.transpose(bank[4 + g % 2][:, n * P:(n + 1) * P], h[:, j * P:(j + 1) * P], m.ident[:, :])
                ins.then_inc(s_hT, 1)

            def out_rows(c, t):
                pe.wait_ge(s_hTl, (c * TPC + t + 1) * NQ)
                if t >= 2:
                    pe.wait_ge(s_x, c * TPC + t - 1)
                for j in range(NI):
                    ins = split_mm(pe, bank[6 + t % 2][:, :], hT_hi[:, j, :], hT_lo[:, j, :], w2_hi[:, j, :], w2_lo[:, j, :],
                                   j == 0, j == NI - 1)
                ins.then_inc(s_o, 1)

            pe.wait_ge(c1l_ok, 1)
            pe.wait_ge(wl_ok, 1 + KD)
            with pe.Fori(0, NCH) as c:
                for k in range(KD):
                    ins = split_mm(pe, bank[6][0:RK3, :], c1_hi[:, k, :], c1_lo[:, k, :], m.xT_hi[:, k, :], m.xT_lo[:, k, :],
                                   k == 0, k == KD - 1)
                ins.then_inc(s_low, 1)
                pe.wait_ge(s_lowl, c + 1)
                for t in range(TPC):
                    rows = slice(t * P, (t + 1) * P)
                    for q in range(NQ):
                        cols = slice(q * QC, (q + 1) * QC)
                        if t >= 1:
                            hidden_T(c, t - 1, q)
                        if t >= 1 or q >= 2:
                            pe.wait_ge(s_eq, c * TPC * NQ + t * NQ + q - 1)
                        pe.matmul(bank[q % 2][:, 0:QC], low[:, rows], c2st[:, cols], start=True, stop=True).then_inc(s_i, 1)
                        if t >= 1 or q >= 2:
                            pe.wait_ge(s_hm, c * TPC * NQ + t * NQ + q - 1)
                        for k in range(KD):
                            ins = split_mm(pe, bank[2 + q % 2][:, 0:QC], m.xT_hi[:, k, rows], m.xT_lo[:, k, rows],
                                           w1_hi[:, k, cols], w1_lo[:, k, cols], k == 0, k == KD - 1)
                        ins.then_inc(s_h, 1)
                    if t == 1:
                        pe.wait_ge(wl_ok, NP)
                    if t >= 1:
                        out_rows(c, t - 1)
                for g in range(NQ):
                    hidden_T(c, TPC - 1, g)
                out_rows(c, TPC - 1)
                prep.pe_transpose(pe, p0 + c + 1, bank[0:4])
                prep.wait_ready(pe, p0 + c + 1)
                pe.wait_ge(s_x, (c + 1) * TPC)


def stage_l1_attention(nc, m, prep, a):
    p0 = 2 * NCH
    with ExitStack() as ctx:
        sb = lambda n, s, d=F32: ctx.enter_context(nc.sbuf_tensor("a1_" + n, s, d))
        sem = lambda n: ctx.enter_context(nc.semaphore("a1_" + n))
        bank = m.bank
        q_raw, kv_raw, o_raw = sb("q_raw", [P, KD, G * HD]), sb("kv_raw", [P, KD, 2 * HD]), sb("o_raw", [P, G, D])
        wq_hi, wq_lo = sb("wq_hi", [P, KD, G * HD], F32R), sb("wq_lo", [P, KD, G * HD], F32R)
        wkv_hi, wkv_lo = sb("wkv_hi", [P, KD, 2 * HD], F32R), sb("wkv_lo", [P, KD, 2 * HD], F32R)
        wo_hi, wo_lo = sb("wo_hi", [P, G, D], F32R), sb("wo_lo", [P, G, D], F32R)
        craw = sb("craw", [P, KD, CHUNK])
        cT_hi, cT_lo = sb("cT_hi", [P, KD, CHUNK], F32R), sb("cT_lo", [P, KD, CHUNK], F32R)
        qT_hi, qT_lo = sb("qT_hi", [P, G, CHUNK], F32R), sb("qT_lo", [P, G, CHUNK], F32R)
        q2 = [sb(f"q2_{n}", [P, CHUNK]) for n in range(2)]
        v_hi, v_lo = sb("v_hi", [P, TPC, HD], F32R), sb("v_lo", [P, TPC, HD], F32R)
        kn = sb("kn", [P, TPC, HD])
        kT_hi, kT_lo = sb("kT_hi", [P, CHUNK], F32R), sb("kT_lo", [P, CHUNK], F32R)
        prob = sb("prob", [P, TPC, G * P])
        pT_hi = [sb(f"pT_hi{n}", [P, G * P], F32R) for n in range(2)]
        pT_lo = [sb(f"pT_lo{n}", [P, G * P], F32R) for n in range(2)]
        oT_hi, oT_lo = sb("oT_hi", [P, TPC, G * P], F32R), sb("oT_lo", [P, TPC, G * P], F32R)
        mask, wqk, knw = sb("mask", [P, P]), sb("wqk", [P, 1]), sb("knw", [P, 1])
        kss, kve, krs = sb("kss", [P, TPC]), sb("kve", [P, TPC]), sb("krs", [P, TPC])
        qve, qrs = sb("qve", [P, TPC * G]), sb("qrs", [P, TPC * G])
        nmx, den, rden = sb("nmx", [P, TPC * G]), sb("den", [P, TPC * G]), sb("rden", [P, TPC * G])

        q_in, kv_in, o_in, c_in, const_in = sem("wq_in"), sem("wkv_in"), sem("wo_in"), sem("ctx_in"), sem("const_in")
        mask_ok, wqk_ok = sem("mask_ok"), sem("wqk_ok")
        wqh_ok, wql_ok, wkvh_ok, wkvl_ok = sem("wq_hi_ok"), sem("wq_ok"), sem("wkv_hi_ok"), sem("wkv_ok")
        woh_ok, wol_ok, s_cTh, s_cTl = sem("wo_hi_ok"), sem("wo_ok"), sem("cT_hi_ok"), sem("cT_ok")
        s_kv, s_kvact, s_vl, s_kve, s_krs, s_kn = (sem("kv_ps"), sem("kv_act"), sem("v_ok"), sem("kve_ok"),
                                                   sem("krs_ok"), sem("kn_ok"))
        s_kT, s_kTh, s_kTl = sem("kT_ps"), sem("kT_hi_ok"), sem("kT_ok")
        s_q, s_qact, s_ql, s_qss, s_qve, s_qrs = (sem("q_ps"), sem("q_act"), sem("q_ok"), sem("qss_ps"),
                                                  sem("qve_ok"), sem("qrs_ok"))
        s_s, s_sS, s_nmx, s_e, s_rden, s_p = (sem("s_ps"), sem("scores_ok"), sem("nmx_ok"), sem("exp_ok"),
                                              sem("rden_ok"), sem("prob_ok"))
        s_pT, s_pTh, s_pTl = sem("pT_ps"), sem("pT_hi_ok"), sem("pT_ok")
        s_pv, s_oTh, s_oTl, s_o, s_x = sem("pv_ps"), sem("oT_hi_ok"), sem("oT_ok"), sem("o_ps"), sem("x_ok")
        block = ctx.enter_context(nc.Block())
        prep_banks = [bank[2], bank[3], bank[6], bank[7]]
        NIT = NCH * KVH
        PT_PV = [("pT", 0), ("pT", 1), ("pv", 0), ("pT", 2), ("pv", 1), ("pT", 3), ("pv", 2), ("pv", 3)]

        @block.sync
        def _(sp):
            sp.dma_start(kv_raw[:, :, :], a.l1_wkv[0]).then_inc(kv_in, 16)
            sp.dma_start(q_raw[:, :, :], a.l1_wq[0]).then_inc(q_in, 16)
            sp.dma_start(o_raw[:, :, :], a.l1_wo[0]).then_inc(o_in, 16)
            with sp.Fori(1, NIT) as i:
                sp.wait_ge(wkvl_ok, i)
                sp.dma_start(kv_raw[:, :, :], a.l1_wkv[i % KVH]).then_inc(kv_in, 16)
                sp.wait_ge(wql_ok, i)
                sp.dma_start(q_raw[:, :, :], a.l1_wq[i % KVH]).then_inc(q_in, 16)
                sp.wait_ge(wol_ok, i)
                sp.dma_start(o_raw[:, :, :], a.l1_wo[i % KVH]).then_inc(o_in, 16)
            sp.wait_ge(wkvl_ok, NIT)
            sp.dma_start(kv_raw[:, :, :], a.l1_wkv[0]).then_inc(kv_in, 16)
            sp.wait_ge(wql_ok, NIT)
            sp.dma_start(q_raw[:, :, :], a.l1_wq[0]).then_inc(q_in, 16)

        @block.gpsimd
        def _(pool):
            def split_kv(i):
                pool.wait_ge(wkvh_ok, i + 1)
                pool.tensor_tensor(wkv_lo[:, :, :], kv_raw[:, :, :], wkv_hi[:, :, :], ALU.subtract).then_inc(wkvl_ok, 1)

            def split_q(i):
                pool.wait_ge(wqh_ok, i + 1)
                pool.tensor_tensor(wq_lo[:, :, :], q_raw[:, :, :], wq_hi[:, :, :], ALU.subtract).then_inc(wql_ok, 1)

            def split_o(i):
                pool.wait_ge(woh_ok, i + 1)
                pool.tensor_tensor(wo_lo[:, :, :], o_raw[:, :, :], wo_hi[:, :, :], ALU.subtract).then_inc(wol_ok, 1)

            def split_ctx(c):
                pool.wait_ge(s_cTh, c + 1)
                pool.tensor_tensor(cT_lo[:, :, :], craw[:, :, :], cT_hi[:, :, :], ALU.subtract).then_inc(s_cTl, 1)

            def body(i, first):
                pool.wait_ge(s_kve, i + 1)
                pool.tensor_tensor(krs[:, :], kve[:, :], m.neg_half[:, 0:TPC], ALU.pow).then_inc(s_krs, 1)
                if not first:
                    split_o(i - 1)
                pool.wait_ge(s_qve, i + 1)
                pool.tensor_tensor(qrs[:, :], qve[:, :], m.neg_half[:, :], ALU.pow).then_inc(s_qrs, 1)
                for t in range(TPC):
                    pool.wait_ge(s_rden, i * TPC + t + 1)
                    pt = prob[:, t, :].rearrange("p (j s) -> p j s", j=G)
                    pool.tensor_tensor(pt, pt, rden[:, t * G:(t + 1) * G].unsqueeze(2).broadcast_to([P, G, P]),
                                       ALU.mult).then_inc(s_p, 1)
                split_kv(i + 1)
                split_q(i + 1)

            pool.memset(mask[:, :], OFF).then_inc(mask_ok, 1)
            split_ctx(0)
            split_kv(0)
            split_q(0)
            with pool.Fori(0, NCH) as c:
                body(c * KVH, True)
                with pool.Fori(1, KVH) as g:
                    body(c * KVH + g, False)
                split_o(c * KVH + KVH - 1)
                prep.pool_rstd(pool, p0 + c + 1)
                split_ctx(c + 1)

        @block.scalar
        def _(act):
            def split_kv(i):
                act.wait_ge(kv_in, (i + 1) * 16)
                act.copy(wkv_hi[:, :, :], kv_raw[:, :, :]).then_inc(wkvh_ok, 1)

            def split_q(i):
                act.wait_ge(q_in, (i + 1) * 16)
                act.copy(wq_hi[:, :, :], q_raw[:, :, :]).then_inc(wqh_ok, 1)

            def split_o(i):
                act.wait_ge(o_in, (i + 1) * 16)
                act.copy(wo_hi[:, :, :], o_raw[:, :, :]).then_inc(woh_ok, 1)

            def split_ctx(c):
                act.wait_ge(c_in, (c + 1) * 16)
                act.copy(cT_hi[:, :, :], craw[:, :, :]).then_inc(s_cTh, 1)

            def body(i, first):
                for b in range(2):
                    act.wait_ge(s_kv, i * 2 + b + 1)
                    kv = bank[b][:, :].rearrange("p (t w) -> p t w", t=2)
                    act.copy(v_hi[:, 2 * b:2 * b + 2, :], kv[:, :, HD:])
                    for u in range(2):
                        ins = act.activation(kn[:, 2 * b + u, :], kv[:, u, 0:HD], ACT.Square,
                                             accum_out=kss[:, 2 * b + u:2 * b + u + 1])
                    ins.then_inc(s_kvact, 1)
                for j in range(G):
                    if j == G - 1:
                        act.wait_ge(s_kT, i + 1)
                        act.activation(kT_hi[:, :], bank[4][:, :], ACT.Copy, scale=wqk[:, :]).then_inc(s_kTh, 1)
                    act.wait_ge(s_q, i * G + j + 1)
                    act.copy(qT_hi[:, j, :], bank[2 + j % 2][:, :])
                    act.activation(q2[j % 2][:, :], bank[2 + j % 2][:, :], ACT.Square).then_inc(s_qact, 1)
                if not first:
                    split_o(i - 1)
                for t in range(TPC):
                    act.wait_ge(s_nmx, i * TPC + t + 1)
                    for j in range(G):
                        pt = prob[:, t, j * P:(j + 1) * P]
                        ins = act.activation(pt, pt, ACT.Exp, bias=nmx[:, t * G + j:t * G + j + 1],
                                             accum_out=den[:, t * G + j:t * G + j + 1])
                    ins.then_inc(s_e, 1)
                split_kv(i + 1)
                split_q(i + 1)
                for what, t in PT_PV:
                    if what == "pT":
                        act.wait_ge(s_pT, i * TPC + t + 1)
                        act.copy(pT_hi[t % 2][:, :], bank[6 + t % 2][:, :]).then_inc(s_pTh, 1)
                    else:
                        act.wait_ge(s_pv, i * TPC + t + 1)
                        act.copy(oT_hi[:, t, :], bank[4 + t % 2][:, :]).then_inc(s_oTh, 1)

            act.dma_start(craw[:, :, :], a.ctxT[0]).then_inc(c_in, 16)
            act.dma_start(wqk[:, :], a.l1_qnw).then_inc(const_in, 16)
            act.dma_start(knw[:, :], a.l1_knw).then_inc(const_in, 16)
            act.wait_ge(mask_ok, 1)
            act.dma_start(mask[0:S, 0:S], a.mask).then_inc(const_in, 16)
            act.dma_start(mask[S:P, S:P], a.mask).then_inc(const_in, 16)
            split_ctx(0)
            split_kv(0)
            split_q(0)
            act.wait_ge(wqk_ok, 1)
            with act.Fori(0, NCH) as c:
                act.wait_ge(s_cTl, c + 1)
                act.dma_start(craw[:, :, :], a.ctxT[(c + 1) % NCH]).then_inc(c_in, 16)
                body(c * KVH, True)
                with act.Fori(1, KVH) as g:
                    body(c * KVH + g, False)
                split_o(c * KVH + KVH - 1)
                split_ctx(c + 1)
                prep.act_hi(act, p0 + c + 1, prep_banks)

        @block.vector
        def _(dve):
            def add_out(i, chunk, t):
                dve.wait_ge(s_o, i * TPC + t + 1)
                xt = m.x[:, bass.ts(chunk * TPC + t, D)]
                dve.tensor_tensor(xt, bank[t % 2][:, :], xt, ALU.add).then_inc(s_x, 1)

            def query_lo(i, j):
                dve.wait_ge(s_qact, i * G + j + 1)
                dve.tensor_tensor(qT_lo[:, j, :], bank[2 + j % 2][:, :], qT_hi[:, j, :], ALU.subtract).then_inc(s_ql, 1)

            def body(c, i, first):
                for b in range(2):
                    dve.wait_ge(s_kvact, i * 2 + b + 1)
                    kv = bank[b][:, :].rearrange("p (t w) -> p t w", t=2)
                    dve.tensor_tensor(v_lo[:, 2 * b:2 * b + 2, :], kv[:, :, HD:], v_hi[:, 2 * b:2 * b + 2, :],
                                      ALU.subtract).then_inc(s_vl, 1)
                dve.tensor_scalar(kve[:, :], kss[:, :], 1.0 / HD, L1_EPS, ALU.mult, ALU.add).then_inc(s_kve, 1)
                query_lo(i, 0)
                dve.wait_ge(s_krs, i + 1)
                for t in range(TPC):
                    ins = dve.tensor_scalar(kn[:, t, :], bank[t // 2][:, (t % 2) * 2 * HD:(t % 2) * 2 * HD + HD],
                                            krs[:, t:t + 1], None, ALU.mult)
                ins.then_inc(s_kn, 1)
                for j in range(1, G):
                    if j == G - 1:
                        dve.wait_ge(s_kTh, i + 1)
                        dve.scalar_tensor_tensor(kT_lo[:, :], bank[4][:, :], wqk[:, :], kT_hi[:, :],
                                                 ALU.mult, ALU.subtract).then_inc(s_kTl, 1)
                    query_lo(i, j)
                dve.wait_ge(s_qss, i + 1)
                dve.tensor_scalar(qve[:, :], bank[5][:, 0:TPC * G], HD * L1_EPS, None, ALU.add).then_inc(s_qve, 1)
                dve.wait_ge(s_qrs, i + 1)
                for t in range(TPC):
                    dve.wait_ge(s_s, i * TPC + t + 1)
                    for j in range(G):
                        cols = slice(j * P, (j + 1) * P)
                        ins = dve.scalar_tensor_tensor(prob[:, t, cols], bank[6 + t % 2][:, cols],
                                                       qrs[:, t * G + j:t * G + j + 1], mask[:, :], ALU.mult, ALU.add)
                    ins.then_inc(s_sS, 1)
                    dve.wait_ge(s_sS, i * TPC + t + 1)
                    dve.tensor_reduce(nmx[:, t * G:(t + 1) * G], prob[:, t, :].rearrange("p (j s) -> p j s", j=G),
                                      AX.X, ALU.max, negate=True).then_inc(s_nmx, 1)
                for t in range(TPC):
                    dve.wait_ge(s_e, i * TPC + t + 1)
                    dve.reciprocal(rden[:, t * G:(t + 1) * G], den[:, t * G:(t + 1) * G]).then_inc(s_rden, 1)
                    if not first and t >= 1:
                        add_out(i - 1, c, t - 1)
                if not first:
                    add_out(i - 1, c, TPC - 1)
                for what, t in PT_PV:
                    if what == "pT":
                        dve.wait_ge(s_pTh, i * TPC + t + 1)
                        dve.tensor_tensor(pT_lo[t % 2][:, :], bank[6 + t % 2][:, :], pT_hi[t % 2][:, :],
                                          ALU.subtract).then_inc(s_pTl, 1)
                    else:
                        dve.wait_ge(s_oTh, i * TPC + t + 1)
                        dve.tensor_tensor(oT_lo[:, t, :], bank[4 + t % 2][:, :], oT_hi[:, t, :],
                                          ALU.subtract).then_inc(s_oTl, 1)

            dve.wait_ge(const_in, 64)
            dve.tensor_tensor(wqk[:, :], wqk[:, :], knw[:, :], ALU.mult).then_inc(wqk_ok, 1)
            dve.wait_ge(wqk_ok, 1)
            with dve.Fori(0, NCH) as c:
                body(c, c * KVH, True)
                with dve.Fori(1, KVH) as g:
                    body(c, c * KVH + g, False)
                prep.dve_stats(dve, p0 + c + 1, (c + 1) % NCH)
                prep.dve_norm(dve, p0 + c + 1, (c + 1) % NCH)
                for t in range(TPC):
                    add_out(c * KVH + KVH - 1, c, t)
                prep.dve_lo(dve, p0 + c + 1, prep_banks)

        @block.tensor
        def _(pe):
            def square_sums(i, j):
                pe.wait_ge(s_qact, i * G + j + 1)
                for t in range(TPC):
                    ins = pe.matmul(bank[5][:, t * G + j:t * G + j + 1], q2[j % 2][:, t * P:(t + 1) * P], m.ones[:, :],
                                    start=True, stop=True)
                return ins

            def out_rows(i):
                pe.wait_ge(wol_ok, i + 1)
                pe.wait_ge(s_oTl, (i + 1) * TPC)
                for t in range(TPC):
                    if t >= 2:
                        pe.wait_ge(s_x, i * TPC + t - 1)
                    for j in range(G):
                        cols = slice(j * P, (j + 1) * P)
                        ins = split_mm(pe, bank[t % 2][:, :], oT_hi[:, t, cols], oT_lo[:, t, cols],
                                       wo_hi[:, j, :], wo_lo[:, j, :], j == 0, j == G - 1)
                    ins.then_inc(s_o, 1)

            def body(i, first):
                pe.wait_ge(wkvl_ok, i + 1)
                for t in range(TPC):
                    rows = slice(t * P, (t + 1) * P)
                    out = bank[t // 2][:, (t % 2) * 2 * HD:(t % 2 + 1) * 2 * HD]
                    for k in range(KD):
                        ins = split_mm(pe, out, cT_hi[:, k, rows], cT_lo[:, k, rows], wkv_hi[:, k, :], wkv_lo[:, k, :],
                                       k == 0, k == KD - 1)
                    if t % 2:
                        ins.then_inc(s_kv, 1)
                pe.wait_ge(wql_ok, i + 1)
                for j in range(G):
                    cols = slice(j * HD, (j + 1) * HD)
                    if j >= 2:
                        pe.wait_ge(s_ql, i * G + j - 1)
                    for k in range(KD):
                        ins = split_mm(pe, bank[2 + j % 2][:, :], wq_hi[:, k, cols], wq_lo[:, k, cols],
                                       m.xT_hi[:, k, :], m.xT_lo[:, k, :], k == 0, k == KD - 1)
                    ins.then_inc(s_q, 1)
                    if j == 1 and not first:
                        pe.wait_ge(s_oTl, i * TPC)
                    if j >= 1:
                        square_sums(i, j - 1)
                    if j == G - 2:
                        pe.wait_ge(s_kn, i + 1)
                        for t in range(TPC):
                            ins = pe.transpose(bank[4][:, t * P:(t + 1) * P], kn[:, t, :], m.ident[:, :])
                        ins.then_inc(s_kT, 1)
                square_sums(i, G - 1).then_inc(s_qss, 1)
                pe.wait_ge(s_kTl, i + 1)
                pe.wait_ge(s_ql, (i + 1) * G)
                for t in range(TPC):
                    rows = slice(t * P, (t + 1) * P)
                    if t >= 2:
                        pe.wait_ge(s_sS, i * TPC + t - 1)
                    for j in range(G):
                        ins = split_mm(pe, bank[6 + t % 2][:, j * P:(j + 1) * P], qT_hi[:, j, rows], qT_lo[:, j, rows],
                                       kT_hi[:, rows], kT_lo[:, rows], True, True)
                    ins.then_inc(s_s, 1)
                pe.wait_ge(s_vl, (i + 1) * 2)
                if not first:
                    out_rows(i - 1)
                for what, t in PT_PV:
                    if what == "pT":
                        pe.wait_ge(s_p, i * TPC + t + 1)
                        if t < 2:
                            pe.wait_ge(s_sS, i * TPC + t + 3)
                        else:
                            pe.wait_ge(s_pTl, i * TPC + t - 1)
                        for j in range(G):
                            cols = slice(j * P, (j + 1) * P)
                            ins = pe.transpose(bank[6 + t % 2][:, cols], prob[:, t, cols], m.ident[:, :])
                        ins.then_inc(s_pT, 1)
                    else:
                        pe.wait_ge(s_pTl, i * TPC + t + 1)
                        if t == 1:
                            pe.wait_ge(s_qve, i + 1)
                        if t >= 2:
                            pe.wait_ge(s_oTl, i * TPC + t - 1)
                        split_mm(pe, bank[4 + t % 2][:, :], v_hi[:, t, :], v_lo[:, t, :], pT_hi[t % 2][:, :],
                                 pT_lo[t % 2][:, :], True, True).then_inc(s_pv, 1)
                if not first:
                    pe.wait_ge(s_x, i * TPC)

            with pe.Fori(0, NCH) as c:
                pe.wait_ge(s_cTl, c + 1)
                body(c * KVH, True)
                with pe.Fori(1, KVH) as g:
                    body(c * KVH + g, False)
                out_rows(c * KVH + KVH - 1)
                prep.pe_transpose(pe, p0 + c + 1, prep_banks)
                prep.wait_ready(pe, p0 + c + 1)
                pe.wait_ge(s_x, (c * KVH + KVH) * TPC)


def stage_gated_ffn(nc, m, prep, a):
    p0 = 3 * NCH
    with ExitStack() as ctx:
        sb = lambda n, s, d=F32: ctx.enter_context(nc.sbuf_tensor("f1_" + n, s, d))
        sem = lambda n: ctx.enter_context(nc.semaphore("f1_" + n))
        bank = m.bank
        w_raw, w_hi, w_lo = sb("w_raw", [P, KD, D]), sb("w_hi", [P, KD, D], F32R), sb("w_lo", [P, KD, D], F32R)
        c_raw, c_hi, c_lo = sb("c_raw", [P, KD, NCL]), sb("c_hi", [P, KD, NCL], F32R), sb("c_lo", [P, KD, NCL], F32R)
        bias = sb("bias", [P, D])
        dense = sb("dense", [P, NT * D])
        lg, ex, hit = sb("logits", [P, TPC, NCL]), sb("ex", [P, TPC, NCL]), sb("hit", [P, TPC, NCL])
        hit_any = sb("hit_any", [P, NCL])
        nmx, nmx10, den, rden, row_sel = (sb("nmx", [P, TPC]), sb("nmx10", [P, TPC]), sb("den", [P, TPC]),
                                          sb("rden", [P, TPC]), sb("row_sel", [P, TPC]))
        assign_i, cluster_id = sb("assign_i", [NCL, D], I32), sb("cluster_id", [NCL, 1], I32)
        assign_f, cluster_f = sb("assign_f", [NCL, D]), sb("cluster_f", [NCL, 1])
        member = sb("member", [NCL, D], BF16)
        cl_sel = sb("cl_sel", [NCL, P], BF16)
        ones_cl = sb("ones_cl", [NCL, P])
        col_sel = sb("col_sel", [P, D])

        w_in, c_in, const_in, out_in = sem("w_in"), sem("cent_in"), sem("const_in"), sem("out_written")
        wh_ok, wl_ok, member_ok = sem("w_hi_ok"), sem("w_ok"), sem("member_ok")
        id_ok, idf_ok, ones_ok, any_ok = sem("id_ok"), sem("idf_ok"), sem("ones_ok"), sem("any_ok")
        s_l, s_nmx, s_nmx10, s_e, s_rden, s_hit, s_any, s_sel = (
            sem("logits_ps"), sem("nmx_ok"), sem("nmx10_ok"), sem("exp_ok"), sem("rden_ok"), sem("hit_ok"),
            sem("hit_any_ok"), sem("row_sel_ok"))
        s_d, s_db, s_dense, s_cnt, s_cl, s_col, s_colsel = (sem("dense_ps"), sem("dense_b_ok"), sem("dense_ok"),
                                                            sem("count_ps"), sem("cl_sel_ok"), sem("col_ps"), sem("col_sel_ok"))
        s_gate, s_gate_p, s_out, s_out_p = sem("gated"), sem("gated_pool"), sem("out_ok"), sem("out_pool_ok")
        block = ctx.enter_context(nc.Block())
        out_rows = a.out.rearrange("(n p) d -> n p d", p=P)
        POOL_TILES = 5
        DVE_TILES = NT - POOL_TILES

        @block.sync
        def _(sp):
            sp.dma_start(c_raw[:, :, :], a.cent).then_inc(c_in, 16)
            sp.dma_start(w_raw[:, :, :], a.l1_w).then_inc(w_in, 16)
            sp.dma_start(assign_i[:, :], a.assign.partition_broadcast(NCL)).then_inc(const_in, 16)
            sp.dma_start(bias[:, :], a.l1_b.partition_broadcast(P)).then_inc(const_in, 16)
            with sp.Fori(0, DVE_TILES) as n:
                sp.wait_ge(s_out, n + 1)
                sp.dma_start(out_rows[n], m.x[:, bass.ts(n, D)]).then_inc(out_in, 16)
            sp.wait_ge(out_in, 16 * NT)

        @block.gpsimd
        def _(pool):
            pool.iota(cluster_id[:, :], pattern=[[0, 1]], base=0, channel_multiplier=1).then_inc(id_ok, 1)
            pool.wait_ge(id_ok, 1)
            pool.memset(hit_any[:, :], 0.0).then_inc(any_ok, 1)
            pool.memset(ones_cl[:, :], 1.0).then_inc(ones_ok, 1)
            pool.wait_ge(ones_ok, 1)
            for p in range(1, NCH):
                prep.pool_rstd(pool, p0 + p)
            pool.wait_ge(s_colsel, 1)
            pool.wait_ge(s_dense, NT)
            with pool.Fori(0, POOL_TILES) as n:
                dn, xt = dense[:, bass.ts(n + DVE_TILES, D)], m.x[:, bass.ts(n + DVE_TILES, D)]
                pool.tensor_tensor(dn, dn, col_sel[:, :], ALU.mult).then_inc(s_gate_p, 1)
                pool.wait_ge(s_gate_p, n + 1)
                pool.tensor_tensor(xt, xt, dn, ALU.add).then_inc(s_out_p, 1)

        @block.scalar
        def _(act):
            act.wait_ge(c_in, 16)
            act.copy(c_hi[:, :, :], c_raw[:, :, :]).then_inc(wh_ok, 1)
            act.wait_ge(w_in, 16)
            act.copy(w_hi[:, :, :], w_raw[:, :, :]).then_inc(wh_ok, 1)

            def chunk(c, last):
                act.wait_ge(s_nmx10, c + 1)
                for t in range(TPC):
                    ins = act.activation(ex[:, t, :], lg[:, t, :], ACT.Exp, bias=nmx10[:, t:t + 1], accum_out=den[:, t:t + 1])
                ins.then_inc(s_e, 1)
                if not last:
                    prep.act_hi(act, p0 + c + 1, bank[0:4])

            with act.Fori(0, NCH - 1) as c:
                chunk(c, False)
            chunk(NCH - 1, True)
            with act.Fori(0, POOL_TILES) as n:
                act.wait_ge(s_out_p, n + 1)
                act.dma_start(out_rows[n + DVE_TILES], m.x[:, bass.ts(n + DVE_TILES, D)]).then_inc(out_in, 16)

        @block.vector
        def _(dve):
            dve.wait_ge(wh_ok, 1)
            dve.tensor_tensor(c_lo[:, :, :], c_raw[:, :, :], c_hi[:, :, :], ALU.subtract).then_inc(wl_ok, 1)
            dve.wait_ge(wh_ok, 2)
            dve.tensor_tensor(w_lo[:, :, :], w_raw[:, :, :], w_hi[:, :, :], ALU.subtract).then_inc(wl_ok, 1)
            dve.wait_ge(id_ok, 1)
            dve.wait_ge(const_in, 32)
            dve.tensor_copy(cluster_f[:, :], cluster_id[:, :])
            dve.tensor_copy(assign_f[:, :], assign_i[:, :]).then_inc(idf_ok, 1)
            dve.wait_ge(idf_ok, 1)
            dve.tensor_scalar(member[:, :], assign_f[:, :], cluster_f[:, :], None, ALU.is_equal).then_inc(member_ok, 1)
            dve.wait_ge(any_ok, 1)

            def chunk(c, last):
                dve.wait_ge(s_l, c + 1)
                lps = bank[4][:, 0:TPC * NCL].rearrange("p (t n) -> p t n", t=TPC)
                dve.tensor_scalar(lg[:, :, :], lps, 10.0, None, ALU.mult).then_inc(s_nmx, 1)
                dve.wait_ge(s_nmx, c + 1)
                dve.tensor_reduce(nmx10[:, :], lg[:, :, :], AX.X, ALU.max, negate=True).then_inc(s_nmx10, 1)
                if not last:
                    prep.dve_stats(dve, p0 + c + 1, c + 1)
                dve.wait_ge(s_e, c + 1)
                dve.reciprocal(rden[:, :], den[:, :]).then_inc(s_rden, 1)
                dve.wait_ge(s_rden, c + 1)
                for t in range(TPC):
                    ins = dve.tensor_scalar(hit[:, t, :], ex[:, t, :], rden[:, t:t + 1], 0.01, ALU.mult, ALU.is_gt)
                ins.then_inc(s_hit, 1)
                dve.wait_ge(s_hit, c + 1)
                dve.tensor_reduce(row_sel[:, :], hit[:, :, :], AX.X, ALU.max).then_inc(s_sel, 1)
                for t in range(TPC):
                    dve.tensor_tensor(hit_any[:, :], hit_any[:, :], hit[:, t, :], ALU.max).then_inc(s_any, 1)
                    dve.wait_ge(s_any, c * TPC + t + 1)
                if not last:
                    prep.dve_norm(dve, p0 + c + 1, c + 1)
                dve.wait_ge(s_sel, c + 1)
                for t in range(TPC):
                    dve.wait_ge(s_d, c * TPC + t + 1)
                    dn = dense[:, bass.ts(c * TPC + t, D)]
                    dve.tensor_tensor(dn, bank[5 + t % 2][:, :], bias[:, :], ALU.add).then_inc(s_db, 1)
                    dve.wait_ge(s_db, c * TPC + t + 1)
                    dve.tensor_scalar(dn, dn, row_sel[:, t:t + 1], None, ALU.mult).then_inc(s_dense, 1)
                if not last:
                    prep.dve_lo(dve, p0 + c + 1, bank[0:4])

            with dve.Fori(0, NCH - 1) as c:
                chunk(c, False)
            chunk(NCH - 1, True)
            dve.wait_ge(s_cnt, 1)
            dve.wait_ge(ones_ok, 1)
            dve.tensor_scalar(cl_sel[:, :], ones_cl[:, :], bank[7][0:NCL, 0:1], None, ALU.is_le).then_inc(s_cl, 1)
            dve.wait_ge(s_col, 1)
            dve.tensor_copy(col_sel[:, :], bank[0][:, :]).then_inc(s_colsel, 1)
            dve.wait_ge(s_colsel, 1)
            dve.wait_ge(s_dense, NT)
            with dve.Fori(0, DVE_TILES) as n:
                dn, xt = dense[:, bass.ts(n, D)], m.x[:, bass.ts(n, D)]
                dve.tensor_tensor(dn, dn, col_sel[:, :], ALU.mult).then_inc(s_gate, 1)
                dve.wait_ge(s_gate, n + 1)
                dve.tensor_tensor(xt, xt, dn, ALU.add).then_inc(s_out, 1)

        @block.tensor
        def _(pe):
            pe.wait_ge(wl_ok, 1)

            def chunk(c, last):
                for t in range(TPC):
                    rows = slice(t * P, (t + 1) * P)
                    for k in range(KD):
                        ins = split_mm(pe, bank[4][:, t * NCL:(t + 1) * NCL], m.xT_hi[:, k, rows], m.xT_lo[:, k, rows],
                                       c_hi[:, k, :], c_lo[:, k, :], k == 0, k == KD - 1)
                ins.then_inc(s_l, 1)
                pe.wait_ge(wl_ok, 2)
                for t in range(TPC):
                    rows = slice(t * P, (t + 1) * P)
                    if t >= 2:
                        pe.wait_ge(s_db, c * TPC + t - 1)
                    for k in range(KD):
                        ins = split_mm(pe, bank[5 + t % 2][:, :], m.xT_hi[:, k, rows], m.xT_lo[:, k, rows],
                                       w_hi[:, k, :], w_lo[:, k, :], k == 0, k == KD - 1)
                    ins.then_inc(s_d, 1)
                if not last:
                    prep.pe_transpose(pe, p0 + c + 1, bank[0:4])
                    prep.wait_ready(pe, p0 + c + 1)
                    pe.wait_ge(s_dense, (c + 1) * TPC)

            with pe.Fori(0, NCH - 1) as c:
                chunk(c, False)
            chunk(NCH - 1, True)
            pe.wait_ge(s_any, NT)
            pe.matmul(bank[7][0:NCL, 0:1], hit_any[:, :], m.ones[:, :], start=True, stop=True).then_inc(s_cnt, 1)
            pe.wait_ge(s_cl, 1)
            pe.wait_ge(member_ok, 1)
            pe.matmul(bank[0][:, :], cl_sel[:, :], member[:, :], start=True, stop=True).then_inc(s_col, 1)


def network(nc, a):
    with ExitStack() as ctx:
        m = persistent(nc, ctx)
        prep = Prep(nc, ctx, m)
        stage_l0_attention(nc, m, prep, a)
        stage_sparse_ffn(nc, m, prep, a)
        stage_l1_attention(nc, m, prep, a)
        stage_gated_ffn(nc, m, prep, a)


def kernel(**inputs):
    import concourse.bacc as bacc
    from concourse.bass_utils import run_bass_kernel_spmd

    given = {n: np.asarray(v) for n, v in inputs.items()}

    def blocks(w, *lead):
        return w.reshape(*lead, -1, P, w.shape[-1]).swapaxes(-3, -2)

    ctx_rows = given["ctx_4096"].reshape(ROWS, D)
    wk = given["L1_xattn_Wk"].T.reshape(D, KVH, HD)
    wv = given["L1_xattn_Wv"].T.reshape(D, KVH, HD)
    laid = {
        "x": given["x"].reshape(ROWS, D),
        "ctx": ctx_rows,
        "ctxT": ctx_rows.reshape(NCH, CHUNK, KD, P).transpose(0, 3, 2, 1),
        "mask": given["mask_1x1xSxS2_ff0"].reshape(S, S),
        "l0_wq": blocks(given["L0_xattn_Wq_w"].T),
        "l0_wk": blocks(given["L0_xattn_Wk_w"].T),
        "l0_bq": given["L0_xattn_Wq_b"].reshape(KD, P).T,
        "l0_bk": given["L0_xattn_Wk_b"],
        "l0_fnw": given["L0_xattn_fn_w"],
        "l0_qnw": given["L0_xattn_qn_w"],
        "l0_knw": given["L0_xattn_kn_w"],
        "c1": blocks(given["L0_ffn_c1_w"].T),
        "c2": given["L0_ffn_c2_w"].T,
        "w1": blocks(given["L0_ffn_w1"].T),
        "w2": blocks(given["L0_ffn_w2t"]).reshape(P, NI * D),
        "l1_wq": blocks(given["L1_xattn_Wq"].T.reshape(D, KVH, G * HD).swapaxes(0, 1), KVH),
        "l1_wkv": blocks(np.concatenate([wk, wv], axis=2).swapaxes(0, 1), KVH),
        "l1_wo": blocks(given["L1_xattn_Wo"].T.reshape(KVH, G * HD, D), KVH),
        "l1_qnw": given["L1_xattn_q_norm_w"].reshape(HD, 1),
        "l1_knw": given["L1_xattn_k_norm_w"].reshape(HD, 1),
        "l1_w": blocks(given["L1_ffn_weight"].T),
        "l1_b": given["L1_ffn_bias"],
        "cent": blocks(given["L1_ffn_centroids"].T),
        "assign": given["L1_ffn_assignments"],
    }
    nc = bacc.Bacc("TRN2", target_bir_lowering=False, num_devices=1)
    a, arrays = Mem(), {}
    for name, v in laid.items():
        v = np.ascontiguousarray(v)
        arrays[f"in_{name}"] = v
        a.__dict__[name] = nc.dram_tensor(f"in_{name}", v.shape, mybir.dt.from_np(v.dtype), kind="ExternalInput").ap()
    a.out = nc.dram_tensor("out_x", (ROWS, D), F32, kind="ExternalOutput").ap()
    network(nc, a)
    r = run_bass_kernel_spmd(nc, [arrays], core_ids=[0])
    return r.results[0]["out_x"].reshape(given["x"].shape)
```

```python
from contextlib import ExitStack

import numpy as np

import concourse.bass as bass
from concourse import mybir

F32 = mybir.dt.float32
F32R = mybir.dt.float32r
BF16 = mybir.dt.bfloat16
I32 = mybir.dt.int32
ALU = mybir.AluOpType
ACT = mybir.ActivationFunctionType
AX = mybir.AxisListType

P = 128
D = 512
KD = D // P
ROWS = 2048
S = 64
CHUNK = 512
TPC = CHUNK // P
NCH = ROWS // CHUNK
NT = ROWS // P
INTER = 1792
NI = INTER // P
QC = 448
NQ = INTER // QC
SPARSE = 32
BPQ = QC // SPARSE
RANK = 16
RK3 = 3 * 32
H = 32
KVH = 8
HD = 128
G = H // KVH
NCL = 64
LN_EPS = 1e-5
L0_EPS = 1e-6
L1_EPS = 1e-5
OFF = -3e38


def split_mm(pe, out, a_hi, a_lo, b_hi, b_lo, first, last):
    pe.matmul(out, a_hi, b_hi, start=first, stop=False)
    pe.matmul(out, a_lo, b_hi, start=False, stop=False)
    return pe.matmul(out, a_hi, b_lo, start=False, stop=last)


class Prep:

    def __init__(self, nc, ctx, mem):
        self.m = mem
        sem = lambda n: ctx.enter_context(nc.semaphore(n))
        self.stat, self.agg, self.var = sem("ln_stat"), sem("ln_agg"), sem("ln_var")
        self.rstd, self.norm, self.ps = sem("ln_rstd"), sem("ln_norm"), sem("xT_ps")
        self.hi, self.lo = sem("xT_hi_done"), sem("xT_lo_done")

    def dve_stats(self, dve, p, cn):
        m = self.m
        for t in range(TPC):
            ins = dve.bn_stats(m.ln_st[:, t, :], m.x[:, bass.ts(cn * TPC + t, D)])
        ins.then_inc(self.stat, 1)
        dve.wait_ge(self.stat, p + 1)
        dve.memset(m.ln_ve[:, :], LN_EPS)
        for t in range(TPC):
            ins = dve.bn_aggr(m.ln_mv[:, t, :], m.ln_st[:, t, :])
        ins.then_inc(self.agg, 1)
        dve.wait_ge(self.agg, p + 1)
        dve.tensor_scalar(m.ln_ve[:, :], m.ln_mv[:, :, 1], LN_EPS, None, ALU.add).then_inc(self.var, 1)

    def pool_rstd(self, pool, p):
        m = self.m
        pool.wait_ge(self.var, p + 1)
        pool.tensor_tensor(m.ln_rs[:, :], m.ln_ve[:, :], m.neg_half[:, 0:TPC], ALU.pow).then_inc(self.rstd, 1)

    def dve_norm(self, dve, p, cn):
        m = self.m
        dve.wait_ge(self.rstd, p + 1)
        for t in range(TPC):
            ins = dve.tensor_scalar(m.xln[:, t, :], m.x[:, bass.ts(cn * TPC + t, D)], m.ln_mv[:, t, 0:1],
                                    m.ln_rs[:, t:t + 1], ALU.subtract, ALU.mult)
        ins.then_inc(self.norm, 1)

    def pe_transpose(self, pe, p, banks):
        m = self.m
        pe.wait_ge(self.norm, p + 1)
        for k in range(KD):
            for t in range(TPC):
                ins = pe.transpose(banks[k][:, t * P:(t + 1) * P], m.xln[:, t, k * P:(k + 1) * P], m.ident[:, :])
            ins.then_inc(self.ps, 1)

    def act_hi(self, act, p, banks):
        for k in range(KD):
            act.wait_ge(self.ps, p * KD + k + 1)
            act.copy(self.m.xT_hi[:, k, :], banks[k][:, :]).then_inc(self.hi, 1)

    def dve_lo(self, dve, p, banks):
        for k in range(KD):
            dve.wait_ge(self.hi, p * KD + k + 1)
            dve.tensor_tensor(self.m.xT_lo[:, k, :], banks[k][:, :], self.m.xT_hi[:, k, :],
                              ALU.subtract).then_inc(self.lo, 1)

    def wait_ready(self, pe, p):
        pe.wait_ge(self.lo, (p + 1) * KD)


class Mem:
    pass


def persistent(nc, ctx):
    m = Mem()
    sb = lambda n, s, d=F32: ctx.enter_context(nc.sbuf_tensor(n, s, d))
    m.x = sb("x_res", [P, NT * D])
    m.xT_hi, m.xT_lo = sb("xT_hi", [P, KD, CHUNK], F32R), sb("xT_lo", [P, KD, CHUNK], F32R)
    m.xln = sb("xln", [P, TPC, D])
    m.ident = sb("ident", [P, P])
    m.ones = sb("ones", [P, 1])
    m.neg_half = sb("neg_half", [P, TPC * G])
    m.ln_st, m.ln_mv = sb("ln_st", [P, TPC, 6]), sb("ln_mv", [P, TPC, 2])
    m.ln_ve, m.ln_rs = sb("ln_ve", [P, TPC]), sb("ln_rs", [P, TPC])
    m.bank = [ctx.enter_context(nc.psum_tensor(f"bank{i}", [P, 512], F32)) for i in range(8)]
    return m


def stage_l0_attention(nc, m, prep, a):
    with ExitStack() as ctx:
        sb = lambda n, s, d=F32: ctx.enter_context(nc.sbuf_tensor("a0_" + n, s, d))
        sem = lambda n: ctx.enter_context(nc.semaphore("a0_" + n))
        bank = m.bank
        wraw = [sb(f"w{n}_raw", [P, KD, D]) for n in "qk"]
        w_hi = [sb(f"w{n}_hi", [P, KD, D], F32R) for n in "qk"]
        w_lo = [sb(f"w{n}_lo", [P, KD, D], F32R) for n in "qk"]
        bq, bk = sb("bq", [P, KD]), sb("bk", [P, D])
        fnw, qnw, wqk = sb("fnw", [P, D]), sb("qnw", [P, D]), sb("wqk", [P, D])
        off = sb("off", [P, P])
        craw, f = sb("craw", [P, TPC, D]), sb("f", [P, TPC, D])
        f_hi, f_lo = sb("f_hi", [P, TPC, D], F32R), sb("f_lo", [P, TPC, D], F32R)
        cT_hi, cT_lo = sb("cT_hi", [P, KD, CHUNK], F32R), sb("cT_lo", [P, KD, CHUNK], F32R)
        qT_hi, qT_lo = sb("qT_hi", [P, KD, CHUNK], F32R), sb("qT_lo", [P, KD, CHUNK], F32R)
        q2 = sb("q2", [P, KD, CHUNK])
        kb = sb("kb", [P, TPC, D])
        kT_hi, kT_lo = cT_hi, cT_lo
        sS, prob = sb("scores", [P, TPC, P]), sb("prob", [P, TPC, P])
        pT_hi, pT_lo = sb("pT_hi", [P, TPC, P], F32R), sb("pT_lo", [P, TPC, P], F32R)
        css, cve, crs = sb("css", [P, TPC]), sb("cve", [P, TPC]), sb("crs", [P, TPC])
        kss, kve, krs = sb("kss", [P, TPC]), sb("kve", [P, TPC]), sb("krs", [P, TPC])
        qve, qrs = sb("qve", [P, TPC]), sb("qrs", [P, TPC])
        nmx, den, rden = sb("nmx", [P, TPC]), sb("den", [P, TPC]), sb("rden", [P, TPC])

        const_in, x_in, w_in, c_in = sem("const_in"), sem("x_in"), [sem("wq_in"), sem("wk_in")], sem("c_in")
        zero, ident_ok, off_ok, half_ok = sem("zero"), sem("ident_ok"), sem("off_ok"), sem("half_ok")
        wh_ok, wl_ok, wqk_ok = sem("w_hi_ok"), sem("w_lo_ok"), sem("wqk_ok")
        s_css, s_cve, s_crs, s_f = sem("css_ok"), sem("cve_ok"), sem("crs_ok"), sem("f_ok")
        s_fh, s_fl, s_cT, s_cTh, s_cTl = sem("f_hi_ok"), sem("f_lo_ok"), sem("cT_ps"), sem("cT_hi_ok"), sem("cT_lo_ok")
        s_q, s_qact, s_ql, s_qss, s_qve, s_qrs = (sem("q_ps"), sem("q_act"), sem("q_lo_ok"), sem("qss_ps"),
                                                  sem("qve_ok"), sem("qrs_ok"))
        s_k, s_kb, s_kss, s_kve, s_krs, s_kn = (sem("k_ps"), sem("kb_ok"), sem("kss_ok"), sem("kve_ok"),
                                                sem("krs_ok"), sem("kn_ok"))
        s_kT, s_kTh, s_kTl = sem("kT_ps"), sem("kT_hi_ok"), sem("kT_lo_ok")
        s_s, s_sS, s_nmx, s_p, s_rden = sem("s_ps"), sem("scores_ok"), sem("nmx_ok"), sem("prob_ok"), sem("rden_ok")
        s_pT, s_pTh, s_pTl, s_att, s_x = sem("pT_ps"), sem("pT_hi_ok"), sem("pT_lo_ok"), sem("att_ps"), sem("x_ok")
        block = ctx.enter_context(nc.Block())

        x_rows = a.x.rearrange("(c t p) d -> c p t d", c=NCH, p=P)
        c_rows = a.ctx.rearrange("(n p) d -> p n d", p=P)

        @block.sync
        def _(sp):
            sp.dma_start(m.x[:, 0:TPC * D].rearrange("p (t d) -> p t d", t=TPC), x_rows[0]).then_inc(x_in, 16)
            sp.dma_start(craw[:, :, :], c_rows[:, 0:TPC, :]).then_inc(c_in, 16)
            sp.dma_start(wraw[0][:, :, :], a.l0_wq).then_inc(w_in[0], 16)
            sp.dma_start(wraw[1][:, :, :], a.l0_wk).then_inc(w_in[1], 16)
            for n in range(1, NCH):
                sp.dma_start(m.x[:, n * TPC * D:(n + 1) * TPC * D].rearrange("p (t d) -> p t d", t=TPC),
                             x_rows[n]).then_inc(x_in, 16)
            with sp.Fori(1, NCH) as c:
                sp.wait_ge(s_f, c)
                sp.dma_start(craw[:, :, :], c_rows[:, bass.ts(c, TPC), :]).then_inc(c_in, 16)

        @block.gpsimd
        def _(pool):
            pool.memset(m.ident[:, :], 0.0).then_inc(zero, 1)
            pool.memset(m.neg_half[:, :], -0.5).then_inc(half_ok, 1)
            pool.wait_ge(zero, 1)
            pool.affine_select(out=m.ident[:, :], in_=m.ident[:, :], compare_op=ALU.not_equal, fill=1.0, base=0,
                               pattern=[[-1, P]], channel_multiplier=1).then_inc(ident_ok, 1)
            pool.memset(m.ones[:, :], 1.0).then_inc(half_ok, 1)
            pool.wait_ge(half_ok, 2)
            prep.pool_rstd(pool, 0)
            with pool.Fori(0, NCH) as c:
                pool.wait_ge(s_cve, c + 1)
                pool.tensor_tensor(crs[:, :], cve[:, :], m.neg_half[:, 0:TPC], ALU.pow).then_inc(s_crs, 1)
                pool.wait_ge(s_fh, c + 1)
                pool.tensor_tensor(f_lo[:, :, :], f[:, :, :], f_hi[:, :, :], ALU.subtract).then_inc(s_fl, 1)
                pool.wait_ge(s_qve, c + 1)
                pool.tensor_tensor(qrs[:, :], qve[:, :], m.neg_half[:, 0:TPC], ALU.pow).then_inc(s_qrs, 1)
                pool.wait_ge(s_kve, c + 1)
                pool.tensor_tensor(krs[:, :], kve[:, :], m.neg_half[:, 0:TPC], ALU.pow).then_inc(s_krs, 1)
                prep.pool_rstd(pool, c + 1)

        @block.scalar
        def _(act):
            act.dma_start(bq[:, :], a.l0_bq).then_inc(const_in, 16)
            act.dma_start(bk[:, :], a.l0_bk.partition_broadcast(P)).then_inc(const_in, 16)
            act.dma_start(fnw[:, :], a.l0_fnw.partition_broadcast(P)).then_inc(const_in, 16)
            act.dma_start(qnw[:, :], a.l0_qnw.partition_broadcast(P)).then_inc(const_in, 16)
            act.dma_start(wqk[:, :], a.l0_knw.partition_broadcast(P)).then_inc(const_in, 16)
            for n in range(2):
                act.wait_ge(w_in[n], 16)
                act.copy(w_hi[n][:, :, :], wraw[n][:, :, :]).then_inc(wh_ok, 1)
            act.wait_ge(const_in, 80)
            prep.act_hi(act, 0, bank[4:8])
            with act.Fori(0, NCH) as c:
                act.wait_ge(c_in, (c + 1) * 16)
                for t in range(TPC):
                    ins = act.activation(f[:, t, :], craw[:, t, :], ACT.Square, accum_out=css[:, t:t + 1])
                ins.then_inc(s_css, 1)
                act.wait_ge(s_f, c + 1)
                act.copy(f_hi[:, :, :], f[:, :, :]).then_inc(s_fh, 1)
                for k in range(KD):
                    act.wait_ge(s_cT, c * KD + k + 1)
                    act.copy(cT_hi[:, k, :], bank[k][:, :]).then_inc(s_cTh, 1)
                for j in range(KD):
                    act.wait_ge(s_q, c * KD + j + 1)
                    act.activation(qT_hi[:, j, :], bank[4 + j][:, :], ACT.Identity, bias=bq[:, j:j + 1])
                    act.activation(q2[:, j, :], bank[4 + j][:, :], ACT.Square, bias=bq[:, j:j + 1]).then_inc(s_qact, 1)
                act.wait_ge(s_fl, c + 1)
                for t in range(TPC):
                    act.wait_ge(s_kb, c * TPC + t + 1)
                    ins = act.activation(f[:, t, :], kb[:, t, :], ACT.Square, accum_out=kss[:, t:t + 1])
                ins.then_inc(s_kss, 1)
                for k in range(KD):
                    act.wait_ge(s_kT, c * KD + k + 1)
                    act.copy(kT_hi[:, k, :], bank[k][:, :]).then_inc(s_kTh, 1)
                act.wait_ge(s_nmx, c + 1)
                for t in range(TPC):
                    ins = act.activation(prob[:, t, :], sS[:, t, :], ACT.Exp, bias=nmx[:, t:t + 1],
                                         accum_out=den[:, t:t + 1])
                ins.then_inc(s_p, 1)
                act.wait_ge(s_pT, c + 1)
                act.copy(pT_hi[:, :, :], bank[6][:, :].rearrange("p (t s) -> p t s", t=TPC)).then_inc(s_pTh, 1)
                prep.act_hi(act, c + 1, bank[0:4])

        @block.vector
        def _(dve):
            dve.memset(off[:, :], OFF).then_inc(off_ok, 1)
            dve.wait_ge(off_ok, 1)
            dve.memset(off[0:S, 0:S], 0.0)
            dve.memset(off[S:P, S:P], 0.0).then_inc(off_ok, 1)
            dve.wait_ge(x_in, 16 * NCH)
            prep.dve_stats(dve, 0, 0)
            prep.dve_norm(dve, 0, 0)
            for n in range(2):
                dve.wait_ge(wh_ok, n + 1)
                dve.tensor_tensor(w_lo[n][:, :, :], wraw[n][:, :, :], w_hi[n][:, :, :], ALU.subtract).then_inc(wl_ok, 1)
            dve.wait_ge(const_in, 80)
            dve.tensor_tensor(wqk[:, :], wqk[:, :], qnw[:, :], ALU.mult).then_inc(wqk_ok, 1)
            dve.wait_ge(off_ok, 2)
            dve.wait_ge(wqk_ok, 1)
            prep.dve_lo(dve, 0, bank[4:8])
            with dve.Fori(0, NCH) as c:
                dve.wait_ge(s_css, c + 1)
                dve.tensor_scalar(cve[:, :], css[:, :], 1.0 / D, L0_EPS, ALU.mult, ALU.add).then_inc(s_cve, 1)
                dve.wait_ge(s_crs, c + 1)
                for t in range(TPC):
                    ins = dve.scalar_tensor_tensor(f[:, t, :], craw[:, t, :], crs[:, t:t + 1], fnw[:, :],
                                                   ALU.mult, ALU.mult)
                ins.then_inc(s_f, 1)
                for k in range(KD):
                    dve.wait_ge(s_cTh, c * KD + k + 1)
                    dve.tensor_tensor(cT_lo[:, k, :], bank[k][:, :], cT_hi[:, k, :], ALU.subtract).then_inc(s_cTl, 1)
                for j in range(KD):
                    dve.wait_ge(s_qact, c * KD + j + 1)
                    dve.scalar_tensor_tensor(qT_lo[:, j, :], bank[4 + j][:, :], bq[:, j:j + 1], qT_hi[:, j, :],
                                             ALU.add, ALU.subtract).then_inc(s_ql, 1)
                for t in range(TPC):
                    dve.wait_ge(s_k, c * TPC + t + 1)
                    dve.tensor_tensor(kb[:, t, :], bank[t][:, :], bk[:, :], ALU.add).then_inc(s_kb, 1)
                dve.wait_ge(s_qss, c + 1)
                dve.tensor_scalar(qve[:, :], bank[4][:, 0:TPC], D * L0_EPS, None, ALU.add).then_inc(s_qve, 1)
                dve.wait_ge(s_kss, c + 1)
                dve.tensor_scalar(kve[:, :], kss[:, :], 1.0 / D, L0_EPS, ALU.mult, ALU.add).then_inc(s_kve, 1)
                dve.wait_ge(s_krs, c + 1)
                for t in range(TPC):
                    ins = dve.scalar_tensor_tensor(kb[:, t, :], kb[:, t, :], krs[:, t:t + 1], wqk[:, :],
                                                   ALU.mult, ALU.mult)
                ins.then_inc(s_kn, 1)
                for k in range(KD):
                    dve.wait_ge(s_kTh, c * KD + k + 1)
                    dve.tensor_tensor(kT_lo[:, k, :], bank[k][:, :], kT_hi[:, k, :], ALU.subtract).then_inc(s_kTl, 1)
                dve.wait_ge(s_qrs, c + 1)
                dve.wait_ge(s_s, c + 1)
                for t in range(TPC):
                    ins = dve.scalar_tensor_tensor(sS[:, t, :], bank[5][:, t * P:(t + 1) * P], qrs[:, t:t + 1],
                                                   off[:, :], ALU.mult, ALU.add)
                ins.then_inc(s_sS, 1)
                dve.wait_ge(s_sS, c + 1)
                dve.tensor_reduce(nmx[:, :], sS[:, :, :], AX.X, ALU.max, negate=True).then_inc(s_nmx, 1)
                prep.dve_stats(dve, c + 1, (c + 1) % NCH)
                dve.wait_ge(s_p, c + 1)
                dve.reciprocal(rden[:, :], den[:, :]).then_inc(s_rden, 1)
                prep.dve_norm(dve, c + 1, (c + 1) % NCH)
                dve.wait_ge(s_pTh, c + 1)
                dve.tensor_tensor(pT_lo[:, :, :], bank[6][:, :].rearrange("p (t s) -> p t s", t=TPC), pT_hi[:, :, :],
                                  ALU.subtract).then_inc(s_pTl, 1)
                prep.dve_lo(dve, c + 1, bank[0:4])
                dve.wait_ge(s_rden, c + 1)
                for t in range(TPC):
                    dve.wait_ge(s_att, c * TPC + t + 1)
                    xt = m.x[:, bass.ts(c * TPC + t, D)]
                    dve.scalar_tensor_tensor(xt, bank[[4, 5, 7, 6][t]][:, :], rden[:, t:t + 1], xt,
                                             ALU.mult, ALU.add).then_inc(s_x, 1)

        @block.tensor
        def _(pe):
            pe.wait_ge(ident_ok, 1)
            pe.wait_ge(half_ok, 2)
            prep.pe_transpose(pe, 0, bank[4:8])
            prep.wait_ready(pe, 0)
            pe.wait_ge(wl_ok, 2)
            with pe.Fori(0, NCH) as c:
                pe.wait_ge(s_f, c + 1)
                for k in range(KD):
                    for t in range(TPC):
                        ins = pe.transpose(bank[k][:, t * P:(t + 1) * P], f[:, t, k * P:(k + 1) * P], m.ident[:, :])
                    ins.then_inc(s_cT, 1)
                for j in range(KD):
                    for k in range(KD):
                        cols = slice(j * P, (j + 1) * P)
                        ins = split_mm(pe, bank[4 + j][:, :], w_hi[0][:, k, cols], w_lo[0][:, k, cols],
                                       m.xT_hi[:, k, :], m.xT_lo[:, k, :], k == 0, k == KD - 1)
                    ins.then_inc(s_q, 1)
                pe.wait_ge(s_cTl, (c + 1) * KD)
                for t in range(TPC):
                    for k in range(KD):
                        rows = slice(t * P, (t + 1) * P)
                        ins = split_mm(pe, bank[t][:, :], cT_hi[:, k, rows], cT_lo[:, k, rows],
                                       w_hi[1][:, k, :], w_lo[1][:, k, :], k == 0, k == KD - 1)
                    ins.then_inc(s_k, 1)
                pe.wait_ge(s_ql, (c + 1) * KD)
                for t in range(TPC):
                    for j in range(KD):
                        ins = pe.matmul(bank[4][:, t:t + 1], q2[:, j, t * P:(t + 1) * P], m.ones[:, :],
                                        start=(j == 0), stop=(j == KD - 1))
                ins.then_inc(s_qss, 1)
                pe.wait_ge(s_kn, c + 1)
                for k in range(KD):
                    for t in range(TPC):
                        ins = pe.transpose(bank[k][:, t * P:(t + 1) * P], kb[:, t, k * P:(k + 1) * P], m.ident[:, :])
                    ins.then_inc(s_kT, 1)
                pe.wait_ge(s_kTl, (c + 1) * KD)
                for t in range(TPC):
                    rows = slice(t * P, (t + 1) * P)
                    for k in range(KD):
                        ins = split_mm(pe, bank[5][:, rows], qT_hi[:, k, rows], qT_lo[:, k, rows],
                                       kT_hi[:, k, rows], kT_lo[:, k, rows], k == 0, k == KD - 1)
                ins.then_inc(s_s, 1)
                pe.wait_ge(s_p, c + 1)
                for t in range(TPC):
                    ins = pe.transpose(bank[6][:, t * P:(t + 1) * P], prob[:, t, :], m.ident[:, :])
                ins.then_inc(s_pT, 1)
                pe.wait_ge(s_fl, c + 1)
                prep.pe_transpose(pe, c + 1, bank[0:4])
                pe.wait_ge(s_pTl, c + 1)
                for t in range(TPC):
                    b = bank[[4, 5, 7, 6][t]]
                    ins = split_mm(pe, b[:, :], pT_hi[:, t, :], pT_lo[:, t, :], f_hi[:, t, :], f_lo[:, t, :], True, True)
                    ins.then_inc(s_att, 1)
                prep.wait_ready(pe, c + 1)
                pe.wait_ge(s_x, (c + 1) * TPC)


def stage_sparse_ffn(nc, m, prep, a):
    p0 = NCH
    with ExitStack() as ctx:
        sb = lambda n, s, d=F32: ctx.enter_context(nc.sbuf_tensor("f0_" + n, s, d))
        sem = lambda n: ctx.enter_context(nc.semaphore("f0_" + n))
        bank = m.bank
        w1_hi, w1_lo = sb("w1_hi", [P, KD, INTER], F32R), sb("w1_lo", [P, KD, INTER], F32R)
        w2_hi, w2_lo = sb("w2_hi", [P, NI, D], F32R), sb("w2_lo", [P, NI, D], F32R)
        h = sb("h", [P, INTER])
        raw = [h[:, :], m.xln[:, :, :].rearrange("p t d -> p (t d)")[:, 0:INTER]]
        c1raw = sb("c1raw", [P, KD, RK3])
        c1_hi, c1_lo = sb("c1_hi", [P, KD, RK3], F32R), sb("c1_lo", [P, KD, RK3], F32R)
        c2st = sb("c2st", [RK3, INTER], F32R)
        low = sb("low", [RK3, CHUNK], F32R)
        desc = sb("desc", [P, SPARSE], BF16)
        desc_i = sb("desc_i", [P, SPARSE], I32)
        bmax = [sb(f"bmax{n}", [P, BPQ]) for n in range(2)]
        eq = [sb(f"eq{n}", [P, QC], BF16) for n in range(2)]
        rank = [sb(f"rank{n}", [P, QC], BF16) for n in range(2)]
        rmax = [sb(f"rmax{n}", [P, BPQ], BF16) for n in range(2)]
        hT_hi, hT_lo = sb("hT_hi", [P, NI, P], F32R), sb("hT_lo", [P, NI, P], F32R)

        raw_in, wh_ok, wl_ok = [sem("raw0_in"), sem("raw1_in")], sem("w_hi_ok"), sem("w_lo_ok")
        c1_zero, c1_in, c1h_ok, c1l_ok, c2_ok = sem("c1_zero"), sem("c1_in"), sem("c1_hi_ok"), sem("c1_lo_ok"), sem("c2_ok")
        iota_ok, desc_ok = sem("iota_ok"), sem("desc_ok")
        s_low, s_lowh, s_lowl = sem("low_ps"), sem("low_hi_ok"), sem("low_ok")
        s_i, s_h, s_max, s_eq, s_rank = sem("inter_ps"), sem("h_ps"), sem("bmax_ok"), sem("eq_ok"), sem("rank_ok")
        s_rmax, s_hot, s_hm = sem("rmax_ok"), sem("one_hot_ok"), sem("h_ok")
        s_hT, s_hTh, s_hTl, s_o, s_x = sem("hT_ps"), sem("hT_hi_ok"), sem("hT_lo_ok"), sem("out_ps"), sem("x_ok")
        block = ctx.enter_context(nc.Block())

        def piece(n):
            if n == 0:
                return c2st[:, :], None
            if n <= KD:
                return w1_hi[:, n - 1, :], w1_lo[:, n - 1, :]
            w = slice((n - 1 - KD) * INTER, (n - KD) * INTER)
            return (w2_hi[:, :, :].rearrange("p j d -> p (j d)")[:, w], w2_lo[:, :, :].rearrange("p j d -> p (j d)")[:, w])

        NP = 1 + 2 * KD
        TG = [slice(4 * g, min(4 * g + 4, NI)) for g in range(NQ)]

        @block.sync
        def _(sp):
            for n in range(3):
                if n == 0:
                    sp.wait_ge(c1_zero, 2)
                sp.dma_start(c1raw[:, :, 32 * n:32 * n + RANK], a.c1).then_inc(c1_in, 16)
                sp.dma_start(raw[0][32 * n:32 * n + RANK, :], a.c2).then_inc(raw_in[0], 16)
            for n in range(1, NP):
                if n >= 2:
                    sp.wait_ge(wl_ok, n - 1)
                src = a.w1[:, n - 1, :] if n <= KD else a.w2[:, (n - 1 - KD) * INTER:(n - KD) * INTER]
                sp.dma_start(raw[n % 2], src).then_inc(raw_in[n % 2], 16)

        @block.gpsimd
        def _(pool):
            pool.memset(c1raw[:, :, :], 0.0).then_inc(c1_zero, 1)
            pool.memset(raw[0][0:RK3, :], 0.0).then_inc(c1_zero, 1)
            pool.wait_ge(c1_zero, 2)
            pool.iota(desc_i[:, :], pattern=[[-1, SPARSE]], base=SPARSE, channel_multiplier=0).then_inc(iota_ok, 1)
            pool.wait_ge(iota_ok, 1)
            pool.tensor_copy(desc[:, :], desc_i[:, :]).then_inc(desc_ok, 1)
            pool.wait_ge(desc_ok, 1)
            with pool.Fori(0, NCH) as c:
                for t in range(TPC):
                    for q in range(NQ):
                        n = c * TPC * NQ + t * NQ + q
                        pool.wait_ge(s_eq, n + 1)
                        pool.tensor_tensor(rank[q % 2][:, :].rearrange("p (b s) -> p b s", s=SPARSE),
                                           eq[q % 2][:, :].rearrange("p (b s) -> p b s", s=SPARSE),
                                           desc[:, :].unsqueeze(1).broadcast_to([P, BPQ, SPARSE]),
                                           ALU.mult).then_inc(s_rank, 1)
                prep.pool_rstd(pool, p0 + c + 1)

        @block.scalar
        def _(act):
            act.wait_ge(c1_in, 48)
            act.copy(c1_hi[:, :, :], c1raw[:, :, :]).then_inc(c1h_ok, 1)
            for n in range(NP):
                act.wait_ge(raw_in[n % 2], 16 * (n // 2 + (3 if n % 2 == 0 else 1)))
                src = raw[0][0:RK3, :] if n == 0 else raw[n % 2]
                act.copy(piece(n)[0], src).then_inc(wh_ok, 1)
            with act.Fori(0, NCH) as c:
                act.wait_ge(s_low, c + 1)
                act.copy(low[:, :], bank[6][0:RK3, :]).then_inc(s_lowh, 1)
                for t in range(1, TPC + 1):
                    for g in range(NQ):
                        w = TG[g].stop - TG[g].start
                        act.wait_ge(s_hT, (c * TPC + t - 1) * NQ + g + 1)
                        act.copy(hT_hi[:, TG[g], :], bank[4 + g % 2][:, 0:w * P].rearrange("p (j s) -> p j s", s=P))\
                           .then_inc(s_hTh, 1)
                prep.act_hi(act, p0 + c + 1, bank[0:4])

        @block.vector
        def _(dve):
            dve.wait_ge(c1h_ok, 1)
            dve.tensor_tensor(c1_lo[:, :, :], c1raw[:, :, :], c1_hi[:, :, :], ALU.subtract).then_inc(c1l_ok, 1)
            for n in range(NP):
                dve.wait_ge(wh_ok, n + 1)
                hi, lo = piece(n)
                if n == 0:
                    dve.tensor_tensor(c2st[64:96, :], raw[0][64:96, :], c2st[64:96, :], ALU.subtract).then_inc(wl_ok, 1)
                else:
                    dve.tensor_tensor(lo, raw[n % 2], hi, ALU.subtract).then_inc(wl_ok, 1)

            def find_max(c, t, q):
                n = c * TPC * NQ + t * NQ + q
                inter = bank[q % 2][:, 0:QC].rearrange("p (b s) -> p b s", s=SPARSE)
                dve.wait_ge(s_i, n + 1)
                dve.tensor_reduce(bmax[q % 2][:, :], inter, AX.X, ALU.max).then_inc(s_max, 1)
                dve.wait_ge(s_max, n + 1)
                dve.tensor_tensor(eq[q % 2][:, :].rearrange("p (b s) -> p b s", s=SPARSE), inter,
                                  bmax[q % 2][:, :].unsqueeze(2).broadcast_to([P, BPQ, SPARSE]),
                                  ALU.is_equal).then_inc(s_eq, 1)

            def select(c, t, q):
                n = c * TPC * NQ + t * NQ + q
                rk = rank[q % 2][:, :].rearrange("p (b s) -> p b s", s=SPARSE)
                dve.wait_ge(s_rank, n + 1)
                dve.tensor_reduce(rmax[q % 2][:, :], rk, AX.X, ALU.max).then_inc(s_rmax, 1)
                dve.wait_ge(s_rmax, n + 1)
                dve.tensor_tensor(rank[q % 2][:, :].rearrange("p (b s) -> p b s", s=SPARSE), rk,
                                  rmax[q % 2][:, :].unsqueeze(2).broadcast_to([P, BPQ, SPARSE]),
                                  ALU.is_equal).then_inc(s_hot, 1)
                dve.wait_ge(s_hot, n + 1)
                dve.wait_ge(s_h, n + 1)
                dve.scalar_tensor_tensor(h[:, q * QC:(q + 1) * QC], bank[2 + q % 2][:, 0:QC], 0.0, rank[q % 2][:, :],
                                         ALU.max, ALU.mult).then_inc(s_hm, 1)

            def hidden_lo(c, t, g):
                w = TG[g].stop - TG[g].start
                dve.wait_ge(s_hTh, (c * TPC + t) * NQ + g + 1)
                dve.tensor_tensor(hT_lo[:, TG[g], :], bank[4 + g % 2][:, 0:w * P].rearrange("p (j s) -> p j s", s=P),
                                  hT_hi[:, TG[g], :], ALU.subtract).then_inc(s_hTl, 1)

            def add_out(c, t):
                dve.wait_ge(s_o, c * TPC + t + 1)
                xt = m.x[:, bass.ts(c * TPC + t, D)]
                dve.tensor_tensor(xt, bank[6 + t % 2][:, :], xt, ALU.add).then_inc(s_x, 1)

            with dve.Fori(0, NCH) as c:
                dve.wait_ge(s_lowh, c + 1)
                dve.tensor_tensor(low[32:64, :], bank[6][32:64, :], low[32:64, :], ALU.subtract).then_inc(s_lowl, 1)
                for t in range(TPC):
                    for q in range(NQ):
                        find_max(c, t, q)
                        if t >= 1:
                            hidden_lo(c, t - 1, q)
                        if q >= 1:
                            select(c, t, q - 1)
                    select(c, t, NQ - 1)
                    if t >= 1:
                        add_out(c, t - 1)
                for g in range(NQ):
                    hidden_lo(c, TPC - 1, g)
                prep.dve_stats(dve, p0 + c + 1, (c + 1) % NCH)
                prep.dve_norm(dve, p0 + c + 1, (c + 1) % NCH)
                add_out(c, TPC - 1)
                prep.dve_lo(dve, p0 + c + 1, bank[0:4])

        @block.tensor
        def _(pe):
            def hidden_T(c, t, g):
                pe.wait_ge(s_hm, (c * TPC + t + 1) * NQ)
                if g >= 2:
                    pe.wait_ge(s_hTl, (c * TPC + t) * NQ + g - 1)
                for n, j in enumerate(range(TG[g].start, TG[g].stop)):
                    ins = pe.transpose(bank[4 + g % 2][:, n * P:(n + 1) * P], h[:, j * P:(j + 1) * P], m.ident[:, :])
                ins.then_inc(s_hT, 1)

            def out_rows(c, t):
                pe.wait_ge(s_hTl, (c * TPC + t + 1) * NQ)
                if t >= 2:
                    pe.wait_ge(s_x, c * TPC + t - 1)
                for j in range(NI):
                    ins = split_mm(pe, bank[6 + t % 2][:, :], hT_hi[:, j, :], hT_lo[:, j, :], w2_hi[:, j, :], w2_lo[:, j, :],
                                   j == 0, j == NI - 1)
                ins.then_inc(s_o, 1)

            pe.wait_ge(c1l_ok, 1)
            pe.wait_ge(wl_ok, 1 + KD)
            with pe.Fori(0, NCH) as c:
                for k in range(KD):
                    ins = split_mm(pe, bank[6][0:RK3, :], c1_hi[:, k, :], c1_lo[:, k, :], m.xT_hi[:, k, :], m.xT_lo[:, k, :],
                                   k == 0, k == KD - 1)
                ins.then_inc(s_low, 1)
                pe.wait_ge(s_lowl, c + 1)
                for t in range(TPC):
                    rows = slice(t * P, (t + 1) * P)
                    for q in range(NQ):
                        cols = slice(q * QC, (q + 1) * QC)
                        if t >= 1:
                            hidden_T(c, t - 1, q)
                        if t >= 1 or q >= 2:
                            pe.wait_ge(s_eq, c * TPC * NQ + t * NQ + q - 1)
                        pe.matmul(bank[q % 2][:, 0:QC], low[:, rows], c2st[:, cols], start=True, stop=True).then_inc(s_i, 1)
                        if t >= 1 or q >= 2:
                            pe.wait_ge(s_hm, c * TPC * NQ + t * NQ + q - 1)
                        for k in range(KD):
                            ins = split_mm(pe, bank[2 + q % 2][:, 0:QC], m.xT_hi[:, k, rows], m.xT_lo[:, k, rows],
                                           w1_hi[:, k, cols], w1_lo[:, k, cols], k == 0, k == KD - 1)
                        ins.then_inc(s_h, 1)
                    if t == 1:
                        pe.wait_ge(wl_ok, NP)
                    if t >= 1:
                        out_rows(c, t - 1)
                for g in range(NQ):
                    hidden_T(c, TPC - 1, g)
                out_rows(c, TPC - 1)
                prep.pe_transpose(pe, p0 + c + 1, bank[0:4])
                prep.wait_ready(pe, p0 + c + 1)
                pe.wait_ge(s_x, (c + 1) * TPC)


def stage_l1_attention(nc, m, prep, a):
    p0 = 2 * NCH
    with ExitStack() as ctx:
        sb = lambda n, s, d=F32: ctx.enter_context(nc.sbuf_tensor("a1_" + n, s, d))
        sem = lambda n: ctx.enter_context(nc.semaphore("a1_" + n))
        bank = m.bank
        q_raw, kv_raw, o_raw = sb("q_raw", [P, KD, G * HD]), sb("kv_raw", [P, KD, 2 * HD]), sb("o_raw", [P, G, D])
        wq_hi, wq_lo = sb("wq_hi", [P, KD, G * HD], F32R), sb("wq_lo", [P, KD, G * HD], F32R)
        wkv_hi, wkv_lo = sb("wkv_hi", [P, KD, 2 * HD], F32R), sb("wkv_lo", [P, KD, 2 * HD], F32R)
        wo_hi, wo_lo = sb("wo_hi", [P, G, D], F32R), sb("wo_lo", [P, G, D], F32R)
        craw = sb("craw", [P, KD, CHUNK])
        cT_hi, cT_lo = sb("cT_hi", [P, KD, CHUNK], F32R), sb("cT_lo", [P, KD, CHUNK], F32R)
        qT_hi, qT_lo = sb("qT_hi", [P, G, CHUNK], F32R), sb("qT_lo", [P, G, CHUNK], F32R)
        q2 = sb("q2", [P, G, CHUNK])
        v_hi, v_lo = sb("v_hi", [P, TPC, HD], F32R), sb("v_lo", [P, TPC, HD], F32R)
        kn = sb("kn", [P, TPC, HD])
        kT_hi, kT_lo = sb("kT_hi", [P, CHUNK], F32R), sb("kT_lo", [P, CHUNK], F32R)
        prob = sb("prob", [P, TPC, G * P])
        pT_hi = [sb(f"pT_hi{n}", [P, G * P], F32R) for n in range(2)]
        pT_lo = [sb(f"pT_lo{n}", [P, G * P], F32R) for n in range(2)]
        oT_hi, oT_lo = sb("oT_hi", [P, TPC, G * P], F32R), sb("oT_lo", [P, TPC, G * P], F32R)
        mask, wqk, knw = sb("mask", [P, P]), sb("wqk", [P, 1]), sb("knw", [P, 1])
        kss, kve, krs = sb("kss", [P, TPC]), sb("kve", [P, TPC]), sb("krs", [P, TPC])
        qss, qve, qrs = sb("qss", [P, TPC * G]), sb("qve", [P, TPC * G]), sb("qrs", [P, TPC * G])
        nmx, den, rden = sb("nmx", [P, TPC * G]), sb("den", [P, TPC * G]), sb("rden", [P, TPC * G])

        q_in, kv_in, o_in, c_in, const_in = sem("wq_in"), sem("wkv_in"), sem("wo_in"), sem("ctx_in"), sem("const_in")
        mask_ok, wqk_ok = sem("mask_ok"), sem("wqk_ok")
        wqh_ok, wql_ok, wkvh_ok, wkvl_ok = sem("wq_hi_ok"), sem("wq_ok"), sem("wkv_hi_ok"), sem("wkv_ok")
        woh_ok, wol_ok, s_cTh, s_cTl = sem("wo_hi_ok"), sem("wo_ok"), sem("cT_hi_ok"), sem("cT_ok")
        s_kv, s_kvact, s_vl, s_kve, s_krs, s_kn = (sem("kv_ps"), sem("kv_act"), sem("v_ok"), sem("kve_ok"),
                                                   sem("krs_ok"), sem("kn_ok"))
        s_kT, s_kTh, s_kTl = sem("kT_ps"), sem("kT_hi_ok"), sem("kT_ok")
        s_q, s_qact, s_ql, s_qss, s_qve, s_qrs = (sem("q_ps"), sem("q_act"), sem("q_ok"), sem("qss_ps"),
                                                  sem("qve_ok"), sem("qrs_ok"))
        s_qsum = sem("qsum_ok")
        s_s, s_sS, s_nmx, s_e, s_rden, s_p = (sem("s_ps"), sem("scores_ok"), sem("nmx_ok"), sem("exp_ok"),
                                              sem("rden_ok"), sem("prob_ok"))
        s_pT, s_pTh, s_pTl = sem("pT_ps"), sem("pT_hi_ok"), sem("pT_ok")
        s_pv, s_oTh, s_oTl, s_o, s_x = sem("pv_ps"), sem("oT_hi_ok"), sem("oT_ok"), sem("o_ps"), sem("x_ok")
        block = ctx.enter_context(nc.Block())
        s_banks = [bank[6], bank[7], bank[4], bank[5]]
        q_banks = [bank[2], bank[3], bank[0], bank[1]]
        sq_banks = [bank[0], bank[1], bank[6], bank[7]]
        kv_banks, kT_bank = [bank[2], bank[3]], bank[2]
        pT_banks, pv_banks, o_banks = [bank[6], bank[7]], [bank[4], bank[5]], [bank[0], bank[1]]
        prep_banks = bank[0:4]
        NIT = NCH * KVH


        @block.sync
        def _(sp):
            def load_qkv(n):
                sp.dma_start(q_raw[:, :, :], a.l1_wq[n % KVH]).then_inc(q_in, 16)
                sp.dma_start(kv_raw[:, :, :], a.l1_wkv[n % KVH]).then_inc(kv_in, 16)

            load_qkv(0)
            sp.dma_start(o_raw[:, :, :], a.l1_wo[0]).then_inc(o_in, 16)
            sp.wait_ge(wql_ok, 1)
            sp.wait_ge(wkvl_ok, 1)
            load_qkv(1)
            with sp.Fori(1, NIT) as i:
                sp.wait_ge(wql_ok, i + 1)
                sp.wait_ge(wkvl_ok, i + 1)
                load_qkv(i + 1)
                sp.wait_ge(wol_ok, i)
                sp.dma_start(o_raw[:, :, :], a.l1_wo[i % KVH]).then_inc(o_in, 16)

        @block.gpsimd
        def _(pool):
            def split_kv(n):
                pool.wait_ge(wkvh_ok, n + 1)
                pool.tensor_tensor(wkv_lo[:, :, :], kv_raw[:, :, :], wkv_hi[:, :, :], ALU.subtract).then_inc(wkvl_ok, 1)

            def split_q(n):
                pool.wait_ge(wqh_ok, n + 1)
                pool.tensor_tensor(wq_lo[:, :, :], q_raw[:, :, :], wq_hi[:, :, :], ALU.subtract).then_inc(wql_ok, 1)

            def split_o(n):
                pool.wait_ge(woh_ok, n + 1)
                pool.tensor_tensor(wo_lo[:, :, :], o_raw[:, :, :], wo_hi[:, :, :], ALU.subtract).then_inc(wol_ok, 1)

            def split_ctx(c):
                pool.wait_ge(s_cTh, c + 1)
                pool.tensor_tensor(cT_lo[:, :, :], craw[:, :, :], cT_hi[:, :, :], ALU.subtract).then_inc(s_cTl, 1)

            def roots(n):
                pool.wait_ge(s_kve, n + 1)
                pool.tensor_tensor(krs[:, :], kve[:, :], m.neg_half[:, 0:TPC], ALU.pow).then_inc(s_krs, 1)
                pool.wait_ge(s_qve, n + 1)
                pool.tensor_tensor(qrs[:, :], qve[:, :], m.neg_half[:, :], ALU.pow).then_inc(s_qrs, 1)

            def body(c, i, switch=False, more=True):
                if switch:
                    prep.pool_rstd(pool, p0 + c + 1)
                    if more:
                        split_ctx(c + 1)
                for t in range(TPC):
                    pool.wait_ge(s_rden, i * TPC + t + 1)
                    pt = prob[:, t, :].rearrange("p (j s) -> p j s", j=G)
                    pool.tensor_tensor(pt, pt, rden[:, t * G:(t + 1) * G].unsqueeze(2).broadcast_to([P, G, P]),
                                       ALU.mult).then_inc(s_p, 1)
                split_o(i)
                if more:
                    split_q(i + 2)
                    split_kv(i + 2)
                    roots(i + 1)

            pool.memset(mask[:, :], OFF).then_inc(mask_ok, 1)
            split_q(0)
            split_ctx(0)
            split_kv(0)
            split_q(1)
            split_kv(1)
            roots(0)
            with pool.Fori(0, NCH - 1) as c:
                with pool.Fori(0, KVH - 1) as g:
                    body(c, c * KVH + g)
                body(c, c * KVH + KVH - 1, switch=True)
            with pool.Fori(0, KVH - 1) as g:
                body(NCH - 1, g + (NIT - KVH))
            body(NCH - 1, NIT - 1, switch=True, more=False)

        @block.scalar
        def _(act):
            def split_kv(n):
                act.wait_ge(kv_in, (n + 1) * 16)
                act.copy(wkv_hi[:, :, :], kv_raw[:, :, :]).then_inc(wkvh_ok, 1)

            def split_q(n):
                act.wait_ge(q_in, (n + 1) * 16)
                act.copy(wq_hi[:, :, :], q_raw[:, :, :]).then_inc(wqh_ok, 1)

            def split_o(n):
                act.wait_ge(o_in, (n + 1) * 16)
                act.wait_ge(s_x, n * TPC + 1)
                act.copy(wo_hi[:, :, :], o_raw[:, :, :]).then_inc(woh_ok, 1)

            def split_ctx(c):
                act.wait_ge(c_in, (c + 1) * 16)
                act.copy(cT_hi[:, :, :], craw[:, :, :]).then_inc(s_cTh, 1)

            def query(n, j):
                act.wait_ge(s_q, n * G + j + 1)
                act.copy(qT_hi[:, j, :], q_banks[j][:, :])
                act.activation(q2[:, j, :], q_banks[j][:, :], ACT.Square).then_inc(s_qact, 1)

            def keys_values(n):
                for b in range(2):
                    act.wait_ge(s_kv, n * 2 + b + 1)
                    kv = kv_banks[b][:, :].rearrange("p (t w) -> p t w", t=2)
                    act.copy(v_hi[:, 2 * b:2 * b + 2, :], kv[:, :, HD:])
                    for u in range(2):
                        ins = act.activation(kn[:, 2 * b + u, :], kv[:, u, 0:HD], ACT.Square,
                                             accum_out=kss[:, 2 * b + u:2 * b + u + 1])
                    ins.then_inc(s_kvact, 1)

            def keys_T(n):
                act.wait_ge(s_kT, n + 1)
                act.activation(kT_hi[:, :], kT_bank[:, :], ACT.Copy, scale=wqk[:, :]).then_inc(s_kTh, 1)

            def exps(i, t):
                act.wait_ge(s_nmx, i * TPC + t + 1)
                for j in range(G):
                    pt = prob[:, t, j * P:(j + 1) * P]
                    ins = act.activation(pt, pt, ACT.Exp, bias=nmx[:, t * G + j:t * G + j + 1],
                                         accum_out=den[:, t * G + j:t * G + j + 1])
                ins.then_inc(s_e, 1)

            def probs_T(i, t):
                act.wait_ge(s_pT, i * TPC + t + 1)
                act.copy(pT_hi[t % 2][:, :], pT_banks[t % 2][:, :]).then_inc(s_pTh, 1)

            def outputs(i, t):
                act.wait_ge(s_pv, i * TPC + t + 1)
                act.copy(oT_hi[:, t, :], pv_banks[t % 2][:, :]).then_inc(s_oTh, 1)

            def body(c, i, switch=False, more=True):
                if switch and more:
                    split_ctx(c + 1)
                split_o(i)
                if switch:
                    prep.act_hi(act, p0 + c + 1, prep_banks)
                exps(i, 0)
                exps(i, 1)
                if more:
                    query(i + 1, 0)
                exps(i, 2)
                if more:
                    query(i + 1, 1)
                exps(i, 3)
                if more:
                    query(i + 1, 2)
                probs_T(i, 0)
                probs_T(i, 1)
                if more:
                    query(i + 1, 3)
                    split_q(i + 2)
                outputs(i, 0)
                outputs(i, 1)
                probs_T(i, 2)
                probs_T(i, 3)
                if more:
                    act.wait_ge(s_kv, (i + 2) * 2)
                    split_kv(i + 2)
                outputs(i, 2)
                outputs(i, 3)
                if more:
                    keys_values(i + 1)
                    keys_T(i + 1)

            def load_ctx(c):
                act.dma_start(craw[:, :, :], a.ctxT[c]).then_inc(c_in, 16)

            load_ctx(0)
            act.dma_start(wqk[:, :], a.l1_qnw).then_inc(const_in, 16)
            act.dma_start(knw[:, :], a.l1_knw).then_inc(const_in, 16)
            act.wait_ge(mask_ok, 1)
            act.dma_start(mask[0:S, 0:S], a.mask).then_inc(const_in, 16)
            act.dma_start(mask[S:P, S:P], a.mask).then_inc(const_in, 16)
            split_q(0)
            split_ctx(0)
            split_kv(0)
            for j in range(G):
                query(0, j)
            split_q(1)
            act.wait_ge(s_kv, 2)
            split_kv(1)
            keys_values(0)
            act.wait_ge(wqk_ok, 1)
            keys_T(0)
            with act.Fori(0, NCH - 1) as c:
                act.wait_ge(s_cTl, c + 1)
                load_ctx(c + 1)
                with act.Fori(0, KVH - 1) as g:
                    body(c, c * KVH + g)
                body(c, c * KVH + KVH - 1, switch=True)
            with act.Fori(0, KVH - 1) as g:
                body(NCH - 1, g + (NIT - KVH))
            body(NCH - 1, NIT - 1, switch=True, more=False)

        @block.vector
        def _(dve):
            def add_out(c, i, t):
                dve.wait_ge(s_o, i * TPC + t + 1)
                xt = m.x[:, bass.ts(c * TPC + t, D)]
                dve.tensor_tensor(xt, o_banks[t % 2][:, :], xt, ALU.add).then_inc(s_x, 1)

            def query(n, j):
                dve.wait_ge(s_qact, n * G + j + 1)
                dve.tensor_tensor(qT_lo[:, j, :], q_banks[j][:, :], qT_hi[:, j, :], ALU.subtract).then_inc(s_ql, 1)

            def query_sums(n):
                for t in range(TPC):
                    dve.wait_ge(s_qss, n * TPC + t + 1)
                    ins = dve.tensor_reduce(qss[:, t * G:(t + 1) * G],
                                            sq_banks[t][:, :].rearrange("p (j f) -> p j f", j=G), AX.X, ALU.add)
                ins.then_inc(s_qsum, 1)
                dve.wait_ge(s_qsum, n + 1)
                dve.tensor_scalar(qve[:, :], qss[:, :], HD * L1_EPS, None, ALU.add).then_inc(s_qve, 1)

            def values(n):
                for b in range(2):
                    dve.wait_ge(s_kvact, n * 2 + b + 1)
                    kv = kv_banks[b][:, :].rearrange("p (t w) -> p t w", t=2)
                    dve.tensor_tensor(v_lo[:, 2 * b:2 * b + 2, :], kv[:, :, HD:], v_hi[:, 2 * b:2 * b + 2, :],
                                      ALU.subtract).then_inc(s_vl, 1)
                dve.tensor_scalar(kve[:, :], kss[:, :], 1.0 / HD, L1_EPS, ALU.mult, ALU.add).then_inc(s_kve, 1)

            def keys(n):
                dve.wait_ge(s_krs, n + 1)
                for t in range(TPC):
                    ins = dve.tensor_scalar(kn[:, t, :], kv_banks[t // 2][:, (t % 2) * 2 * HD:(t % 2) * 2 * HD + HD],
                                            krs[:, t:t + 1], None, ALU.mult)
                ins.then_inc(s_kn, 1)

            def keys_T(n):
                dve.wait_ge(s_kTh, n + 1)
                dve.scalar_tensor_tensor(kT_lo[:, :], kT_bank[:, :], wqk[:, :], kT_hi[:, :],
                                         ALU.mult, ALU.subtract).then_inc(s_kTl, 1)

            def scores(i, t):
                dve.wait_ge(s_s, i * TPC + t + 1)
                for j in range(G):
                    cols = slice(j * P, (j + 1) * P)
                    ins = dve.scalar_tensor_tensor(prob[:, t, cols], s_banks[t][:, cols],
                                                   qrs[:, t * G + j:t * G + j + 1], mask[:, :], ALU.mult, ALU.add)
                ins.then_inc(s_sS, 1)
                dve.wait_ge(s_sS, i * TPC + t + 1)
                dve.tensor_reduce(nmx[:, t * G:(t + 1) * G], prob[:, t, :].rearrange("p (j s) -> p j s", j=G),
                                  AX.X, ALU.max, negate=True).then_inc(s_nmx, 1)

            def denominators(i, t):
                dve.wait_ge(s_e, i * TPC + t + 1)
                dve.reciprocal(rden[:, t * G:(t + 1) * G], den[:, t * G:(t + 1) * G]).then_inc(s_rden, 1)

            def probs_T(i, t):
                dve.wait_ge(s_pTh, i * TPC + t + 1)
                dve.tensor_tensor(pT_lo[t % 2][:, :], pT_banks[t % 2][:, :], pT_hi[t % 2][:, :],
                                  ALU.subtract).then_inc(s_pTl, 1)

            def outputs(i, t):
                dve.wait_ge(s_oTh, i * TPC + t + 1)
                dve.tensor_tensor(oT_lo[:, t, :], pv_banks[t % 2][:, :], oT_hi[:, t, :],
                                  ALU.subtract).then_inc(s_oTl, 1)

            def body(c, i, switch=False, more=True):
                if switch:
                    prep.dve_stats(dve, p0 + c + 1, (c + 1) % NCH)
                    prep.dve_norm(dve, p0 + c + 1, (c + 1) % NCH)
                dve.wait_ge(s_qrs, i + 1)
                scores(i, 0)
                if switch:
                    prep.dve_lo(dve, p0 + c + 1, prep_banks)
                scores(i, 1)
                scores(i, 2)
                denominators(i, 0)
                scores(i, 3)
                denominators(i, 1)
                if more:
                    query(i + 1, 0)
                denominators(i, 2)
                if more:
                    query(i + 1, 1)
                denominators(i, 3)
                if more:
                    query(i + 1, 2)
                probs_T(i, 0)
                probs_T(i, 1)
                if more:
                    query(i + 1, 3)
                outputs(i, 0)
                outputs(i, 1)
                probs_T(i, 2)
                probs_T(i, 3)
                if more:
                    query_sums(i + 1)
                outputs(i, 2)
                outputs(i, 3)
                if more:
                    values(i + 1)
                add_out(c, i, 0)
                if more:
                    keys(i + 1)
                add_out(c, i, 1)
                if more:
                    keys_T(i + 1)
                add_out(c, i, 2)
                add_out(c, i, 3)

            dve.memset(nmx[:, :], 0.0).then_inc(s_x, 1)
            dve.wait_ge(const_in, 64)
            dve.tensor_tensor(wqk[:, :], wqk[:, :], knw[:, :], ALU.mult).then_inc(wqk_ok, 1)
            dve.wait_ge(wqk_ok, 1)
            for j in range(G):
                query(0, j)
            query_sums(0)
            values(0)
            keys(0)
            keys_T(0)
            with dve.Fori(0, NCH - 1) as c:
                with dve.Fori(0, KVH - 1) as g:
                    body(c, c * KVH + g)
                body(c, c * KVH + KVH - 1, switch=True)
            with dve.Fori(0, KVH - 1) as g:
                body(NCH - 1, g + (NIT - KVH))
            body(NCH - 1, NIT - 1, switch=True, more=False)

        @block.tensor
        def _(pe):
            def query(n, j, first=False):
                if j == 0:
                    pe.wait_ge(wql_ok, n + 1)
                if j == 2 and not first:
                    pe.wait_ge(s_x, (n - 1) * TPC + 1)
                cols = slice(j * HD, (j + 1) * HD)
                for k in range(KD):
                    ins = split_mm(pe, q_banks[j][:, :], wq_hi[:, k, cols], wq_lo[:, k, cols],
                                   m.xT_hi[:, k, :], m.xT_lo[:, k, :], k == 0, k == KD - 1)
                ins.then_inc(s_q, 1)

            def keys_values(n):
                pe.wait_ge(wkvl_ok, n + 1)
                pe.wait_ge(s_ql, n * G + 2)
                for t in range(TPC):
                    rows = slice(t * P, (t + 1) * P)
                    out = kv_banks[t // 2][:, (t % 2) * 2 * HD:(t % 2 + 1) * 2 * HD]
                    for k in range(KD):
                        ins = split_mm(pe, out, cT_hi[:, k, rows], cT_lo[:, k, rows], wkv_hi[:, k, :], wkv_lo[:, k, :],
                                       k == 0, k == KD - 1)
                    if t % 2:
                        ins.then_inc(s_kv, 1)

            def query_squares_T(n, first=False):
                pe.wait_ge(s_ql, (n + 1) * G)
                if not first:
                    pe.wait_ge(s_pTl, n * TPC)
                for t in range(TPC):
                    for j in range(G):
                        ins = pe.transpose(sq_banks[t][:, j * P:(j + 1) * P], q2[:, j, t * P:(t + 1) * P], m.ident[:, :])
                    ins.then_inc(s_qss, 1)

            def keys_T(n):
                pe.wait_ge(s_kn, n + 1)
                for t in range(TPC):
                    ins = pe.transpose(kT_bank[:, t * P:(t + 1) * P], kn[:, t, :], m.ident[:, :])
                ins.then_inc(s_kT, 1)

            def scores(i):
                pe.wait_ge(s_kTl, i + 1)
                pe.wait_ge(s_ql, (i + 1) * G)
                pe.wait_ge(s_qve, i + 1)
                for t in range(TPC):
                    rows = slice(t * P, (t + 1) * P)
                    for j in range(G):
                        ins = split_mm(pe, s_banks[t][:, j * P:(j + 1) * P], qT_hi[:, j, rows], qT_lo[:, j, rows],
                                       kT_hi[:, rows], kT_lo[:, rows], True, True)
                    ins.then_inc(s_s, 1)

            def probs_T(i, t):
                pe.wait_ge(s_p, i * TPC + t + 1)
                if t >= 2:
                    pe.wait_ge(s_pTl, i * TPC + t - 1)
                else:
                    pe.wait_ge(s_sS, i * TPC + t + 1)
                for j in range(G):
                    cols = slice(j * P, (j + 1) * P)
                    ins = pe.transpose(pT_banks[t % 2][:, cols], prob[:, t, cols], m.ident[:, :])
                ins.then_inc(s_pT, 1)

            def attend(i, t):
                pe.wait_ge(s_pTl, i * TPC + t + 1)
                if t == 0:
                    pe.wait_ge(s_vl, (i + 1) * 2)
                if t >= 2:
                    pe.wait_ge(s_oTl, i * TPC + t - 1)
                else:
                    pe.wait_ge(s_sS, i * TPC + t + 3)
                split_mm(pe, pv_banks[t % 2][:, :], v_hi[:, t, :], v_lo[:, t, :], pT_hi[t % 2][:, :],
                         pT_lo[t % 2][:, :], True, True).then_inc(s_pv, 1)

            def out_rows(i, t, last):
                if t == 0:
                    pe.wait_ge(wol_ok, i + 1)
                    if not last:
                        pe.wait_ge(s_qve, i + 2)
                pe.wait_ge(s_oTl, i * TPC + t + 1)
                if t >= 2:
                    pe.wait_ge(s_x, i * TPC + t)
                for j in range(G):
                    cols = slice(j * P, (j + 1) * P)
                    ins = split_mm(pe, o_banks[t % 2][:, :], oT_hi[:, t, cols], oT_lo[:, t, cols],
                                   wo_hi[:, j, :], wo_lo[:, j, :], j == 0, j == G - 1)
                ins.then_inc(s_o, 1)

            def body(c, i, switch=False, more=True):
                scores(i)
                if switch:
                    pe.wait_ge(s_x, i * TPC + 1)
                    prep.pe_transpose(pe, p0 + c + 1, prep_banks)
                    prep.wait_ready(pe, p0 + c + 1)
                if more:
                    query(i + 1, 0)
                    query(i + 1, 1)
                    query(i + 1, 2)
                probs_T(i, 0)
                probs_T(i, 1)
                if more:
                    query(i + 1, 3)
                attend(i, 0)
                attend(i, 1)
                probs_T(i, 2)
                probs_T(i, 3)
                if more:
                    if switch:
                        pe.wait_ge(s_cTl, c + 2)
                    keys_values(i + 1)
                    query_squares_T(i + 1)
                attend(i, 2)
                attend(i, 3)
                out_rows(i, 0, not more)
                out_rows(i, 1, not more)
                if more:
                    keys_T(i + 1)
                out_rows(i, 2, not more)
                out_rows(i, 3, not more)

            for j in range(G):
                query(0, j, first=True)
            pe.wait_ge(s_cTl, 1)
            keys_values(0)
            query_squares_T(0, first=True)
            keys_T(0)
            with pe.Fori(0, NCH - 1) as c:
                with pe.Fori(0, KVH - 1) as g:
                    body(c, c * KVH + g)
                body(c, c * KVH + KVH - 1, switch=True)
            with pe.Fori(0, KVH - 1) as g:
                body(NCH - 1, g + (NIT - KVH))
            body(NCH - 1, NIT - 1, switch=True, more=False)


def stage_gated_ffn(nc, m, prep, a):
    p0 = 3 * NCH
    with ExitStack() as ctx:
        sb = lambda n, s, d=F32: ctx.enter_context(nc.sbuf_tensor("f1_" + n, s, d))
        sem = lambda n: ctx.enter_context(nc.semaphore("f1_" + n))
        bank = m.bank
        w_raw, w_hi, w_lo = sb("w_raw", [P, KD, D]), sb("w_hi", [P, KD, D], F32R), sb("w_lo", [P, KD, D], F32R)
        c_raw, c_hi, c_lo = sb("c_raw", [P, KD, NCL]), sb("c_hi", [P, KD, NCL], F32R), sb("c_lo", [P, KD, NCL], F32R)
        bias = sb("bias", [P, D])
        dense = sb("dense", [P, NT * D])
        lg, ex, hit = sb("logits", [P, TPC, NCL]), sb("ex", [P, TPC, NCL]), sb("hit", [P, TPC, NCL])
        hit_any = sb("hit_any", [P, NCL])
        nmx, nmx10, den, rden, row_sel = (sb("nmx", [P, TPC]), sb("nmx10", [P, TPC]), sb("den", [P, TPC]),
                                          sb("rden", [P, TPC]), sb("row_sel", [P, TPC]))
        assign_i, cluster_id = sb("assign_i", [NCL, D], I32), sb("cluster_id", [NCL, 1], I32)
        assign_f, cluster_f = sb("assign_f", [NCL, D]), sb("cluster_f", [NCL, 1])
        member = sb("member", [NCL, D], BF16)
        cl_sel = sb("cl_sel", [NCL, P], BF16)
        ones_cl = sb("ones_cl", [NCL, P])
        col_sel = sb("col_sel", [P, D])

        w_in, c_in, const_in, out_in = sem("w_in"), sem("cent_in"), sem("const_in"), sem("out_written")
        wh_ok, wl_ok, member_ok = sem("w_hi_ok"), sem("w_ok"), sem("member_ok")
        id_ok, idf_ok, ones_ok, any_ok = sem("id_ok"), sem("idf_ok"), sem("ones_ok"), sem("any_ok")
        s_l, s_nmx, s_nmx10, s_e, s_rden, s_hit, s_any, s_sel = (
            sem("logits_ps"), sem("nmx_ok"), sem("nmx10_ok"), sem("exp_ok"), sem("rden_ok"), sem("hit_ok"),
            sem("hit_any_ok"), sem("row_sel_ok"))
        s_d, s_db, s_dense, s_cnt, s_cl, s_col, s_colsel = (sem("dense_ps"), sem("dense_b_ok"), sem("dense_ok"),
                                                            sem("count_ps"), sem("cl_sel_ok"), sem("col_ps"), sem("col_sel_ok"))
        s_gate, s_gate_p, s_out, s_out_p = sem("gated"), sem("gated_pool"), sem("out_ok"), sem("out_pool_ok")
        block = ctx.enter_context(nc.Block())
        out_rows = a.out.rearrange("(n p) d -> n p d", p=P)
        POOL_TILES = 5
        DVE_TILES = NT - POOL_TILES

        @block.sync
        def _(sp):
            sp.dma_start(c_raw[:, :, :], a.cent).then_inc(c_in, 16)
            sp.dma_start(w_raw[:, :, :], a.l1_w).then_inc(w_in, 16)
            sp.dma_start(assign_i[:, :], a.assign.partition_broadcast(NCL)).then_inc(const_in, 16)
            sp.dma_start(bias[:, :], a.l1_b.partition_broadcast(P)).then_inc(const_in, 16)
            with sp.Fori(0, DVE_TILES) as n:
                sp.wait_ge(s_out, n + 1)
                sp.dma_start(out_rows[n], m.x[:, bass.ts(n, D)]).then_inc(out_in, 16)
            sp.wait_ge(out_in, 16 * NT)

        @block.gpsimd
        def _(pool):
            pool.iota(cluster_id[:, :], pattern=[[0, 1]], base=0, channel_multiplier=1).then_inc(id_ok, 1)
            pool.wait_ge(id_ok, 1)
            pool.memset(hit_any[:, :], 0.0).then_inc(any_ok, 1)
            pool.memset(ones_cl[:, :], 1.0).then_inc(ones_ok, 1)
            pool.wait_ge(ones_ok, 1)
            for p in range(1, NCH):
                prep.pool_rstd(pool, p0 + p)
            pool.wait_ge(s_colsel, 1)
            pool.wait_ge(s_dense, NT)
            with pool.Fori(0, POOL_TILES) as n:
                dn, xt = dense[:, bass.ts(n + DVE_TILES, D)], m.x[:, bass.ts(n + DVE_TILES, D)]
                pool.tensor_tensor(dn, dn, col_sel[:, :], ALU.mult).then_inc(s_gate_p, 1)
                pool.wait_ge(s_gate_p, n + 1)
                pool.tensor_tensor(xt, xt, dn, ALU.add).then_inc(s_out_p, 1)

        @block.scalar
        def _(act):
            act.wait_ge(c_in, 16)
            act.copy(c_hi[:, :, :], c_raw[:, :, :]).then_inc(wh_ok, 1)
            act.wait_ge(w_in, 16)
            act.copy(w_hi[:, :, :], w_raw[:, :, :]).then_inc(wh_ok, 1)

            def chunk(c, last):
                act.wait_ge(s_nmx10, c + 1)
                for t in range(TPC):
                    ins = act.activation(ex[:, t, :], lg[:, t, :], ACT.Exp, bias=nmx10[:, t:t + 1], accum_out=den[:, t:t + 1])
                ins.then_inc(s_e, 1)
                if not last:
                    prep.act_hi(act, p0 + c + 1, bank[0:4])

            with act.Fori(0, NCH - 1) as c:
                chunk(c, False)
            chunk(NCH - 1, True)
            with act.Fori(0, POOL_TILES) as n:
                act.wait_ge(s_out_p, n + 1)
                act.dma_start(out_rows[n + DVE_TILES], m.x[:, bass.ts(n + DVE_TILES, D)]).then_inc(out_in, 16)

        @block.vector
        def _(dve):
            dve.wait_ge(wh_ok, 1)
            dve.tensor_tensor(c_lo[:, :, :], c_raw[:, :, :], c_hi[:, :, :], ALU.subtract).then_inc(wl_ok, 1)
            dve.wait_ge(wh_ok, 2)
            dve.tensor_tensor(w_lo[:, :, :], w_raw[:, :, :], w_hi[:, :, :], ALU.subtract).then_inc(wl_ok, 1)
            dve.wait_ge(id_ok, 1)
            dve.wait_ge(const_in, 32)
            dve.tensor_copy(cluster_f[:, :], cluster_id[:, :])
            dve.tensor_copy(assign_f[:, :], assign_i[:, :]).then_inc(idf_ok, 1)
            dve.wait_ge(idf_ok, 1)
            dve.tensor_scalar(member[:, :], assign_f[:, :], cluster_f[:, :], None, ALU.is_equal).then_inc(member_ok, 1)
            dve.wait_ge(any_ok, 1)

            def chunk(c, last):
                dve.wait_ge(s_l, c + 1)
                lps = bank[4][:, 0:TPC * NCL].rearrange("p (t n) -> p t n", t=TPC)
                dve.tensor_scalar(lg[:, :, :], lps, 10.0, None, ALU.mult).then_inc(s_nmx, 1)
                dve.wait_ge(s_nmx, c + 1)
                dve.tensor_reduce(nmx10[:, :], lg[:, :, :], AX.X, ALU.max, negate=True).then_inc(s_nmx10, 1)
                if not last:
                    prep.dve_stats(dve, p0 + c + 1, c + 1)
                dve.wait_ge(s_e, c + 1)
                dve.reciprocal(rden[:, :], den[:, :]).then_inc(s_rden, 1)
                dve.wait_ge(s_rden, c + 1)
                for t in range(TPC):
                    ins = dve.tensor_scalar(hit[:, t, :], ex[:, t, :], rden[:, t:t + 1], 0.01, ALU.mult, ALU.is_gt)
                ins.then_inc(s_hit, 1)
                dve.wait_ge(s_hit, c + 1)
                dve.tensor_reduce(row_sel[:, :], hit[:, :, :], AX.X, ALU.max).then_inc(s_sel, 1)
                for t in range(TPC):
                    dve.tensor_tensor(hit_any[:, :], hit_any[:, :], hit[:, t, :], ALU.max).then_inc(s_any, 1)
                    dve.wait_ge(s_any, c * TPC + t + 1)
                if not last:
                    prep.dve_norm(dve, p0 + c + 1, c + 1)
                dve.wait_ge(s_sel, c + 1)
                for t in range(TPC):
                    dve.wait_ge(s_d, c * TPC + t + 1)
                    dn = dense[:, bass.ts(c * TPC + t, D)]
                    dve.tensor_tensor(dn, bank[5 + t % 2][:, :], bias[:, :], ALU.add).then_inc(s_db, 1)
                    dve.wait_ge(s_db, c * TPC + t + 1)
                    dve.tensor_scalar(dn, dn, row_sel[:, t:t + 1], None, ALU.mult).then_inc(s_dense, 1)
                if not last:
                    prep.dve_lo(dve, p0 + c + 1, bank[0:4])

            with dve.Fori(0, NCH - 1) as c:
                chunk(c, False)
            chunk(NCH - 1, True)
            dve.wait_ge(s_cnt, 1)
            dve.wait_ge(ones_ok, 1)
            dve.tensor_scalar(cl_sel[:, :], ones_cl[:, :], bank[7][0:NCL, 0:1], None, ALU.is_le).then_inc(s_cl, 1)
            dve.wait_ge(s_col, 1)
            dve.tensor_copy(col_sel[:, :], bank[0][:, :]).then_inc(s_colsel, 1)
            dve.wait_ge(s_colsel, 1)
            dve.wait_ge(s_dense, NT)
            with dve.Fori(0, DVE_TILES) as n:
                dn, xt = dense[:, bass.ts(n, D)], m.x[:, bass.ts(n, D)]
                dve.tensor_tensor(dn, dn, col_sel[:, :], ALU.mult).then_inc(s_gate, 1)
                dve.wait_ge(s_gate, n + 1)
                dve.tensor_tensor(xt, xt, dn, ALU.add).then_inc(s_out, 1)

        @block.tensor
        def _(pe):
            pe.wait_ge(wl_ok, 1)

            def chunk(c, last):
                for t in range(TPC):
                    rows = slice(t * P, (t + 1) * P)
                    for k in range(KD):
                        ins = split_mm(pe, bank[4][:, t * NCL:(t + 1) * NCL], m.xT_hi[:, k, rows], m.xT_lo[:, k, rows],
                                       c_hi[:, k, :], c_lo[:, k, :], k == 0, k == KD - 1)
                ins.then_inc(s_l, 1)
                pe.wait_ge(wl_ok, 2)
                for t in range(TPC):
                    rows = slice(t * P, (t + 1) * P)
                    if t >= 2:
                        pe.wait_ge(s_db, c * TPC + t - 1)
                    for k in range(KD):
                        ins = split_mm(pe, bank[5 + t % 2][:, :], m.xT_hi[:, k, rows], m.xT_lo[:, k, rows],
                                       w_hi[:, k, :], w_lo[:, k, :], k == 0, k == KD - 1)
                    ins.then_inc(s_d, 1)
                if not last:
                    prep.pe_transpose(pe, p0 + c + 1, bank[0:4])
                    prep.wait_ready(pe, p0 + c + 1)
                    pe.wait_ge(s_dense, (c + 1) * TPC)

            with pe.Fori(0, NCH - 1) as c:
                chunk(c, False)
            chunk(NCH - 1, True)
            pe.wait_ge(s_any, NT)
            pe.matmul(bank[7][0:NCL, 0:1], hit_any[:, :], m.ones[:, :], start=True, stop=True).then_inc(s_cnt, 1)
            pe.wait_ge(s_cl, 1)
            pe.wait_ge(member_ok, 1)
            pe.matmul(bank[0][:, :], cl_sel[:, :], member[:, :], start=True, stop=True).then_inc(s_col, 1)


def network(nc, a):
    with ExitStack() as ctx:
        m = persistent(nc, ctx)
        prep = Prep(nc, ctx, m)
        stage_l0_attention(nc, m, prep, a)
        stage_sparse_ffn(nc, m, prep, a)
        stage_l1_attention(nc, m, prep, a)
        stage_gated_ffn(nc, m, prep, a)


def kernel(**inputs):
    import concourse.bacc as bacc
    from concourse.bass_utils import run_bass_kernel_spmd

    given = {n: np.asarray(v) for n, v in inputs.items()}

    def blocks(w, *lead):
        return w.reshape(*lead, -1, P, w.shape[-1]).swapaxes(-3, -2)

    ctx_rows = given["ctx_4096"].reshape(ROWS, D)
    wk = given["L1_xattn_Wk"].T.reshape(D, KVH, HD)
    wv = given["L1_xattn_Wv"].T.reshape(D, KVH, HD)
    laid = {
        "x": given["x"].reshape(ROWS, D),
        "ctx": ctx_rows,
        "ctxT": ctx_rows.reshape(NCH, CHUNK, KD, P).transpose(0, 3, 2, 1),
        "mask": given["mask_1x1xSxS2_ff0"].reshape(S, S),
        "l0_wq": blocks(given["L0_xattn_Wq_w"].T),
        "l0_wk": blocks(given["L0_xattn_Wk_w"].T),
        "l0_bq": given["L0_xattn_Wq_b"].reshape(KD, P).T,
        "l0_bk": given["L0_xattn_Wk_b"],
        "l0_fnw": given["L0_xattn_fn_w"],
        "l0_qnw": given["L0_xattn_qn_w"],
        "l0_knw": given["L0_xattn_kn_w"],
        "c1": blocks(given["L0_ffn_c1_w"].T),
        "c2": given["L0_ffn_c2_w"].T,
        "w1": blocks(given["L0_ffn_w1"].T),
        "w2": blocks(given["L0_ffn_w2t"]).reshape(P, NI * D),
        "l1_wq": blocks(given["L1_xattn_Wq"].T.reshape(D, KVH, G * HD).swapaxes(0, 1), KVH),
        "l1_wkv": blocks(np.concatenate([wk, wv], axis=2).swapaxes(0, 1), KVH),
        "l1_wo": blocks(given["L1_xattn_Wo"].T.reshape(KVH, G * HD, D), KVH),
        "l1_qnw": given["L1_xattn_q_norm_w"].reshape(HD, 1),
        "l1_knw": given["L1_xattn_k_norm_w"].reshape(HD, 1),
        "l1_w": blocks(given["L1_ffn_weight"].T),
        "l1_b": given["L1_ffn_bias"],
        "cent": blocks(given["L1_ffn_centroids"].T),
        "assign": given["L1_ffn_assignments"],
    }
    nc = bacc.Bacc("TRN2", target_bir_lowering=False, num_devices=1)
    a, arrays = Mem(), {}
    for name, v in laid.items():
        v = np.ascontiguousarray(v)
        arrays[f"in_{name}"] = v
        a.__dict__[name] = nc.dram_tensor(f"in_{name}", v.shape, mybir.dt.from_np(v.dtype), kind="ExternalInput").ap()
    a.out = nc.dram_tensor("out_x", (ROWS, D), F32, kind="ExternalOutput").ap()
    network(nc, a)
    r = run_bass_kernel_spmd(nc, [arrays], core_ids=[0])
    return r.results[0]["out_x"].reshape(given["x"].shape)
```

```python
from contextlib import ExitStack

import numpy as np

import concourse.bass as bass
from concourse import mybir

F32 = mybir.dt.float32
F32R = mybir.dt.float32r
BF16 = mybir.dt.bfloat16
I32 = mybir.dt.int32
ALU = mybir.AluOpType
ACT = mybir.ActivationFunctionType
AX = mybir.AxisListType

P = 128
D = 512
KD = D // P
ROWS = 2048
S = 64
CHUNK = 512
TPC = CHUNK // P
NCH = ROWS // CHUNK
NT = ROWS // P
INTER = 1792
NI = INTER // P
QC = 448
NQ = INTER // QC
SPARSE = 32
BPQ = QC // SPARSE
RANK = 16
RK3 = 3 * 32
H = 32
KVH = 8
HD = 128
G = H // KVH
NCL = 64
LN_EPS = 1e-5
L0_EPS = 1e-6
L1_EPS = 1e-5
OFF = -3e38


def split_mm(pe, out, a_hi, a_lo, b_hi, b_lo, first, last):
    pe.matmul(out, a_hi, b_hi, start=first, stop=False)
    pe.matmul(out, a_lo, b_hi, start=False, stop=False)
    return pe.matmul(out, a_hi, b_lo, start=False, stop=last)


class Prep:

    def __init__(self, nc, ctx, mem):
        self.m = mem
        sem = lambda n: ctx.enter_context(nc.semaphore(n))
        self.var = sem("ln_var_steps")
        self.rstd, self.norm, self.ps = sem("ln_rstd"), sem("ln_norm"), sem("xT_ps")
        self.hi, self.lo = sem("xT_hi_done"), sem("xT_lo_done")

    def dve_stats(self, dve, p, cn, tiles=range(TPC)):
        m = self.m
        for t in tiles:
            ins = dve.bn_stats(m.ln_st[:, t, :], m.x[:, bass.ts(cn * TPC + t, D)])
        if t != TPC - 1:
            return
        ins.then_inc(self.var, 1)
        dve.wait_ge(self.var, 3 * p + 1)
        dve.memset(m.ln_ve[:, :], LN_EPS)
        for t in range(TPC):
            ins = dve.bn_aggr(m.ln_mv[:, t, :], m.ln_st[:, t, :])
        ins.then_inc(self.var, 1)
        dve.wait_ge(self.var, 3 * p + 2)
        dve.tensor_scalar(m.ln_ve[:, :], m.ln_mv[:, :, 1], LN_EPS, None, ALU.add).then_inc(self.var, 1)

    def pool_rstd(self, pool, p):
        m = self.m
        pool.wait_ge(self.var, 3 * p + 3)
        pool.tensor_tensor(m.ln_rs[:, :], m.ln_ve[:, :], m.neg_half[:, 0:TPC], ALU.pow).then_inc(self.rstd, 1)

    def dve_norm(self, dve, p, cn):
        m = self.m
        dve.wait_ge(self.rstd, p + 1)
        for t in range(TPC):
            ins = dve.tensor_scalar(m.xln[:, t, :], m.x[:, bass.ts(cn * TPC + t, D)], m.ln_mv[:, t, 0:1],
                                    m.ln_rs[:, t:t + 1], ALU.subtract, ALU.mult)
        ins.then_inc(self.norm, 1)

    def pe_transpose(self, pe, p, banks, ks=range(KD)):
        m = self.m
        pe.wait_ge(self.norm, p + 1)
        for k in ks:
            for t in range(TPC):
                ins = pe.transpose(banks[k][:, t * P:(t + 1) * P], m.xln[:, t, k * P:(k + 1) * P], m.ident[:, :])
            ins.then_inc(self.ps, 1)

    def act_hi(self, act, p, banks, ks=range(KD)):
        for k in ks:
            act.wait_ge(self.ps, p * KD + k + 1)
            act.copy(self.m.xT_hi[:, k, :], banks[k][:, :]).then_inc(self.hi, 1)

    def dve_lo(self, dve, p, banks, ks=range(KD)):
        for k in ks:
            dve.wait_ge(self.hi, p * KD + k + 1)
            dve.tensor_tensor(self.m.xT_lo[:, k, :], banks[k][:, :], self.m.xT_hi[:, k, :],
                              ALU.subtract).then_inc(self.lo, 1)

    def wait_ready(self, pe, p, k=KD - 1):
        pe.wait_ge(self.lo, p * KD + k + 1)


class Mem:
    pass


def persistent(nc, ctx):
    m = Mem()
    sb = lambda n, s, d=F32: ctx.enter_context(nc.sbuf_tensor(n, s, d))
    m.x = sb("x_res", [P, NT * D])
    m.xT_hi, m.xT_lo = sb("xT_hi", [P, KD, CHUNK], F32R), sb("xT_lo", [P, KD, CHUNK], F32R)
    m.xln = sb("xln", [P, TPC, D])
    m.ident = sb("ident", [P, P])
    m.ones = sb("ones", [P, 1])
    m.neg_half = sb("neg_half", [P, TPC * G])
    m.ln_st, m.ln_mv = sb("ln_st", [P, TPC, 6]), sb("ln_mv", [P, TPC, 2])
    m.ln_ve, m.ln_rs = sb("ln_ve", [P, TPC]), sb("ln_rs", [P, TPC])
    m.next_in = ctx.enter_context(nc.semaphore("next_in"))
    m.bank = [ctx.enter_context(nc.psum_tensor(f"bank{i}", [P, 512], F32)) for i in range(8)]
    return m


def stage_l0_attention(nc, m, prep, fw, a):
    with ExitStack() as ctx:
        sb = lambda n, s, d=F32: ctx.enter_context(nc.sbuf_tensor("a0_" + n, s, d))
        sem = lambda n: ctx.enter_context(nc.semaphore("a0_" + n))
        bq_bank, bk_bank, bxT, bcT, bqT, bkT, b_s, b_att = m.bank
        b_pT = b_s[:, P:2 * P]
        RING = 4
        w_raw = [m.x[:, (NT - 8 + 4 * n) * D:(NT - 4 + 4 * n) * D].rearrange("p (k f) -> p k f", k=KD)
                 for n in range(2)]
        w_hi = [sb(f"w{n}_hi", [P, KD, D], F32R) for n in "qk"]
        w_lo = [sb(f"w{n}_lo", [P, KD, D], F32R) for n in "qk"]
        w1_raw = sb("w1_raw", [P, QC])
        bq, bk = sb("bq", [P, D]), sb("bk", [P, D])
        fnw, wqk = sb("fnw", [P, D]), sb("wqk", [P, D])
        off = sb("off", [P, P])
        craw = sb("craw", [P, 2 * D])
        xn, cw, f, kn = (m.xln[:, n, :] for n in range(4))
        f_hi, f_lo = sb("f_hi", [P, RING * D], F32R), sb("f_lo", [P, RING * D], F32R)
        xT_hi, cT_hi, qT_hi, kT_hi = (m.xT_hi[:, :, n * P:(n + 1) * P] for n in range(4))
        xT_lo, cT_lo, qT_lo, kT_lo = (m.xT_lo[:, :, n * P:(n + 1) * P] for n in range(4))
        qb, kb, qnw, sq = sb("qb", [P, D]), sb("kb", [P, D]), sb("qnw", [P, D]), sb("sq", [P, D])
        prob = sb("prob", [P, P])
        pT_hi, pT_lo = sb("pT_hi", [P, P], F32R), sb("pT_lo", [P, P], F32R)
        st, mv, ve, rs = sb("ln_st", [P, 6]), sb("ln_mv", [P, 2]), sb("ln_ve", [P, 1]), sb("ln_rs", [P, 1])
        css, cve, crs = sb("css", [P, 1]), sb("cve", [P, 1]), sb("crs", [P, 1])
        qkss, qkve, qkrs = sb("qkss", [P, 2]), sb("qkve", [P, 2]), sb("qkrs", [P, 2])
        qrs = sb("qrs", [P, 1])
        nmx, den, rden = sb("nmx", [P, 1]), sb("den", [P, 1]), sb("rden", [P, 1])

        const_in, fnw_in, w_in, xc_in, w1_in = sem("const_in"), sem("fnw_in"), [sem("wq_in"), sem("wk_in")], sem("xc_in"), sem("w1_in")
        ident_ok, off_ok, half_ok = sem("ident_steps"), sem("off_ok"), sem("half_ok")
        c_zero, c_in, ch_ok, cl_ok = sem("c_zero"), sem("c_in"), sem("c_hi_ok"), sem("c_ok")
        wh_ok, wl_ok, wqk_ok, w1h_ok, w1l_ok = sem("w_hi_ok"), sem("w_lo_ok"), sem("wqk_ok"), sem("w1_hi_ok"), sem("w1_ok")
        s_ve, s_rs, s_xn = sem("ln_var_steps"), sem("ln_rs_ok"), sem("xn_ok")
        s_css, s_cve, s_crs, s_cw, s_f, s_fl = (sem("css_ok"), sem("cve_ok"), sem("crs_ok"), sem("cw_ok"), sem("f_ok"),
                                                sem("f_lo_ok"))
        s_xT, s_cT, s_xTh, s_cTh, s_cTl = sem("xT_ps"), sem("cT_ps"), sem("xT_hi_ok"), sem("cT_hi_ok"), sem("xcT_ok")
        s_q, s_k, s_qb, s_kb, s_ss, s_qkve, s_qkrs, s_kn = (
            sem("q_ps"), sem("k_ps"), sem("qb_ok"), sem("kb_ok"), sem("qkss_ok"), sem("qkve_ok"), sem("qkrs_ok"),
            sem("kn_ok"))
        s_qT, s_kT, s_qTh, s_kTh, s_kTl = sem("qT_ps"), sem("kT_ps"), sem("qT_hi_ok"), sem("kT_hi_ok"), sem("qkT_ok")
        s_s, s_nmx, s_p, s_rden = sem("s_ps"), sem("scores_max_steps"), sem("prob_ok"), sem("rden_ok")
        s_pT, s_pTh, s_pTl, s_att, s_x = sem("pT_ps"), sem("pT_hi_ok"), sem("pT_ok"), sem("att_ps"), sem("x_ok")
        block = ctx.enter_context(nc.Block())

        blk = lambda bank: bank[:, :].rearrange("p (k s) -> p k s", k=KD)
        x_rows, c_rows = a.x.rearrange("(n p) d -> n p d", p=P), a.ctx.rearrange("(n p) d -> n p d", p=P)

        def run(body, tail=None):
            def go(eng):
                body(0, first=True)
                with eng.Fori(1, NT - 2) as n:
                    body(n)
                body(NT - 2, ahead=False)
                body(NT - 1, ahead=False, project=False)
                if tail:
                    tail(NT - 1)
            return go

        @block.sync
        def _(sp):
            def load(n):
                sp.dma_start(m.x[:, bass.ts(n, D)], x_rows[n]).then_inc(xc_in, 16)
                sp.dma_start(craw[:, bass.ts(n % 2, D)], c_rows[n]).then_inc(xc_in, 16)

            load(0)
            sp.dma_start(fnw[:, :], a.l0_fnw.partition_broadcast(P)).then_inc(fnw_in, 16)
            sp.dma_start(w_raw[0], a.l0_wq).then_inc(w_in[0], 16)
            sp.dma_start(w_raw[1], a.l0_wk).then_inc(w_in[1], 16)
            sp.dma_start(bq[:, :], a.l0_bq.partition_broadcast(P)).then_inc(const_in, 16)
            sp.dma_start(bk[:, :], a.l0_bk.partition_broadcast(P)).then_inc(const_in, 16)
            sp.dma_start(qnw[:, :], a.l0_qnw.partition_broadcast(P)).then_inc(const_in, 16)
            sp.dma_start(wqk[:, :], a.l0_knw.partition_broadcast(P)).then_inc(const_in, 16)
            sp.wait_ge(xc_in, 32)
            load(1)
            sp.dma_start(w1_raw[:, :], a.w1[:, 0:QC]).then_inc(w1_in, 16)
            sp.wait_ge(wl_ok, 2 * KD)
            sp.wait_ge(c_zero, 2)
            for n in range(3):
                sp.dma_start(fw.c1_raw[:, :, 32 * n:32 * n + RANK], a.c1).then_inc(c_in, 16)
                sp.dma_start(fw.c2_raw[32 * n:32 * n + RANK, :], a.c2).then_inc(c_in, 16)
            with sp.Fori(2, NT) as n:
                sp.wait_ge(s_f, n * 2)
                load(n)

        @block.gpsimd
        def _(pool):
            pool.memset(m.ident[:, :], 0.0).then_inc(ident_ok, 1)
            pool.memset(m.neg_half[:, :], -0.5).then_inc(half_ok, 1)
            pool.wait_ge(ident_ok, 1)
            pool.affine_select(out=m.ident[:, :], in_=m.ident[:, :], compare_op=ALU.not_equal, fill=1.0, base=0,
                               pattern=[[-1, P]], channel_multiplier=1).then_inc(ident_ok, 1)
            pool.memset(m.ones[:, :], 1.0).then_inc(half_ok, 1)
            pool.memset(fw.c1_raw[:, :, :], 0.0).then_inc(c_zero, 1)
            pool.memset(fw.c2_raw[0:RK3, :], 0.0).then_inc(c_zero, 1)
            pool.wait_ge(half_ok, 2)
            pool.wait_ge(c_zero, 2)
            pool.wait_ge(fnw_in, 16)

            def normalise(n):
                pool.wait_ge(xc_in, (n + 1) * 32)
                pool.tensor_tensor(cw, craw[:, bass.ts(n % 2, D)], fnw[:, :], ALU.mult).then_inc(s_cw, 1)
                pool.wait_ge(s_ve, n * 3 + 3)
                pool.tensor_tensor(rs[:, :], ve[:, :], m.neg_half[:, 0:1], ALU.pow).then_inc(s_rs, 1)
                pool.wait_ge(s_cve, n + 1)
                pool.tensor_tensor(crs[:, :], cve[:, :], m.neg_half[:, 0:1], ALU.pow).then_inc(s_crs, 1)

            def features_lo(n):
                pool.wait_ge(s_f, n * 2 + 2)
                pool.tensor_tensor(f_lo[:, bass.ts(n % RING, D)], f, f_hi[:, bass.ts(n % RING, D)],
                                   ALU.subtract).then_inc(s_fl, 1)

            def project_qk(n):
                pool.wait_ge(s_qkve, n + 1)
                pool.tensor_tensor(qkrs[:, :], qkve[:, :], m.neg_half[:, 0:2], ALU.pow).then_inc(s_qkrs, 1)

            def body(n, first=False, ahead=True, project=True):
                if ahead:
                    normalise(n + 2)
                if project and not first:
                    split_w1(n - 1)
                if project:
                    project_qk(n + 1)
                if ahead:
                    features_lo(n + 2)
                elif project:
                    split_w1(n)
                    prep.pool_rstd(pool, 0)
                else:
                    split_c1_c2()

            def split_w1(n):
                pool.wait_ge(w1h_ok, n + 1)
                pool.tensor_tensor(fw.w1_lo[:, bass.ts(n, QC)], w1_raw[:, :], fw.w1_hi[:, bass.ts(n, QC)],
                                   ALU.subtract).then_inc(w1l_ok, 1)

            normalise(0)
            features_lo(0)
            normalise(1)
            features_lo(1)
            project_qk(0)

            def split_c1_c2():
                pool.wait_ge(ch_ok, 2)
                pool.tensor_tensor(fw.c1_lo[:, :, :], fw.c1_raw[:, :, :], fw.c1_hi[:, :, :], ALU.subtract).then_inc(cl_ok, 1)
                pool.wait_ge(cl_ok, 1)
                pool.tensor_tensor(fw.c2st[64:96, :], fw.c2_raw[64:96, :], fw.c2st[64:96, :], ALU.subtract).then_inc(cl_ok, 1)
                pool.wait_ge(cl_ok, 2)

            run(body, split_w1)(pool)

        @block.scalar
        def _(act):
            def normalise(n):
                act.wait_ge(xc_in, (n + 1) * 32)
                act.activation(sq[:, :], craw[:, bass.ts(n % 2, D)], ACT.Square, accum_out=css[:, :]).then_inc(s_css, 1)
                act.wait_ge(s_cw, n + 1)
                act.wait_ge(s_crs, n + 1)
                act.activation(f, cw, ACT.Copy, scale=crs[:, :]).then_inc(s_f, 1)

            def features_hi(n):
                act.activation(f_hi[:, bass.ts(n % RING, D)], cw, ACT.Copy, scale=crs[:, :]).then_inc(s_f, 1)

            def rows_T(n):
                act.wait_ge(s_xT, n + 1)
                act.copy(xT_hi[:, :, :], blk(bxT)).then_inc(s_xTh, 1)

            def features_T(n):
                act.wait_ge(s_cT, n + 1)
                act.copy(cT_hi[:, :, :], blk(bcT)).then_inc(s_cTh, 1)

            def squares(n):
                act.wait_ge(s_qb, n + 1)
                act.activation(qnw[:, :], qb[:, :], ACT.Square, accum_out=qkss[:, 0:1])
                act.wait_ge(s_kb, n + 1)
                act.activation(sq[:, :], kb[:, :], ACT.Square, accum_out=qkss[:, 1:2]).then_inc(s_ss, 1)

            def qk_T(n):
                act.wait_ge(s_qT, n + 1)
                act.copy(qT_hi[:, :, :], blk(bqT)).then_inc(s_qTh, 1)
                act.wait_ge(s_kT, n + 1)
                act.copy(kT_hi[:, :, :], blk(bkT)).then_inc(s_kTh, 1)

            def body(n, first=False, ahead=True, project=True):
                if ahead:
                    normalise(n + 2)
                if project:
                    squares(n + 1)
                if ahead:
                    features_hi(n + 2)
                    rows_T(n + 2)
                act.wait_ge(s_nmx, n * 2 + 2)
                act.activation(prob[:, :], prob[:, :], ACT.Exp, bias=nmx[:, :], accum_out=den[:, :]).then_inc(s_p, 1)
                if ahead:
                    features_T(n + 2)
                if not first:
                    act.wait_ge(w1l_ok, n)
                    act.dma_start(w1_raw[:, :], a.w1[:, bass.ts(n, QC)]).then_inc(w1_in, 16)
                if project:
                    qk_T(n + 1)
                act.wait_ge(s_pT, n + 1)
                act.copy(pT_hi[:, :], b_pT).then_inc(s_pTh, 1)
                if not project:
                    prep.act_hi(act, 0, m.bank[2:6])
                act.wait_ge(w1_in, (n + 1) * 16)
                act.copy(fw.w1_hi[:, bass.ts(n, QC)], w1_raw[:, :]).then_inc(w1h_ok, 1)
                if project and not ahead:
                    act.wait_ge(c_in, 96)
                    act.copy(fw.c1_hi[:, :, :], fw.c1_raw[:, :, :]).then_inc(ch_ok, 1)
                    act.copy(fw.c2st[:, :], fw.c2_raw[0:RK3, :]).then_inc(ch_ok, 1)

            normalise(0)
            features_hi(0)
            rows_T(0)
            features_T(0)
            for n in range(2):
                act.wait_ge(w_in[n], 16)
                for k in range(KD):
                    act.copy(w_hi[n][:, k, :], w_raw[n][:, k, :]).then_inc(wh_ok, 1)
            normalise(1)
            features_hi(1)
            squares(0)
            rows_T(1)
            features_T(1)
            qk_T(0)
            run(body)(act)

        @block.vector
        def _(dve):
            def normalise(n):
                xt = m.x[:, bass.ts(n, D)]
                dve.wait_ge(xc_in, (n + 1) * 32)
                dve.bn_stats(st[:, :], xt).then_inc(s_ve, 1)
                dve.wait_ge(s_ve, n * 3 + 1)
                dve.memset(ve[:, :], LN_EPS)
                dve.bn_aggr(mv[:, :], st[:, :]).then_inc(s_ve, 1)
                dve.wait_ge(s_ve, n * 3 + 2)
                dve.tensor_scalar(ve[:, :], mv[:, 1:2], LN_EPS, None, ALU.add).then_inc(s_ve, 1)
                dve.wait_ge(s_css, n + 1)
                dve.tensor_scalar(cve[:, :], css[:, :], 1.0 / D, L0_EPS, ALU.mult, ALU.add).then_inc(s_cve, 1)
                dve.wait_ge(s_rs, n + 1)
                dve.tensor_scalar(xn, xt, mv[:, 0:1], rs[:, :], ALU.subtract, ALU.mult).then_inc(s_xn, 1)

            def rows_T(n):
                dve.wait_ge(s_xTh, n + 1)
                dve.tensor_tensor(xT_lo[:, :, :], blk(bxT), xT_hi[:, :, :], ALU.subtract).then_inc(s_cTl, 1)

            def features_T(n):
                dve.wait_ge(s_cTh, n + 1)
                dve.tensor_tensor(cT_lo[:, :, :], blk(bcT), cT_hi[:, :, :], ALU.subtract).then_inc(s_cTl, 1)

            def biases(n):
                dve.wait_ge(s_q, n + 1)
                dve.tensor_tensor(qb[:, :], bq_bank[:, :], bq[:, :], ALU.add).then_inc(s_qb, 1)
                dve.wait_ge(s_k, n + 1)
                dve.tensor_tensor(kb[:, :], bk_bank[:, :], bk[:, :], ALU.add).then_inc(s_kb, 1)

            def mean_squares(n):
                dve.wait_ge(s_ss, n + 1)
                dve.tensor_scalar(qkve[:, :], qkss[:, :], D * L0_EPS, None, ALU.add).then_inc(s_qkve, 1)

            def scale_keys(n):
                dve.wait_ge(s_qkrs, n + 1)
                dve.scalar_tensor_tensor(kn, kb[:, :], qkrs[:, 1:2], wqk[:, :], ALU.mult, ALU.mult).then_inc(s_kn, 1)

            def qk_T(n):
                dve.wait_ge(s_qTh, n + 1)
                dve.tensor_tensor(qT_lo[:, :, :], blk(bqT), qT_hi[:, :, :], ALU.subtract)
                dve.wait_ge(s_kTh, n + 1)
                dve.tensor_tensor(kT_lo[:, :, :], blk(bkT), kT_hi[:, :, :], ALU.subtract).then_inc(s_kTl, 1)

            def attended(n):
                dve.wait_ge(s_att, n + 1)
                dve.wait_ge(s_rden, n + 1)
                xt = m.x[:, bass.ts(n, D)]
                dve.scalar_tensor_tensor(xt, b_att[:, :], rden[:, :], xt, ALU.mult, ALU.add).then_inc(s_x, 1)

            def body(n, first=False, ahead=True, project=True):
                if ahead:
                    normalise(n + 2)
                if project:
                    biases(n + 1)
                dve.wait_ge(s_s, n + 1)
                dve.scalar_tensor_tensor(prob[:, :], b_s[:, 0:P], qrs[:, :], off[:, :], ALU.mult, ALU.add).then_inc(s_nmx, 1)
                if project:
                    mean_squares(n + 1)
                dve.wait_ge(s_nmx, n * 2 + 1)
                dve.tensor_reduce(nmx[:, :], prob[:, :], AX.X, ALU.max, negate=True).then_inc(s_nmx, 1)
                if project:
                    scale_keys(n + 1)
                else:
                    prep.dve_norm(dve, 0, 0)
                if ahead:
                    rows_T(n + 2)
                    features_T(n + 2)
                if not first:
                    attended(n - 1)
                    dve.wait_ge(s_x, n)
                dve.wait_ge(s_p, n + 1)
                dve.reciprocal(rden[:, :], den[:, :]).then_inc(s_rden, 1)
                if project:
                    dve.tensor_copy(qrs[:, :], qkrs[:, 0:1])
                    qk_T(n + 1)
                dve.wait_ge(s_pTh, n + 1)
                dve.tensor_tensor(pT_lo[:, :], b_pT, pT_hi[:, :], ALU.subtract).then_inc(s_pTl, 1)
                if not project:
                    prep.dve_lo(dve, 0, m.bank[2:6])
                elif not ahead:
                    prep.dve_stats(dve, 0, 0)

            dve.memset(off[:, :], OFF).then_inc(off_ok, 1)
            dve.wait_ge(off_ok, 1)
            dve.memset(off[0:S, 0:S], 0.0)
            dve.memset(off[S:P, S:P], 0.0).then_inc(off_ok, 1)
            normalise(0)
            rows_T(0)
            features_T(0)
            for n in range(2):
                for k in range(KD):
                    dve.wait_ge(wh_ok, n * KD + k + 1)
                    dve.tensor_tensor(w_lo[n][:, k, :], w_raw[n][:, k, :], w_hi[n][:, k, :], ALU.subtract).then_inc(wl_ok, 1)
            normalise(1)
            dve.wait_ge(const_in, 64)
            dve.scalar_tensor_tensor(wqk[:, :], qnw[:, :], float(D) ** 0.5, wqk[:, :], ALU.mult, ALU.mult).then_inc(wqk_ok, 1)
            dve.wait_ge(wqk_ok, 1)
            dve.wait_ge(off_ok, 2)
            biases(0)
            mean_squares(0)
            rows_T(1)
            scale_keys(0)
            features_T(1)
            dve.tensor_copy(qrs[:, :], qkrs[:, 0:1])
            qk_T(0)
            run(body, attended)(dve)

        @block.tensor
        def _(pe):
            def rows_T(n):
                pe.wait_ge(s_xn, n + 1)
                for k in range(KD):
                    ins = pe.transpose(bxT[:, k * P:(k + 1) * P], xn[:, k * P:(k + 1) * P], m.ident[:, :])
                ins.then_inc(s_xT, 1)
                pe.wait_ge(s_f, n * 2 + 1)
                for k in range(KD):
                    ins = pe.transpose(bcT[:, k * P:(k + 1) * P], f[:, k * P:(k + 1) * P], m.ident[:, :])
                ins.then_inc(s_cT, 1)

            def project_qk(n, first=False):
                for bank, hi, lo, w, s in ((bq_bank, xT_hi, xT_lo, 0, s_q), (bk_bank, cT_hi, cT_lo, 1, s_k)):
                    pe.wait_ge(s_cTl, n * 2 + w + 1)
                    for k in range(KD):
                        if first:
                            pe.wait_ge(wl_ok, w * KD + k + 1)
                        ins = split_mm(pe, bank[:, :], hi[:, k, :], lo[:, k, :], w_hi[w][:, k, :], w_lo[w][:, k, :],
                                       k == 0, k == KD - 1)
                    ins.then_inc(s, 1)

            def q_T(n):
                pe.wait_ge(s_qb, n + 1)
                for k in range(KD):
                    ins = pe.transpose(bqT[:, k * P:(k + 1) * P], qb[:, k * P:(k + 1) * P], m.ident[:, :])
                ins.then_inc(s_qT, 1)

            def k_T(n):
                pe.wait_ge(s_kn, n + 1)
                for k in range(KD):
                    ins = pe.transpose(bkT[:, k * P:(k + 1) * P], kn[:, k * P:(k + 1) * P], m.ident[:, :])
                ins.then_inc(s_kT, 1)

            def attend(n):
                pe.wait_ge(s_pTl, n + 1)
                pe.wait_ge(s_fl, n + 1)
                pe.wait_ge(s_rden, n + 1)
                row = bass.ts(n % RING, D)
                split_mm(pe, b_att[:, :], pT_hi[:, :], pT_lo[:, :], f_hi[:, row], f_lo[:, row], True, True).then_inc(s_att, 1)

            def body(n, first=False, ahead=True, project=True):
                if project:
                    project_qk(n + 1)
                pe.wait_ge(s_kTl, n + 1)
                if not first:
                    pe.wait_ge(s_pTl, n)
                for k in range(KD):
                    ins = split_mm(pe, b_s[:, 0:P], qT_hi[:, k, :], qT_lo[:, k, :], kT_hi[:, k, :], kT_lo[:, k, :],
                                   k == 0, k == KD - 1)
                ins.then_inc(s_s, 1)
                if ahead:
                    rows_T(n + 2)
                if not first:
                    attend(n - 1)
                if project:
                    q_T(n + 1)
                pe.wait_ge(s_p, n + 1)
                pe.transpose(b_pT, prob[:, :], m.ident[:, :]).then_inc(s_pT, 1)
                if project:
                    k_T(n + 1)
                else:
                    prep.pe_transpose(pe, 0, m.bank[2:6])

            pe.wait_ge(ident_ok, 2)
            pe.wait_ge(half_ok, 2)
            rows_T(0)
            project_qk(0, first=True)
            rows_T(1)
            q_T(0)
            k_T(0)
            run(body, attend)(pe)


def stage_sparse_ffn(nc, m, prep, fw, a):
    with ExitStack() as ctx:
        sb = lambda n, s, d=F32: ctx.enter_context(nc.sbuf_tensor("f0_" + n, s, d))
        sem = lambda n: ctx.enter_context(nc.semaphore("f0_" + n))
        bank = m.bank
        i_banks, h_banks, hT_banks, o_banks = bank[0:2], bank[2:4], bank[4:6], bank[6:8]
        low_bank = bank[7]
        prep_banks = [bank[0], bank[1], bank[4], bank[5]]
        w1_hi, w1_lo = (w[:, :].rearrange("p (k i) -> p k i", k=KD) for w in (fw.w1_hi, fw.w1_lo))
        c1_hi, c1_lo, c2st = fw.c1_hi, fw.c1_lo, fw.c2st
        h = fw.c2_raw
        w2_hi, w2_lo = sb("w2_hi", [P, NI * D], F32R), sb("w2_lo", [P, NI * D], F32R)
        NP = 7
        PW = NI * D // NP
        raw = [m.xln[:, :, :].rearrange("p t d -> p (t d)")[:, n * PW:(n + 1) * PW] for n in range(2)]
        low = sb("low", [RK3, CHUNK], F32R)
        desc = sb("desc", [P, SPARSE], BF16)
        desc_i = sb("desc_i", [P, SPARSE], I32)
        bmax = [sb(f"bmax{n}", [P, BPQ]) for n in range(2)]
        eq = [sb(f"eq{n}", [P, QC], BF16) for n in range(2)]
        rank = [sb(f"rank{n}", [P, QC], BF16) for n in range(2)]
        rmax = [sb(f"rmax{n}", [P, BPQ], BF16) for n in range(2)]
        hT_hi, hT_lo = sb("hT_hi", [P, NI, P], F32R), sb("hT_lo", [P, NI, P], F32R)

        raw_in, wh_ok, wl_ok = [sem("raw0_in"), sem("raw1_in")], sem("w2_hi_ok"), sem("w2_ok")
        iota_ok, desc_ok = sem("iota_ok"), sem("desc_ok")
        s_low, s_lowh, s_lowl = sem("low_ps"), sem("low_hi_ok"), sem("low_ok")
        s_i, s_h, s_max, s_eq, s_rank = sem("inter_ps"), sem("h_ps"), sem("bmax_ok"), sem("eq_ok"), sem("rank_ok")
        s_rmax, s_hot, s_hm = sem("rmax_ok"), sem("one_hot_ok"), sem("h_ok")
        s_hT, s_hTh, s_hTl, s_o, s_x = sem("hT_ps"), sem("hT_hi_ok"), sem("hT_ok"), sem("out_ps"), sem("x_ok")
        block = ctx.enter_context(nc.Block())

        TG = [slice(4 * g, min(4 * g + 4, NI)) for g in range(NQ)]

        @block.sync
        def _(sp):
            for n in range(NP):
                if n >= 2:
                    sp.wait_ge(wl_ok, n - 1)
                sp.dma_start(raw[n % 2], a.w2[:, n * PW:(n + 1) * PW]).then_inc(raw_in[n % 2], 16)
            sp.wait_ge(prep.ps, (NCH + 1) * KD)
            sp.dma_start(m.xln[:, :, :], a.l1_wq[0]).then_inc(m.next_in, 16)

        @block.gpsimd
        def _(pool):
            pool.iota(desc_i[:, :], pattern=[[-1, SPARSE]], base=SPARSE, channel_multiplier=0).then_inc(iota_ok, 1)
            pool.wait_ge(iota_ok, 1)
            pool.tensor_copy(desc[:, :], desc_i[:, :]).then_inc(desc_ok, 1)
            pool.wait_ge(desc_ok, 1)

            def rank_marks(n, q):
                pool.wait_ge(s_eq, n * NQ + q + 1)
                pool.tensor_tensor(rank[q % 2][:, :].rearrange("p (b s) -> p b s", s=SPARSE),
                                   eq[q % 2][:, :].rearrange("p (b s) -> p b s", s=SPARSE),
                                   desc[:, :].unsqueeze(1).broadcast_to([P, BPQ, SPARSE]), ALU.mult).then_inc(s_rank, 1)

            def split_w2(n):
                cols = slice(n * PW, (n + 1) * PW)
                pool.wait_ge(wh_ok, n + 1)
                pool.tensor_tensor(w2_lo[:, cols], raw[n % 2], w2_hi[:, cols], ALU.subtract).then_inc(wl_ok, 1)

            w2_pieces = {(0, 1): [1], (0, 3): [2, 3], (1, 0): [4], (1, 1): [5], (1, 2): [6]}

            def chunk(c, first=False):
                if first:
                    split_w2(0)
                for t in range(TPC):
                    for q in range(NQ):
                        rank_marks(c * TPC + t, q)
                        if first:
                            for n in w2_pieces.get((t, q), []):
                                split_w2(n)
                    if t == TPC - 3:
                        prep.pool_rstd(pool, c + 1)

            chunk(0, first=True)
            with pool.Fori(1, NCH) as c:
                chunk(c)

        @block.scalar
        def _(act):
            def low_hi(c):
                act.wait_ge(s_low, c + 1)
                act.copy(low[:, :], low_bank[0:RK3, :]).then_inc(s_lowh, 1)

            def hidden_hi(n, g):
                w = TG[g].stop - TG[g].start
                act.wait_ge(s_hT, n * NQ + g + 1)
                act.copy(hT_hi[:, TG[g], :], hT_banks[g % 2][:, 0:w * P].rearrange("p (j s) -> p j s", s=P))\
                   .then_inc(s_hTh, 1)

            def split_w2(n):
                act.wait_ge(raw_in[n % 2], 16 * (n // 2 + 1))
                act.copy(w2_hi[:, n * PW:(n + 1) * PW], raw[n % 2]).then_inc(wh_ok, 1)

            def chunk(c, first=False):
                low_hi(c)
                for t in range(TPC):
                    for g in range(NQ):
                        if not (first and t == 0):
                            hidden_hi(c * TPC + t - 1, g)
                        if first and t < 2 and t * NQ + g < NP:
                            split_w2(t * NQ + g)
                prep.act_hi(act, c + 1, prep_banks)

            chunk(0, first=True)
            with act.Fori(1, NCH) as c:
                chunk(c)
            for g in range(NQ):
                hidden_hi(NT - 1, g)

        @block.vector
        def _(dve):
            blocks = lambda ap: ap.rearrange("p (b s) -> p b s", s=SPARSE)

            def find_max(n, q):
                e = n * NQ + q + 1
                inter = blocks(i_banks[q % 2][:, 0:QC])
                dve.wait_ge(s_i, e)
                dve.tensor_reduce(bmax[q % 2][:, :], inter, AX.X, ALU.max).then_inc(s_max, 1)
                dve.wait_ge(s_max, e)
                dve.tensor_tensor(blocks(eq[q % 2][:, :]), inter,
                                  bmax[q % 2][:, :].unsqueeze(2).broadcast_to([P, BPQ, SPARSE]),
                                  ALU.is_equal).then_inc(s_eq, 1)

            def select(n, q):
                e = n * NQ + q + 1
                rk = blocks(rank[q % 2][:, :])
                dve.wait_ge(s_rank, e)
                dve.tensor_reduce(rmax[q % 2][:, :], rk, AX.X, ALU.max).then_inc(s_rmax, 1)
                dve.wait_ge(s_rmax, e)
                dve.tensor_tensor(rk, rk, rmax[q % 2][:, :].unsqueeze(2).broadcast_to([P, BPQ, SPARSE]),
                                  ALU.is_equal).then_inc(s_hot, 1)
                dve.wait_ge(s_hot, e)
                dve.wait_ge(s_h, e)
                dve.scalar_tensor_tensor(h[:, q * QC:(q + 1) * QC], h_banks[q % 2][:, 0:QC], 0.0, rank[q % 2][:, :],
                                         ALU.max, ALU.mult).then_inc(s_hm, 1)

            def hidden_lo(n, g):
                w = TG[g].stop - TG[g].start
                dve.wait_ge(s_hTh, n * NQ + g + 1)
                dve.tensor_tensor(hT_lo[:, TG[g], :], hT_banks[g % 2][:, 0:w * P].rearrange("p (j s) -> p j s", s=P),
                                  hT_hi[:, TG[g], :], ALU.subtract).then_inc(s_hTl, 1)

            def add_out(n, odd):
                dve.wait_ge(s_o, n + 1)
                xt = m.x[:, bass.ts(n, D)]
                dve.tensor_tensor(xt, o_banks[odd][:, :], xt, ALU.add).then_inc(s_x, 1)

            def chunk(c, first=False):
                dve.wait_ge(s_lowh, c + 1)
                dve.tensor_tensor(low[32:64, :], low_bank[32:64, :], low[32:64, :], ALU.subtract).then_inc(s_lowl, 1)
                for t in range(TPC):
                    n, before = c * TPC + t, not (first and t == 0)
                    for q in range(NQ):
                        find_max(n, q)
                        if before:
                            hidden_lo(n - 1, q)
                        if q >= 1:
                            select(n, q - 1)
                    select(n, NQ - 1)
                    if t < 2:
                        prep.dve_stats(dve, c + 1, (c + 1) % NCH, range(t * TPC // 2, (t + 1) * TPC // 2))
                    if before:
                        if t == TPC - 1:
                            prep.dve_lo(dve, c + 1, prep_banks)
                        add_out(n - 1, (t + 1) % 2)
                    if t == TPC - 2:
                        prep.dve_norm(dve, c + 1, (c + 1) % NCH)

            chunk(0, first=True)
            with dve.Fori(1, NCH) as c:
                chunk(c)
            for g in range(NQ):
                hidden_lo(NT - 1, g)
            add_out(NT - 1, 1)

        @block.tensor
        def _(pe):
            def hidden_T(n, g):
                if g == 0:
                    pe.wait_ge(s_hm, (n + 1) * NQ)
                if g >= 2:
                    pe.wait_ge(s_hTl, n * NQ + g - 1)
                for b, j in enumerate(range(TG[g].start, TG[g].stop)):
                    ins = pe.transpose(hT_banks[g % 2][:, b * P:(b + 1) * P], h[:, j * P:(j + 1) * P], m.ident[:, :])
                ins.then_inc(s_hT, 1)

            def out_rows(n, g, odd, free=True, split=False):
                pe.wait_ge(s_hTl, n * NQ + g + 1)
                if split:
                    pe.wait_ge(wl_ok, -(-TG[g].stop * D // PW))
                if free and g == 0:
                    pe.wait_ge(s_x, n - 1)
                for j in range(TG[g].start, TG[g].stop):
                    cols = slice(j * D, (j + 1) * D)
                    ins = split_mm(pe, o_banks[odd][:, :], hT_hi[:, j, :], hT_lo[:, j, :], w2_hi[:, cols], w2_lo[:, cols],
                                   j == 0, j == NI - 1)
                if g == NQ - 1:
                    ins.then_inc(s_o, 1)

            def block_scores(c, t, n, q, before, first):
                cols = slice(q * QC, (q + 1) * QC)
                if t == 0 and q == 0:
                    pe.wait_ge(s_lowl, c + 1)
                if before or q >= 2:
                    pe.wait_ge(s_eq, n * NQ + q - 1)
                pe.matmul(i_banks[q % 2][:, 0:QC], low[:, t * P:(t + 1) * P], c2st[:, cols], start=True, stop=True).then_inc(s_i, 1)

            def hidden(n, q, t, before):
                rows, cols = slice(t * P, (t + 1) * P), slice(q * QC, (q + 1) * QC)
                if before or q >= 2:
                    pe.wait_ge(s_hm, n * NQ + q - 1)
                for k in range(KD):
                    ins = split_mm(pe, h_banks[q % 2][:, 0:QC], m.xT_hi[:, k, rows], m.xT_lo[:, k, rows],
                                   w1_hi[:, k, cols], w1_lo[:, k, cols], k == 0, k == KD - 1)
                ins.then_inc(s_h, 1)

            def chunk(c, first=False):
                for k in range(KD):
                    ins = split_mm(pe, low_bank[0:RK3, :], c1_hi[:, k, :], c1_lo[:, k, :], m.xT_hi[:, k, :], m.xT_lo[:, k, :],
                                   k == 0, k == KD - 1)
                ins.then_inc(s_low, 1)
                for t in range(TPC):
                    n, before = c * TPC + t, not (first and t == 0)
                    late_low = t == 0
                    old = dict(odd=(t + 1) % 2, free=not (first and t < 3), split=first and t == 1)
                    for q in range(NQ):
                        if before:
                            hidden_T(n - 1, q)
                        for what in ("hi" if late_low and q == 0 else "ih"):
                            if what == "i":
                                block_scores(c, t, n, q, before, first)
                            else:
                                hidden(n, q, t, before)
                        if before and q >= 1:
                            out_rows(n - 1, q - 1, **old)
                    if t == TPC - 1:
                        pe.wait_ge(s_eq, (n + 1) * NQ)
                        pe.wait_ge(s_hTl, n * NQ)
                        prep.pe_transpose(pe, c + 1, prep_banks)
                    if before:
                        out_rows(n - 1, NQ - 1, **old)
                prep.wait_ready(pe, c + 1)
                pe.wait_ge(s_x, (c + 1) * TPC - 2)

            chunk(0, first=True)
            with pe.Fori(1, NCH) as c:
                chunk(c)
            for g in range(NQ):
                hidden_T(NT - 1, g)
                if g >= 1:
                    out_rows(NT - 1, g - 1, 1)
            out_rows(NT - 1, NQ - 1, 1)


def stage_l1_attention(nc, m, prep, a):
    p0 = NCH
    with ExitStack() as ctx:
        sb = lambda n, s, d=F32: ctx.enter_context(nc.sbuf_tensor("a1_" + n, s, d))
        sem = lambda n: ctx.enter_context(nc.semaphore("a1_" + n))
        bank = m.bank
        q_raw, kv_raw, o_raw = sb("q_raw", [P, KD, G * HD]), sb("kv_raw", [P, KD, 2 * HD]), sb("o_raw", [P, G, D])
        wq_hi, wq_lo = sb("wq_hi", [P, KD, G * HD], F32R), sb("wq_lo", [P, KD, G * HD], F32R)
        wkv_hi, wkv_lo = sb("wkv_hi", [P, KD, 2 * HD], F32R), sb("wkv_lo", [P, KD, 2 * HD], F32R)
        wo_hi, wo_lo = sb("wo_hi", [P, G, D], F32R), sb("wo_lo", [P, G, D], F32R)
        craw = sb("craw", [P, KD, CHUNK])
        cT_hi, cT_lo = sb("cT_hi", [P, KD, CHUNK], F32R), sb("cT_lo", [P, KD, CHUNK], F32R)
        qT_hi, qT_lo = sb("qT_hi", [P, G, CHUNK], F32R), sb("qT_lo", [P, G, CHUNK], F32R)
        q2 = sb("q2", [P, G, CHUNK])
        v_hi, v_lo = sb("v_hi", [P, TPC, HD], F32R), sb("v_lo", [P, TPC, HD], F32R)
        kn = sb("kn", [P, TPC, HD])
        kT = sb("kT", [P, TPC, 2, P], F32R)
        prob = sb("prob", [P, TPC, G * P])
        pT_hi = [sb(f"pT_hi{n}", [P, G * P], F32R) for n in range(2)]
        pT_lo = [sb(f"pT_lo{n}", [P, G * P], F32R) for n in range(2)]
        oT_hi, oT_lo = sb("oT_hi", [P, TPC, G * P], F32R), sb("oT_lo", [P, TPC, G * P], F32R)
        mask, wqk, knw = sb("mask", [P, P]), sb("wqk", [P, 1]), sb("knw", [P, 1])
        kss, kve, krs = sb("kss", [P, TPC]), sb("kve", [P, TPC]), sb("krs", [P, TPC])
        qss, qve, qrs = sb("qss", [P, TPC * G]), sb("qve", [P, TPC * G]), sb("qrs", [P, TPC * G])
        nmx, den, rden = sb("nmx", [P, TPC * G]), sb("den", [P, TPC * G]), sb("rden", [P, TPC * G])

        q_in, kv_in, o_in, c_in, const_in = sem("wq_in"), sem("wkv_in"), sem("wo_in"), sem("ctx_in"), sem("const_in")
        mask_ok, wqk_ok = sem("mask_ok"), sem("wqk_ok")
        wqh_ok, wql_ok, wkvh_ok, wkvl_ok = sem("wq_hi_ok"), sem("wq_ok"), sem("wkv_hi_ok"), sem("wkv_ok")
        woh_ok, wol_ok, s_cTh, s_cTl = sem("wo_hi_ok"), sem("wo_ok"), sem("cT_hi_ok"), sem("cT_ok")
        s_kv, s_kvact, s_vl, s_kve, s_krs, s_kn = (sem("kv_ps"), sem("kv_act"), sem("v_ok"), sem("kve_ok"),
                                                   sem("krs_ok"), sem("kn_ok"))
        s_kT, s_kTh, s_kTl = sem("kT_ps"), sem("kT_hi_ok"), sem("kT_ok")
        s_q, s_qact, s_ql, s_qss, s_qve, s_qrs = (sem("q_ps"), sem("q_act"), sem("q_ok"), sem("qss_ps"),
                                                  sem("qve_ok"), sem("qrs_ok"))
        s_qsum, wq0_ok = sem("qsum_ok"), sem("wq0_ok")
        s_s, s_sc, s_e, s_rden, s_p = (sem("s_ps"), sem("scores_steps"), sem("exp_ok"), sem("rden_ok"), sem("prob_ok"))
        s_pT, s_pTh, s_pTl = sem("pT_ps"), sem("pT_hi_ok"), sem("pT_ok")
        s_pv, s_oTh, s_oTl, s_o, s_x = sem("pv_ps"), sem("oT_hi_ok"), sem("oT_ok"), sem("o_ps"), sem("x_ok")
        block = ctx.enter_context(nc.Block())
        s_banks = [bank[6:8], bank[4:6], bank[6:8], bank[4:6]]
        q_banks = [bank[2], bank[3], bank[0], bank[1]]
        sq_banks = [bank[0], bank[1], bank[6], bank[7]]
        kv_banks, kT_bank = [bank[2], bank[3]], bank[2]
        pT_banks, pv_banks, o_banks = [bank[6], bank[7]], [bank[4], bank[5]], [bank[0], bank[1]]
        prep_banks = [bank[2], bank[3], bank[0], bank[1]]
        NIT = NCH * KVH


        def run(eng, body, chunk_start=None):
            with eng.Fori(0, NCH - 1) as c:
                if chunk_start:
                    chunk_start(c)
                with eng.Fori(0, KVH - 2) as g:
                    body(c, c * KVH + g)
                body(c, c * KVH + KVH - 2, norm=True)
                body(c, c * KVH + KVH - 1, switch=True)
            with eng.Fori(0, KVH - 1) as g:
                body(NCH - 1, g + (NIT - KVH))
            body(NCH - 1, NIT - 1, more=False)

        @block.sync
        def _(sp):
            def load_qkv(n):
                sp.dma_start(q_raw[:, :, :], a.l1_wq[n % KVH]).then_inc(q_in, 16)
                sp.dma_start(kv_raw[:, :, :], a.l1_wkv[n % KVH]).then_inc(kv_in, 16)

            sp.dma_start(kv_raw[:, :, :], a.l1_wkv[0]).then_inc(kv_in, 16)
            sp.dma_start(craw[:, :, :], a.ctxT[0]).then_inc(c_in, 16)
            sp.dma_start(wqk[:, :], a.l1_qnw).then_inc(const_in, 16)
            sp.dma_start(knw[:, :], a.l1_knw).then_inc(const_in, 16)
            sp.wait_ge(mask_ok, 1)
            sp.dma_start(mask[0:S, 0:S], a.mask).then_inc(const_in, 16)
            sp.dma_start(mask[S:P, S:P], a.mask).then_inc(const_in, 16)
            sp.wait_ge(c_in, 16)
            sp.dma_start(q_raw[:, :, :], a.l1_wq[1]).then_inc(q_in, 16)
            sp.dma_start(o_raw[:, :, :], a.l1_wo[0]).then_inc(o_in, 16)
            sp.wait_ge(wkvl_ok, 1)
            sp.dma_start(kv_raw[:, :, :], a.l1_wkv[1]).then_inc(kv_in, 16)
            with sp.Fori(1, NIT) as i:
                sp.wait_ge(wql_ok, i + 1)
                sp.wait_ge(wkvl_ok, i + 1)
                load_qkv(i + 1)
                sp.wait_ge(wol_ok, i)
                sp.dma_start(o_raw[:, :, :], a.l1_wo[i % KVH]).then_inc(o_in, 16)
            sp.wait_ge(prep.ps, 2 * NCH * KD)
            sp.dma_start(m.xln[:, :, :], a.l1_w).then_inc(m.next_in, 16)

        @block.gpsimd
        def _(pool):
            def split_kv(n):
                pool.wait_ge(wkvh_ok, n + 1)
                pool.tensor_tensor(wkv_lo[:, :, :], kv_raw[:, :, :], wkv_hi[:, :, :], ALU.subtract).then_inc(wkvl_ok, 1)

            def split_q(n):
                pool.wait_ge(wqh_ok, n + KD)
                pool.tensor_tensor(wq_lo[:, :, :], q_raw[:, :, :], wq_hi[:, :, :], ALU.subtract).then_inc(wql_ok, 1)

            def split_o(n):
                pool.wait_ge(woh_ok, n + 1)
                pool.tensor_tensor(wo_lo[:, :, :], o_raw[:, :, :], wo_hi[:, :, :], ALU.subtract).then_inc(wol_ok, 1)

            def split_ctx(c):
                pool.wait_ge(s_cTh, c + 1)
                pool.tensor_tensor(cT_lo[:, :, :], craw[:, :, :], cT_hi[:, :, :], ALU.subtract).then_inc(s_cTl, 1)

            def roots(n):
                pool.wait_ge(s_kve, n + 1)
                pool.tensor_tensor(krs[:, :], kve[:, :], m.neg_half[:, 0:TPC], ALU.pow).then_inc(s_krs, 1)
                pool.wait_ge(s_qve, n + 1)
                pool.tensor_tensor(qrs[:, :], qve[:, :], m.neg_half[:, :], ALU.pow).then_inc(s_qrs, 1)

            def body(c, i, norm=False, switch=False, more=True):
                for t in range(TPC):
                    pool.wait_ge(s_rden, i * TPC + t + 1)
                    pt = prob[:, t, :].rearrange("p (j s) -> p j s", j=G)
                    pool.tensor_tensor(pt, pt, rden[:, t * G:(t + 1) * G].unsqueeze(2).broadcast_to([P, G, P]),
                                       ALU.mult).then_inc(s_p, 1)
                split_o(i)
                if more:
                    split_q(i + 2)
                    split_kv(i + 2)
                    roots(i + 1)
                if norm:
                    prep.pool_rstd(pool, p0 + c + 1)
                    split_ctx(c + 1)

            pool.memset(mask[:, :], OFF).then_inc(mask_ok, 1)
            split_kv(0)
            roots(0)
            split_kv(1)
            run(pool, body)

        @block.scalar
        def _(act):
            def split_kv(n):
                act.wait_ge(kv_in, (n + 1) * 16)
                act.copy(wkv_hi[:, :, :], kv_raw[:, :, :]).then_inc(wkvh_ok, 1)

            def split_q(n):
                act.wait_ge(q_in, n * 16)
                act.copy(wq_hi[:, :, :], q_raw[:, :, :]).then_inc(wqh_ok, 1)

            def split_o(n):
                act.wait_ge(o_in, (n + 1) * 16)
                act.wait_ge(s_x, n * TPC + 1)
                act.copy(wo_hi[:, :, :], o_raw[:, :, :]).then_inc(woh_ok, 1)

            def split_ctx(c):
                act.wait_ge(c_in, (c + 1) * 16)
                act.copy(cT_hi[:, :, :], craw[:, :, :]).then_inc(s_cTh, 1)

            def query(n, j):
                act.wait_ge(s_q, n * G + j + 1)
                act.copy(qT_hi[:, j, :], q_banks[j][:, :])
                act.activation(q2[:, j, :], q_banks[j][:, :], ACT.Square).then_inc(s_qact, 1)

            def keys_values(n, b):
                act.wait_ge(s_kv, n * 2 + b + 1)
                kv = kv_banks[b][:, :].rearrange("p (t w) -> p t w", t=2)
                act.copy(v_hi[:, 2 * b:2 * b + 2, :], kv[:, :, HD:])
                for u in range(2):
                    ins = act.activation(kn[:, 2 * b + u, :], kv[:, u, 0:HD], ACT.Square,
                                         accum_out=kss[:, 2 * b + u:2 * b + u + 1])
                ins.then_inc(s_kvact, 1)

            def keys_T(n):
                act.wait_ge(s_kT, n + 1)
                act.activation(kT[:, :, 0, :], kT_bank[:, :].rearrange("p (t s) -> p t s", t=TPC), ACT.Copy,
                               scale=wqk[:, :]).then_inc(s_kTh, 1)

            def exps(i, t):
                act.wait_ge(s_sc, (i * TPC + t) * 3 + 3)
                for j in range(G):
                    pt = prob[:, t, j * P:(j + 1) * P]
                    ins = act.activation(pt, pt, ACT.Exp, bias=nmx[:, t * G + j:t * G + j + 1],
                                         accum_out=den[:, t * G + j:t * G + j + 1])
                ins.then_inc(s_e, 1)

            def probs_T(i, t):
                act.wait_ge(s_pT, i * TPC + t + 1)
                act.copy(pT_hi[t % 2][:, :], pT_banks[t % 2][:, :]).then_inc(s_pTh, 1)

            def outputs(i, t):
                act.wait_ge(s_pv, i * TPC + t + 1)
                act.copy(oT_hi[:, t, :], pv_banks[t % 2][:, :]).then_inc(s_oTh, 1)

            def body(c, i, norm=False, switch=False, more=True):
                if switch:
                    prep.act_hi(act, p0 + c + 1, prep_banks)
                split_o(i)
                exps(i, 0)
                exps(i, 1)
                exps(i, 2)
                if more:
                    act.wait_ge(s_s, (i + 1) * TPC)
                    query(i + 1, 0)
                    query(i + 1, 1)
                exps(i, 3)
                if more:
                    query(i + 1, 2)
                probs_T(i, 0)
                probs_T(i, 1)
                if more:
                    query(i + 1, 3)
                    split_q(i + 2)
                outputs(i, 0)
                outputs(i, 1)
                probs_T(i, 2)
                probs_T(i, 3)
                if more:
                    keys_values(i + 1, 0)
                    act.wait_ge(s_kv, (i + 2) * 2)
                    split_kv(i + 2)
                outputs(i, 2)
                outputs(i, 3)
                if more:
                    keys_values(i + 1, 1)
                if norm:
                    split_ctx(c + 1)
                if more:
                    keys_T(i + 1)

            def load_next_ctx(c):
                act.wait_ge(s_cTl, c + 1)
                act.dma_start(craw[:, :, :], a.ctxT[c + 1]).then_inc(c_in, 16)

            act.wait_ge(m.next_in, 16)
            for k in range(KD):
                act.copy(wq_hi[:, k, :], m.xln[:, k, :]).then_inc(wqh_ok, 1)
            split_kv(0)
            split_ctx(0)
            for j in range(G):
                query(0, j)
            keys_values(0, 0)
            keys_values(0, 1)
            act.wait_ge(wqk_ok, 1)
            keys_T(0)
            split_q(1)
            split_kv(1)
            run(act, body, load_next_ctx)

        @block.vector
        def _(dve):
            def add_out(c, i, t):
                dve.wait_ge(s_o, i * TPC + t + 1)
                xt = m.x[:, bass.ts(c * TPC + t, D)]
                dve.tensor_tensor(xt, o_banks[t % 2][:, :], xt, ALU.add).then_inc(s_x, 1)

            def query(n, j):
                dve.wait_ge(s_qact, n * G + j + 1)
                dve.tensor_tensor(qT_lo[:, j, :], q_banks[j][:, :], qT_hi[:, j, :], ALU.subtract).then_inc(s_ql, 1)

            def query_sums(n, tiles=range(TPC)):
                for t in tiles:
                    dve.wait_ge(s_qss, n * TPC + t + 1)
                    ins = dve.tensor_reduce(qss[:, t * G:(t + 1) * G],
                                            sq_banks[t][:, :].rearrange("p (j f) -> p j f", j=G), AX.X, ALU.add)
                    ins.then_inc(s_qsum, 1)
                if t != TPC - 1:
                    return
                dve.wait_ge(s_qsum, (n + 1) * TPC)
                dve.tensor_scalar(qve[:, :], qss[:, :], HD * L1_EPS, None, ALU.add).then_inc(s_qve, 1)

            def values(n, b):
                dve.wait_ge(s_kvact, n * 2 + b + 1)
                kv = kv_banks[b][:, :].rearrange("p (t w) -> p t w", t=2)
                dve.tensor_tensor(v_lo[:, 2 * b:2 * b + 2, :], kv[:, :, HD:], v_hi[:, 2 * b:2 * b + 2, :],
                                  ALU.subtract).then_inc(s_vl, 1)

            def key_squares(n):
                dve.tensor_scalar(kve[:, :], kss[:, :], 1.0 / HD, L1_EPS, ALU.mult, ALU.add).then_inc(s_kve, 1)

            def keys(n):
                dve.wait_ge(s_krs, n + 1)
                for t in range(TPC):
                    ins = dve.tensor_scalar(kn[:, t, :], kv_banks[t // 2][:, (t % 2) * 2 * HD:(t % 2) * 2 * HD + HD],
                                            krs[:, t:t + 1], None, ALU.mult)
                ins.then_inc(s_kn, 1)

            def keys_T(n):
                dve.wait_ge(s_kTh, n + 1)
                dve.scalar_tensor_tensor(kT[:, :, 1, :], kT_bank[:, :].rearrange("p (t s) -> p t s", t=TPC), wqk[:, :],
                                         kT[:, :, 0, :], ALU.mult, ALU.subtract).then_inc(s_kTl, 1)

            def scores(i, t):
                dve.wait_ge(s_s, i * TPC + t + 1)
                for h in range(2):
                    for j in range(G):
                        pt, col = prob[:, t, j * P:(j + 1) * P], (j % 2) * 2 * P + h * P
                        ins = dve.scalar_tensor_tensor(pt, s_banks[t][j // 2][:, col:col + P], qrs[:, t * G + j:t * G + j + 1],
                                                       pt if h else mask[:, :], ALU.mult, ALU.add)
                    ins.then_inc(s_sc, 1)
                    dve.wait_ge(s_sc, (i * TPC + t) * 3 + h + 1)
                dve.tensor_reduce(nmx[:, t * G:(t + 1) * G], prob[:, t, :].rearrange("p (j s) -> p j s", j=G),
                                  AX.X, ALU.max, negate=True).then_inc(s_sc, 1)

            def denominators(i, t):
                dve.wait_ge(s_e, i * TPC + t + 1)
                dve.reciprocal(rden[:, t * G:(t + 1) * G], den[:, t * G:(t + 1) * G]).then_inc(s_rden, 1)

            def probs_T(i, t):
                dve.wait_ge(s_pTh, i * TPC + t + 1)
                dve.tensor_tensor(pT_lo[t % 2][:, :], pT_banks[t % 2][:, :], pT_hi[t % 2][:, :],
                                  ALU.subtract).then_inc(s_pTl, 1)

            def outputs(i, t):
                dve.wait_ge(s_oTh, i * TPC + t + 1)
                dve.tensor_tensor(oT_lo[:, t, :], pv_banks[t % 2][:, :], oT_hi[:, t, :],
                                  ALU.subtract).then_inc(s_oTl, 1)

            def body(c, i, norm=False, switch=False, more=True):
                dve.wait_ge(s_qrs, i + 1)
                scores(i, 0)
                if switch:
                    prep.dve_lo(dve, p0 + c + 1, prep_banks)
                scores(i, 1)
                denominators(i, 0)
                scores(i, 2)
                denominators(i, 1)
                scores(i, 3)
                denominators(i, 2)
                if more:
                    query(i + 1, 0)
                    query(i + 1, 1)
                denominators(i, 3)
                if more:
                    query(i + 1, 2)
                probs_T(i, 0)
                probs_T(i, 1)
                if more:
                    query(i + 1, 3)
                outputs(i, 0)
                outputs(i, 1)
                probs_T(i, 2)
                probs_T(i, 3)
                if more:
                    values(i + 1, 0)
                    query_sums(i + 1)
                outputs(i, 2)
                outputs(i, 3)
                if more:
                    values(i + 1, 1)
                    key_squares(i + 1)
                add_out(c, i, 0)
                if more:
                    keys(i + 1)
                if norm:
                    prep.dve_stats(dve, p0 + c + 1, c + 1, range(0, 2))
                add_out(c, i, 1)
                if more:
                    keys_T(i + 1)
                if norm:
                    prep.dve_stats(dve, p0 + c + 1, c + 1, range(2, TPC))
                add_out(c, i, 2)
                if norm:
                    prep.dve_norm(dve, p0 + c + 1, c + 1)
                add_out(c, i, 3)

            dve.memset(nmx[:, :], 0.0).then_inc(s_x, 1)
            for k in range(KD):
                dve.wait_ge(wqh_ok, k + 1)
                dve.tensor_tensor(wq_lo[:, k, :], m.xln[:, k, :], wq_hi[:, k, :],
                                  ALU.subtract).then_inc(wql_ok if k == KD - 1 else wq0_ok, 1)
            dve.wait_ge(const_in, 64)
            dve.tensor_tensor(wqk[:, :], wqk[:, :], knw[:, :], ALU.mult).then_inc(wqk_ok, 1)
            dve.wait_ge(wqk_ok, 1)
            dve.wait_ge(s_cTh, 1)
            dve.tensor_tensor(cT_lo[:, :, :], craw[:, :, :], cT_hi[:, :, :], ALU.subtract).then_inc(s_cTl, 1)
            for j in range(G):
                query(0, j)
            values(0, 0)
            values(0, 1)
            key_squares(0)
            query_sums(0, range(0, 2))
            keys(0)
            query_sums(0, range(2, TPC))
            keys_T(0)
            dve.wait_ge(wqh_ok, KD + 1)
            dve.tensor_tensor(wq_lo[:, :, :], q_raw[:, :, :], wq_hi[:, :, :], ALU.subtract).then_inc(wql_ok, 1)
            run(dve, body)

        @block.tensor
        def _(pe):
            def query(n, j, first=False, fresh=None):
                if j == 0 and not first:
                    pe.wait_ge(wql_ok, n + 1)
                if j == 2 and not first:
                    pe.wait_ge(s_x, (n - 1) * TPC + 1)
                cols = slice(j * HD, (j + 1) * HD)
                for k in range(KD):
                    if j == 0 and first:
                        if k < KD - 1:
                            pe.wait_ge(wq0_ok, k + 1)
                        else:
                            pe.wait_ge(wql_ok, 1)
                    if fresh is not None:
                        prep.wait_ready(pe, fresh, k)
                    ins = split_mm(pe, q_banks[j][:, :], wq_hi[:, k, cols], wq_lo[:, k, cols],
                                   m.xT_hi[:, k, :], m.xT_lo[:, k, :], k == 0, k == KD - 1)
                ins.then_inc(s_q, 1)

            def keys_values(n, tiles):
                if 0 in tiles:
                    pe.wait_ge(wkvl_ok, n + 1)
                    pe.wait_ge(s_ql, n * G + 2)
                for t in tiles:
                    rows = slice(t * P, (t + 1) * P)
                    out = kv_banks[t // 2][:, (t % 2) * 2 * HD:(t % 2 + 1) * 2 * HD]
                    for k in range(KD):
                        ins = split_mm(pe, out, cT_hi[:, k, rows], cT_lo[:, k, rows], wkv_hi[:, k, :], wkv_lo[:, k, :],
                                       k == 0, k == KD - 1)
                    if t % 2:
                        ins.then_inc(s_kv, 1)

            def query_squares_T(n, first=False):
                pe.wait_ge(s_ql, (n + 1) * G)
                for t in range(TPC):
                    if t == 2 and not first:
                        pe.wait_ge(s_pTl, n * TPC)
                    for j in range(G):
                        ins = pe.transpose(sq_banks[t][:, j * P:(j + 1) * P], q2[:, j, t * P:(t + 1) * P], m.ident[:, :])
                    ins.then_inc(s_qss, 1)

            def keys_T(n):
                pe.wait_ge(s_kn, n + 1)
                for t in range(TPC):
                    ins = pe.transpose(kT_bank[:, t * P:(t + 1) * P], kn[:, t, :], m.ident[:, :])
                ins.then_inc(s_kT, 1)

            def scores(i, t):
                if t == 0:
                    pe.wait_ge(s_kTl, i + 1)
                    pe.wait_ge(s_ql, (i + 1) * G)
                    pe.wait_ge(s_qve, i + 1)
                if t >= 2:
                    pe.wait_ge(s_sc, (i * TPC + t - 2) * 3 + 2)
                rows = slice(t * P, (t + 1) * P)
                for j in range(G):
                    out = s_banks[t][j // 2][:, (j % 2) * 2 * P:(j % 2 + 1) * 2 * P]
                    pe.matmul(out, qT_hi[:, j, rows], kT[:, t, :, :], start=True, stop=False)
                    ins = pe.matmul(out[:, 0:P], qT_lo[:, j, rows], kT[:, t, 0, :], start=False, stop=True)
                ins.then_inc(s_s, 1)

            def probs_T(i, t):
                pe.wait_ge(s_p, i * TPC + t + 1)
                if t >= 2:
                    pe.wait_ge(s_pTl, i * TPC + t - 1)
                else:
                    pe.wait_ge(s_sc, (i * TPC + 2) * 3 + 2)
                for j in range(G):
                    cols = slice(j * P, (j + 1) * P)
                    ins = pe.transpose(pT_banks[t % 2][:, cols], prob[:, t, cols], m.ident[:, :])
                ins.then_inc(s_pT, 1)

            def attend(i, t):
                pe.wait_ge(s_pTl, i * TPC + t + 1)
                if t == 0:
                    pe.wait_ge(s_vl, (i + 1) * 2)
                if t >= 2:
                    pe.wait_ge(s_oTl, i * TPC + t - 1)
                else:
                    pe.wait_ge(s_sc, (i * TPC + 3) * 3 + 2)
                split_mm(pe, pv_banks[t % 2][:, :], v_hi[:, t, :], v_lo[:, t, :], pT_hi[t % 2][:, :],
                         pT_lo[t % 2][:, :], True, True).then_inc(s_pv, 1)

            def out_rows(i, t, last):
                if t == 0:
                    pe.wait_ge(wol_ok, i + 1)
                    if not last:
                        pe.wait_ge(s_qsum, (i + 1) * TPC + 2)
                pe.wait_ge(s_oTl, i * TPC + t + 1)
                if t >= 2:
                    pe.wait_ge(s_x, i * TPC + t)
                for j in range(G):
                    cols = slice(j * P, (j + 1) * P)
                    ins = split_mm(pe, o_banks[t % 2][:, :], oT_hi[:, t, cols], oT_lo[:, t, cols],
                                   wo_hi[:, j, :], wo_lo[:, j, :], j == 0, j == G - 1)
                ins.then_inc(s_o, 1)

            def body(c, i, norm=False, switch=False, more=True):
                p = p0 + c + 1
                scores(i, 0)
                scores(i, 1)
                if switch:
                    prep.pe_transpose(pe, p, prep_banks, range(0, 2))
                    pe.wait_ge(s_x, i * TPC + 1)
                    prep.pe_transpose(pe, p, prep_banks, range(2, KD))
                if more:
                    query(i + 1, 0, fresh=p if switch else None)
                    scores(i, 2)
                    query(i + 1, 1)
                    scores(i, 3)
                else:
                    scores(i, 2)
                    scores(i, 3)
                if more:
                    query(i + 1, 2)
                    query(i + 1, 3)
                probs_T(i, 0)
                probs_T(i, 1)
                if more:
                    if switch:
                        pe.wait_ge(s_cTl, c + 2)
                    keys_values(i + 1, range(0, 3))
                attend(i, 0)
                attend(i, 1)
                probs_T(i, 2)
                probs_T(i, 3)
                if more:
                    keys_values(i + 1, range(3, TPC))
                    query_squares_T(i + 1)
                attend(i, 2)
                attend(i, 3)
                out_rows(i, 0, not more)
                out_rows(i, 1, not more)
                if more:
                    keys_T(i + 1)
                out_rows(i, 2, not more)
                out_rows(i, 3, not more)

            for j in range(G):
                query(0, j, first=True)
            pe.wait_ge(s_cTl, 1)
            keys_values(0, range(TPC))
            query_squares_T(0, first=True)
            keys_T(0)
            run(pe, body)


def stage_gated_ffn(nc, m, a):
    with ExitStack() as ctx:
        sb = lambda n, s, d=F32: ctx.enter_context(nc.sbuf_tensor("f1_" + n, s, d))
        sem = lambda n: ctx.enter_context(nc.semaphore("f1_" + n))
        WF = NCL + D
        HF = WF // 2
        cent_raw, w_raw = sb("cent_raw", [P, KD, NCL]), m.xln
        w_hi, w_lo = sb("w_hi", [P, KD, WF], F32R), sb("w_lo", [P, KD, WF], F32R)
        bias = sb("bias", [P, D])
        dense = sb("dense", [P, NT * D])
        two = lambda n, s, d=F32: [sb(f"{n}{e}", s, d) for e in range(2)]
        xn, xT_hi, xT_lo = two("xn", [P, D]), two("xT_hi", [P, KD, P], F32R), two("xT_lo", [P, KD, P], F32R)
        bias_row, ex, hit = two("bias_row", [P, D]), two("ex", [P, NCL]), two("hit", [P, NCL])
        st, mv, ve, rs = two("ln_st", [P, 6]), two("ln_mv", [P, 2]), two("ln_ve", [P, 1]), two("ln_rs", [P, 1])
        nmx, nmx10, den, rden, row_sel = (two("nmx", [P, 1]), two("nmx10", [P, 1]), two("den", [P, 1]),
                                          two("rden", [P, 1]), two("row_sel", [P, 1]))
        hit_any = sb("hit_any", [P, NCL])
        assign_i, cluster_id = sb("assign_i", [NCL, D], I32), sb("cluster_id", [NCL, 1], I32)
        assign_f, cluster_f = sb("assign_f", [NCL, D]), sb("cluster_f", [NCL, 1])
        member = sb("member", [NCL, D], BF16)
        cl_sel = sb("cl_sel", [NCL, P], BF16)
        ones_cl = sb("ones_cl", [NCL, P])
        col_sel = sb("col_sel", [P, D])
        xT_banks, a_banks, b_banks, cnt_bank, col_bank = m.bank[0:2], m.bank[2:4], m.bank[4:6], m.bank[6], m.bank[7]

        cent_in, const_in, out_in = sem("cent_in"), sem("const_in"), sem("out_written")
        wh_ok, wl_ok, member_ok = sem("w_hi_ok"), sem("w_ok"), sem("member_steps")
        const_ok = sem("const_steps")
        s_ve, s_rs, s_xn = sem("ln_var_steps"), sem("ln_rs_ok"), sem("xn_ok")
        s_xT, s_xh, s_xl = sem("xT_ps"), sem("xT_hi_ok"), sem("xT_ok")
        s_l, s_d, s_nmx, s_e = sem("logits_ps"), sem("dense_ps"), sem("max_steps"), sem("exp_ok")
        s_hit, s_any, s_gated, s_dense = sem("hit_steps"), sem("hit_any_ok"), sem("row_gated_ok"), sem("dense_ok")
        s_cnt, s_cl, s_col, s_colsel = sem("count_ps"), sem("cl_sel_ok"), sem("col_ps"), sem("col_sel_ok")
        s_out, s_out_p = sem("out_steps"), sem("out_pool_steps")
        block = ctx.enter_context(nc.Block())
        out_rows = a.out.rearrange("(n p) d -> n p d", p=P)
        out_pairs = a.out.rearrange("(n e p) d -> n p e d", e=2, p=P)
        POOL_TILES = 4
        DVE_TILES = NT - POOL_TILES

        def run(eng, step):
            step(0, 0, first=True, early=True)
            step(1, 1, early=True)
            with eng.Fori(1, NT // 2 - 1) as pair:
                step(pair * 2, 0)
                step(pair * 2 + 1, 1)
            step(NT - 2, 0, left=1)
            step(NT - 1, 1, left=0)

        @block.sync
        def _(sp):
            sp.dma_start(cent_raw[:, :, :], a.cent).then_inc(cent_in, 16)
            sp.dma_start(bias[:, :], a.l1_b.partition_broadcast(P)).then_inc(const_in, 16)
            sp.dma_start(assign_i[:, :], a.assign.partition_broadcast(NCL)).then_inc(const_in, 16)
            with sp.Fori(0, DVE_TILES // 2) as pair:
                sp.wait_ge(s_out, pair * 4 + 4)
                sp.dma_start(out_pairs[pair], m.x[:, bass.ts(pair, 2 * D)].rearrange("p (e d) -> p e d", e=2)).then_inc(
                    out_in, 16)
            sp.wait_ge(out_in, 16 * (DVE_TILES // 2 + POOL_TILES))

        @block.gpsimd
        def _(pool):
            def rstd(n, e):
                pool.wait_ge(s_ve, n * 3 + 3)
                pool.tensor_tensor(rs[e][:, :], ve[e][:, :], m.neg_half[:, 0:1], ALU.pow).then_inc(s_rs, 1)

            def add_bias(n, e):
                pool.wait_ge(s_gated, n + 1)
                dn = dense[:, bass.ts(n, D)]
                pool.tensor_tensor(dn, dn, bias_row[e][:, :], ALU.add).then_inc(s_dense, 1)

            def step(n, e, first=False, early=False, left=2):
                if left >= 2:
                    rstd(n + 2, e)
                if not first:
                    add_bias(n - 1, 1 - e)

            pool.iota(cluster_id[:, :], pattern=[[0, 1]], base=0, channel_multiplier=1).then_inc(const_ok, 1)
            pool.wait_ge(const_ok, 1)
            pool.memset(hit_any[:, :], 0.0).then_inc(const_ok, 1)
            pool.memset(ones_cl[:, :], 1.0).then_inc(const_ok, 1)
            pool.wait_ge(const_ok, 3)
            pool.memset(bias_row[0][:, :], 0.0).then_inc(s_dense, 1)
            rstd(0, 0)
            rstd(1, 1)
            run(pool, step)
            add_bias(NT - 1, 1)
            pool.wait_ge(s_dense, NT + 1)
            pool.wait_ge(s_colsel, 1)
            with pool.Fori(0, POOL_TILES) as n:
                dn, xt = dense[:, bass.ts(n + DVE_TILES, D)], m.x[:, bass.ts(n + DVE_TILES, D)]
                pool.tensor_tensor(dn, dn, col_sel[:, :], ALU.mult).then_inc(s_out_p, 1)
                pool.wait_ge(s_out_p, n * 2 + 1)
                pool.tensor_tensor(xt, xt, dn, ALU.add).then_inc(s_out_p, 1)

        @block.scalar
        def _(act):
            def rows_T(n, e):
                act.wait_ge(s_xT, n + 1)
                act.copy(xT_hi[e][:, :, :], xT_banks[e][:, :].rearrange("p (k s) -> p k s", k=KD)).then_inc(s_xh, 1)

            def exps(n, e):
                act.wait_ge(s_nmx, n * 2 + 2)
                act.activation(ex[e][:, :], a_banks[e][:, 0:NCL], ACT.Exp, scale=10.0, bias=nmx10[e][:, :],
                               accum_out=den[e][:, :]).then_inc(s_e, 1)

            def gate_rows(n, e, first=False):
                act.wait_ge(s_d, n + 1)
                act.wait_ge(s_hit, n * 3 + 3)
                dn = dense[:, bass.ts(n, D)]
                act.activation(dn[:, 0:HF - NCL], a_banks[e][:, NCL:HF], ACT.Copy, scale=row_sel[e][:, :])
                act.activation(dn[:, HF - NCL:], b_banks[e][:, 0:HF], ACT.Copy, scale=row_sel[e][:, :])
                if not first:
                    act.wait_ge(s_dense, n)
                act.activation(bias_row[e][:, :], bias[:, :], ACT.Copy, scale=row_sel[e][:, :]).then_inc(s_gated, 1)

            def step(n, e, first=False, early=False, left=2):
                if left >= 1:
                    rows_T(n + 1, 1 - e)
                if not first:
                    gate_rows(n - 1, 1 - e, early)
                exps(n, e)

            act.wait_ge(m.next_in, 32)
            for k in range(KD):
                act.copy(w_hi[:, k, NCL:], w_raw[:, k, :]).then_inc(wh_ok, 1)
                if k == 0:
                    rows_T(0, 0)
                    act.wait_ge(cent_in, 16)
                    act.copy(w_hi[:, :, 0:NCL], cent_raw[:, :, :]).then_inc(wh_ok, 1)
            act.wait_ge(const_in, 32)
            run(act, step)
            gate_rows(NT - 1, 1)
            with act.Fori(0, POOL_TILES) as n:
                act.wait_ge(s_out_p, n * 2 + 2)
                act.dma_start(out_rows[n + DVE_TILES], m.x[:, bass.ts(n + DVE_TILES, D)]).then_inc(out_in, 16)

        @block.vector
        def _(dve):
            def variance(n, e):
                dve.bn_stats(st[e][:, :], m.x[:, bass.ts(n, D)]).then_inc(s_ve, 1)
                dve.wait_ge(s_ve, n * 3 + 1)
                dve.memset(ve[e][:, :], LN_EPS)
                dve.bn_aggr(mv[e][:, :], st[e][:, :]).then_inc(s_ve, 1)
                dve.wait_ge(s_ve, n * 3 + 2)
                dve.tensor_scalar(ve[e][:, :], mv[e][:, 1:2], LN_EPS, None, ALU.add).then_inc(s_ve, 1)

            def normalise(n, e):
                dve.wait_ge(s_rs, n + 1)
                dve.tensor_scalar(xn[e][:, :], m.x[:, bass.ts(n, D)], mv[e][:, 0:1], rs[e][:, :],
                                  ALU.subtract, ALU.mult).then_inc(s_xn, 1)

            def rows_T(n, e):
                dve.wait_ge(s_xh, n + 1)
                dve.tensor_tensor(xT_lo[e][:, :, :], xT_banks[e][:, :].rearrange("p (k s) -> p k s", k=KD),
                                  xT_hi[e][:, :, :], ALU.subtract).then_inc(s_xl, 1)

            def largest(n, e):
                dve.wait_ge(s_l, n + 1)
                dve.tensor_reduce(nmx[e][:, :], a_banks[e][:, 0:NCL], AX.X, ALU.max, negate=True).then_inc(s_nmx, 1)
                dve.wait_ge(s_nmx, n * 2 + 1)
                dve.tensor_scalar(nmx10[e][:, :], nmx[e][:, :], 10.0, None, ALU.mult).then_inc(s_nmx, 1)

            def hits(n, e):
                dve.wait_ge(s_e, n + 1)
                dve.reciprocal(rden[e][:, :], den[e][:, :]).then_inc(s_hit, 1)
                dve.wait_ge(s_hit, n * 3 + 1)
                dve.tensor_scalar(hit[e][:, :], ex[e][:, :], rden[e][:, :], 0.01, ALU.mult, ALU.is_gt).then_inc(s_hit, 1)
                dve.wait_ge(s_hit, n * 3 + 2)
                dve.tensor_reduce(row_sel[e][:, :], hit[e][:, :], AX.X, ALU.max).then_inc(s_hit, 1)
                dve.wait_ge(s_any, n)
                dve.tensor_tensor(hit_any[:, :], hit_any[:, :], hit[e][:, :], ALU.max).then_inc(s_any, 1)

            def variance_and_hits(n, e, early):
                v, o = n + 2, 1 - e
                dve.bn_stats(st[e][:, :], m.x[:, bass.ts(v, D)]).then_inc(s_ve, 1)
                dve.wait_ge(s_e, n)
                dve.reciprocal(rden[o][:, :], den[o][:, :]).then_inc(s_hit, 1)
                dve.wait_ge(s_ve, v * 3 + 1)
                dve.memset(ve[e][:, :], LN_EPS)
                dve.bn_aggr(mv[e][:, :], st[e][:, :]).then_inc(s_ve, 1)
                dve.wait_ge(s_hit, n * 3 - 2)
                dve.tensor_scalar(hit[o][:, :], ex[o][:, :], rden[o][:, :], 0.01, ALU.mult, ALU.is_gt).then_inc(s_hit, 1)
                dve.wait_ge(s_ve, v * 3 + 2)
                dve.tensor_scalar(ve[e][:, :], mv[e][:, 1:2], LN_EPS, None, ALU.add).then_inc(s_ve, 1)
                dve.wait_ge(s_hit, n * 3 - 1)
                dve.tensor_reduce(row_sel[o][:, :], hit[o][:, :], AX.X, ALU.max).then_inc(s_hit, 1)
                if not early:
                    dve.wait_ge(s_any, n - 1)
                dve.tensor_tensor(hit_any[:, :], hit_any[:, :], hit[o][:, :], ALU.max).then_inc(s_any, 1)

            def members():
                dve.wait_ge(const_in, 32)
                dve.tensor_copy(cluster_f[:, :], cluster_id[:, :])
                dve.tensor_copy(assign_f[:, :], assign_i[:, :]).then_inc(member_ok, 1)
                dve.wait_ge(member_ok, 1)
                dve.tensor_scalar(member[:, :], assign_f[:, :], cluster_f[:, :], None, ALU.is_equal).then_inc(member_ok, 1)

            def step(n, e, first=False, early=False, left=2):
                if left >= 2 and not first:
                    variance_and_hits(n, e, early)
                elif left >= 2:
                    variance(n + 2, e)
                else:
                    hits(n - 1, 1 - e)
                if left >= 1:
                    rows_T(n + 1, 1 - e)
                if left == 0:
                    members()
                if left >= 2:
                    normalise(n + 2, e)
                largest(n, e)

            variance(0, 0)
            variance(1, 1)
            normalise(0, 0)
            normalise(1, 1)
            rows_T(0, 0)
            dve.wait_ge(wh_ok, 2)
            dve.tensor_tensor(w_lo[:, :, 0:NCL], cent_raw[:, :, :], w_hi[:, :, 0:NCL], ALU.subtract).then_inc(wl_ok, 1)
            for k in range(KD):
                if k:
                    dve.wait_ge(wh_ok, k + 2)
                dve.tensor_tensor(w_lo[:, k, NCL:], w_raw[:, k, :], w_hi[:, k, NCL:], ALU.subtract).then_inc(wl_ok, 1)
            dve.wait_ge(const_ok, 3)
            run(dve, step)
            hits(NT - 1, 1)
            dve.wait_ge(s_cnt, 1)
            dve.tensor_scalar(cl_sel[:, :], ones_cl[:, :], cnt_bank[0:NCL, 0:1], None, ALU.is_le).then_inc(s_cl, 1)
            dve.wait_ge(s_col, 1)
            dve.tensor_copy(col_sel[:, :], col_bank[:, :]).then_inc(s_colsel, 1)
            dve.wait_ge(s_colsel, 1)
            dve.wait_ge(s_dense, DVE_TILES + 1)
            with dve.Fori(0, DVE_TILES // 2) as pair:
                tiles = [(dense[:, bass.ts(pair * 2 + e, D)], m.x[:, bass.ts(pair * 2 + e, D)]) for e in range(2)]
                for dn, _ in tiles:
                    dve.tensor_tensor(dn, dn, col_sel[:, :], ALU.mult).then_inc(s_out, 1)
                for e, (dn, xt) in enumerate(tiles):
                    dve.wait_ge(s_out, pair * 4 + e + 1)
                    dve.tensor_tensor(xt, xt, dn, ALU.add).then_inc(s_out, 1)

        @block.tensor
        def _(pe):
            def rows_T(n, e):
                pe.wait_ge(s_xn, n + 1)
                for k in range(KD):
                    ins = pe.transpose(xT_banks[e][:, k * P:(k + 1) * P], xn[e][:, k * P:(k + 1) * P], m.ident[:, :])
                ins.then_inc(s_xT, 1)

            def step(n, e, first=False, early=False, left=2):
                if left >= 1:
                    rows_T(n + 1, 1 - e)
                pe.wait_ge(s_xl, n + 1)
                if not early:
                    pe.wait_ge(s_gated, n - 1)
                for bank, half, s in ((a_banks[e], slice(0, HF), s_l), (b_banks[e], slice(HF, WF), s_d)):
                    for k in range(KD):
                        if first and half.start == 0:
                            pe.wait_ge(wl_ok, k + 2)
                        ins = split_mm(pe, bank[:, 0:HF], xT_hi[e][:, k, :], xT_lo[e][:, k, :],
                                       w_hi[:, k, half], w_lo[:, k, half], k == 0, k == KD - 1)
                    ins.then_inc(s, 1)

            rows_T(0, 0)
            run(pe, step)
            pe.wait_ge(s_any, NT)
            pe.matmul(cnt_bank[0:NCL, 0:1], hit_any[:, :], m.ones[:, :], start=True, stop=True).then_inc(s_cnt, 1)
            pe.wait_ge(s_cl, 1)
            pe.wait_ge(member_ok, 2)
            pe.matmul(col_bank[:, :], cl_sel[:, :], member[:, :], start=True, stop=True).then_inc(s_col, 1)


def network(nc, a):
    with ExitStack() as ctx:
        m = persistent(nc, ctx)
        prep = Prep(nc, ctx, m)
        with ExitStack() as early:
            fw = Mem()
            sb = lambda n, s, d=F32R: early.enter_context(nc.sbuf_tensor(n, s, d))
            fw.w1_hi, fw.w1_lo = sb("w1_hi", [P, KD * INTER]), sb("w1_lo", [P, KD * INTER])
            fw.c1_raw, fw.c2_raw = sb("c1_raw", [P, KD, RK3], F32), sb("h", [P, INTER], F32)
            fw.c1_hi, fw.c1_lo, fw.c2st = sb("c1_hi", [P, KD, RK3]), sb("c1_lo", [P, KD, RK3]), sb("c2st", [RK3, INTER])
            stage_l0_attention(nc, m, prep, fw, a)
            stage_sparse_ffn(nc, m, prep, fw, a)
        stage_l1_attention(nc, m, prep, a)
        stage_gated_ffn(nc, m, a)


def kernel(**inputs):
    import concourse.bacc as bacc
    from concourse.bass_utils import run_bass_kernel_spmd

    given = {n: np.asarray(v) for n, v in inputs.items()}

    def blocks(w, *lead):
        return w.reshape(*lead, -1, P, w.shape[-1]).swapaxes(-3, -2)

    ctx_rows = given["ctx_4096"].reshape(ROWS, D)
    wk = given["L1_xattn_Wk"].T.reshape(D, KVH, HD)
    wv = given["L1_xattn_Wv"].T.reshape(D, KVH, HD)
    laid = {
        "x": given["x"].reshape(ROWS, D),
        "ctx": ctx_rows,
        "ctxT": ctx_rows.reshape(NCH, CHUNK, KD, P).transpose(0, 3, 2, 1),
        "mask": given["mask_1x1xSxS2_ff0"].reshape(S, S),
        "l0_wq": blocks(given["L0_xattn_Wq_w"].T),
        "l0_wk": blocks(given["L0_xattn_Wk_w"].T),
        "l0_bq": given["L0_xattn_Wq_b"],
        "l0_bk": given["L0_xattn_Wk_b"],
        "l0_fnw": given["L0_xattn_fn_w"],
        "l0_qnw": given["L0_xattn_qn_w"],
        "l0_knw": given["L0_xattn_kn_w"],
        "c1": blocks(given["L0_ffn_c1_w"].T),
        "c2": given["L0_ffn_c2_w"].T,
        "w1": blocks(given["L0_ffn_w1"].T).reshape(P, KD * INTER),
        "w2": blocks(given["L0_ffn_w2t"]).reshape(P, NI * D),
        "l1_wq": blocks(given["L1_xattn_Wq"].T.reshape(D, KVH, G * HD).swapaxes(0, 1), KVH),
        "l1_wkv": blocks(np.concatenate([wk, wv], axis=2).swapaxes(0, 1), KVH),
        "l1_wo": blocks(given["L1_xattn_Wo"].T.reshape(KVH, G * HD, D), KVH),
        "l1_qnw": given["L1_xattn_q_norm_w"].reshape(HD, 1),
        "l1_knw": given["L1_xattn_k_norm_w"].reshape(HD, 1),
        "l1_w": blocks(given["L1_ffn_weight"].T),
        "l1_b": given["L1_ffn_bias"],
        "cent": blocks(given["L1_ffn_centroids"].T),
        "assign": given["L1_ffn_assignments"],
    }
    nc = bacc.Bacc("TRN2", target_bir_lowering=False, num_devices=1)
    a, arrays = Mem(), {}
    for name, v in laid.items():
        v = np.ascontiguousarray(v)
        arrays[f"in_{name}"] = v
        a.__dict__[name] = nc.dram_tensor(f"in_{name}", v.shape, mybir.dt.from_np(v.dtype), kind="ExternalInput").ap()
    a.out = nc.dram_tensor("out_x", (ROWS, D), F32, kind="ExternalOutput").ap()
    network(nc, a)
    r = run_bass_kernel_spmd(nc, [arrays], core_ids=[0])
    return r.results[0]["out_x"].reshape(given["x"].shape)
```
